# Optimizing a Trainium2 kernel written in Bass

```python
import numpy as np
import jax
import jax.numpy as jnp

def _softmax(x, axis=-1):
    return jax.nn.softmax(x, axis=axis)

def _gelu(x):
    return jax.nn.gelu(x, approximate=True)

def _silu(x):
    return jax.nn.silu(x)

def _sigmoid(x):
    return jax.nn.sigmoid(x)

def _layernorm(x, axis=-1, eps=1e-05):
    m = jnp.mean(x, axis=axis, keepdims=True)
    v = jnp.var(x, axis=axis, keepdims=True)
    return (x - m) / jnp.sqrt(v + eps)

def _scatter_add(tgt, idx, src, axis=0):
    return tgt.at[idx].add(src)

def _segment_sum(src, seg, n):
    return jax.ops.segment_sum(src, seg, n)
kernel_name = 'mk_xattn_ffn_d1_seqx_r4_a3441d'

def setup_inputs(seed: int=0):
    np.random.seed(seed)
    _w = jnp.asarray

    def _rec_inputs():
        import jax
        import jax.numpy as jnp
        _rk = jax.random.key(seed)
        x = 4.136e-05 + 0.9999 * jax.random.normal(jax.random.fold_in(_rk, 1), (4, 512, 512), jnp.float32)
        _lenS = 512 - jax.random.randint(jax.random.fold_in(_rk, 7), (4,), 0, max(1, 512 // 4) + 1, jnp.int32)
        _lenS2 = 512 - jax.random.randint(jax.random.fold_in(_rk, 8), (4,), 0, max(1, 512 // 4) + 1, jnp.int32)
        _ctx_1024P = jax.random.normal(jax.random.fold_in(_rk, 11), (4, 16, 256), jnp.float32)
        _ctx_1024c = jax.random.dirichlet(jax.random.fold_in(_rk, 511), 0.3 * jnp.ones((16,), jnp.float32), (4, 512))
        _ctx_1024t = jnp.einsum('bsk,bkd->bsd', _ctx_1024c, _ctx_1024P)
        _ctx_1024t = _ctx_1024t * jax.lax.rsqrt(jnp.mean(jnp.square(_ctx_1024t)) + 1e-12) * 0.953939
        ctx_1024 = -0.000292821 + 1.00034 * (_ctx_1024t + 0.3 * jax.random.normal(jax.random.fold_in(_rk, 611), (4, 512, 256), jnp.float32))
        return (x, ctx_1024)
    x, ctx_1024 = _rec_inputs()

    def _L0_xattn_setup():
        import jax, jax.numpy as jnp
        import numpy as np
        import math
        B, L, DM = (2, 512, 256)
        DS, DC, EXP = (16, 4, 2)
        DI = EXP * DM
        DR = math.ceil(DM / 16)
        DT_MIN, DT_MAX, DT_FLOOR = (0.001, 0.1, 0.0001)

        def _ssm_forward(hidden_states, z, in_proj_w, conv_w, conv_b, x_proj_w, dt_proj_w, dt_proj_b, A_log, D):
            b = hidden_states.shape[0]
            x = jnp.einsum('ed,bld->bel', in_proj_w, hidden_states)
            xp = jnp.pad(x, ((0, 0), (0, 0), (DC - 1, 0)))
            xc = jax.lax.conv_general_dilated(xp, conv_w[:, None, :], window_strides=(1,), padding='VALID', dimension_numbers=('NCH', 'OIH', 'NCH'), feature_group_count=DI)
            u = jax.nn.silu(xc + conv_b[None, :, None])
            x_dbl = jnp.einsum('ke,bel->bkl', x_proj_w, u)
            dt_lo = x_dbl[:, :DR]
            Bm = x_dbl[:, DR:DR + DS]
            Cm = x_dbl[:, DR + DS:]
            delta = jax.nn.softplus(jnp.einsum('er,brl->bel', dt_proj_w, dt_lo) + dt_proj_b[None, :, None])
            A = -jnp.exp(A_log)

            def step(state, xs):
                d_t, B_t, C_t, u_t = xs
                dA = jnp.exp(d_t[..., None] * A)
                state = state * dA + (d_t * u_t)[..., None] * B_t[:, None, :]
                y_t = jnp.einsum('ben,bn->be', state, C_t)
                return (state, y_t)
            xs = (jnp.moveaxis(delta, -1, 0), jnp.moveaxis(Bm, -1, 0), jnp.moveaxis(Cm, -1, 0), jnp.moveaxis(u, -1, 0))
            state0 = jnp.zeros((b, DI, DS), delta.dtype)
            _, ys = jax.lax.scan(step, state0, xs)
            y = jnp.moveaxis(ys, 0, -1)
            y = y + D[None, :, None] * u
            y = y * jax.nn.silu(z)
            return jnp.swapaxes(y, 1, 2)
        key = jax.random.key(seed)
        ks = jax.random.split(key, 8)
        hidden_states = jax.random.normal(ks[0], (B, L, DM), jnp.float32)
        z = jax.random.normal(ks[1], (B, DI, L), jnp.float32)
        in_proj_w = jax.random.normal(ks[2], (DI, DM), jnp.float32) * DM ** (-0.5)
        conv_w = jax.random.normal(ks[3], (DI, DC), jnp.float32) * DC ** (-0.5)
        conv_b = jnp.zeros((DI,), jnp.float32)
        x_proj_w = jax.random.normal(ks[4], (DR + 2 * DS, DI), jnp.float32) * DI ** (-0.5)
        dt_std = DR ** (-0.5)
        dt_proj_w = jax.random.uniform(ks[5], (DI, DR), jnp.float32, -dt_std, dt_std)
        dt = jnp.exp(jax.random.uniform(ks[6], (DI,), jnp.float32) * (math.log(DT_MAX) - math.log(DT_MIN)) + math.log(DT_MIN))
        dt = jnp.clip(dt, DT_FLOOR)
        dt_proj_b = dt + jnp.log(-jnp.expm1(-dt))
        A_log = jnp.log(jnp.broadcast_to(jnp.arange(1, DS + 1, dtype=jnp.float32), (DI, DS)))
        D = jnp.ones((DI,), jnp.float32)
        return dict(hidden_states=hidden_states, z=z, in_proj_w=in_proj_w, conv_w=conv_w, conv_b=conv_b, x_proj_w=x_proj_w, dt_proj_w=dt_proj_w, dt_proj_b=dt_proj_b, A_log=A_log, D=D)
    _L0_xattn_all = _L0_xattn_setup()
    _L0_xattn_in = {k: v for k, v in _L0_xattn_all.items() if k in ('in_proj_w', 'conv_w', 'conv_b', 'x_proj_w', 'dt_proj_w', 'dt_proj_b', 'A_log', 'D')}
    del _L0_xattn_all

    def _L0_ffn_setup():
        import jax, jax.numpy as jnp
        import numpy as np
        B, S, D, F, E, SH, K = (2, 512, 512, 256, 16, 2, 2)

        def _experts_all(x, g, gb, w1, b1, w2, b2):
            y = jax.nn.gelu(jnp.einsum('bsd,edf->bsef', x, g) + gb, approximate=False)
            y = y * (jnp.einsum('bsd,edf->bsef', x, w1) + b1)
            return jnp.einsum('bsef,efd->bsed', y, w2) + b2
        key = jax.random.key(seed)
        ks = jax.random.split(key, 8)
        std = 0.02
        mk = lambda k, sh: jax.random.normal(k, sh, jnp.float32) * std
        return {'x': jax.random.normal(ks[0], (B, S, D), jnp.float32), 'wa': mk(ks[1], (D, E)), 'rg': mk(ks[2], (E, D, F)), 'rgb': jnp.zeros((E, F), jnp.float32), 'rw1': mk(ks[3], (E, D, F)), 'rb1': jnp.zeros((E, F), jnp.float32), 'rw2': mk(ks[4], (E, F, D)), 'rb2': jnp.zeros((E, D), jnp.float32), 'sg': mk(ks[5], (SH, D, F)), 'sgb': jnp.zeros((SH, F), jnp.float32), 'sw1': mk(ks[6], (SH, D, F)), 'sb1': jnp.zeros((SH, F), jnp.float32), 'sw2': mk(ks[7], (SH, F, D)), 'sb2': jnp.zeros((SH, D), jnp.float32)}
    _L0_ffn_all = _L0_ffn_setup()
    _L0_ffn_in = {k: v for k, v in _L0_ffn_all.items() if k in ('wa', 'rg', 'rgb', 'rw1', 'rb1', 'rw2', 'rb2', 'sg', 'sgb', 'sw1', 'sb1', 'sw2', 'sb2')}
    del _L0_ffn_all
    return {'x': x, 'ctx_1024': ctx_1024, 'L0_xattn_in_proj_w': _L0_xattn_in['in_proj_w'], 'L0_xattn_conv_w': _L0_xattn_in['conv_w'], 'L0_xattn_conv_b': _L0_xattn_in['conv_b'], 'L0_xattn_x_proj_w': _L0_xattn_in['x_proj_w'], 'L0_xattn_dt_proj_w': _L0_xattn_in['dt_proj_w'], 'L0_xattn_dt_proj_b': _L0_xattn_in['dt_proj_b'], 'L0_xattn_A_log': _L0_xattn_in['A_log'], 'L0_xattn_D': _L0_xattn_in['D'], 'L0_ffn_wa': _L0_ffn_in['wa'], 'L0_ffn_rg': _L0_ffn_in['rg'], 'L0_ffn_rgb': _L0_ffn_in['rgb'], 'L0_ffn_rw1': _L0_ffn_in['rw1'], 'L0_ffn_rb1': _L0_ffn_in['rb1'], 'L0_ffn_rw2': _L0_ffn_in['rw2'], 'L0_ffn_rb2': _L0_ffn_in['rb2'], 'L0_ffn_sg': _L0_ffn_in['sg'], 'L0_ffn_sgb': _L0_ffn_in['sgb'], 'L0_ffn_sw1': _L0_ffn_in['sw1'], 'L0_ffn_sb1': _L0_ffn_in['sb1'], 'L0_ffn_sw2': _L0_ffn_in['sw2'], 'L0_ffn_sb2': _L0_ffn_in['sb2']}

def reference(x, ctx_1024, L0_xattn_in_proj_w, L0_xattn_conv_w, L0_xattn_conv_b, L0_xattn_x_proj_w, L0_xattn_dt_proj_w, L0_xattn_dt_proj_b, L0_xattn_A_log, L0_xattn_D, L0_ffn_wa, L0_ffn_rg, L0_ffn_rgb, L0_ffn_rw1, L0_ffn_rb1, L0_ffn_rw2, L0_ffn_rb2, L0_ffn_sg, L0_ffn_sgb, L0_ffn_sw1, L0_ffn_sb1, L0_ffn_sw2, L0_ffn_sb2):
    import jax
    import jax.numpy as jnp

    def _L0_xattn_ref(hidden_states, z, in_proj_w, conv_w, conv_b, x_proj_w, dt_proj_w, dt_proj_b, A_log, D):
        import jax, jax.numpy as jnp
        import numpy as np
        import math
        B, L, DM = (2, 512, 256)
        DS, DC, EXP = (16, 4, 2)
        DI = EXP * DM
        DR = math.ceil(DM / 16)
        DT_MIN, DT_MAX, DT_FLOOR = (0.001, 0.1, 0.0001)

        def _ssm_forward(hidden_states, z, in_proj_w, conv_w, conv_b, x_proj_w, dt_proj_w, dt_proj_b, A_log, D):
            b = hidden_states.shape[0]
            x = jnp.einsum('ed,bld->bel', in_proj_w, hidden_states)
            xp = jnp.pad(x, ((0, 0), (0, 0), (DC - 1, 0)))
            xc = jax.lax.conv_general_dilated(xp, conv_w[:, None, :], window_strides=(1,), padding='VALID', dimension_numbers=('NCH', 'OIH', 'NCH'), feature_group_count=DI)
            u = jax.nn.silu(xc + conv_b[None, :, None])
            x_dbl = jnp.einsum('ke,bel->bkl', x_proj_w, u)
            dt_lo = x_dbl[:, :DR]
            Bm = x_dbl[:, DR:DR + DS]
            Cm = x_dbl[:, DR + DS:]
            delta = jax.nn.softplus(jnp.einsum('er,brl->bel', dt_proj_w, dt_lo) + dt_proj_b[None, :, None])
            A = -jnp.exp(A_log)

            def step(state, xs):
                d_t, B_t, C_t, u_t = xs
                dA = jnp.exp(d_t[..., None] * A)
                state = state * dA + (d_t * u_t)[..., None] * B_t[:, None, :]
                y_t = jnp.einsum('ben,bn->be', state, C_t)
                return (state, y_t)
            xs = (jnp.moveaxis(delta, -1, 0), jnp.moveaxis(Bm, -1, 0), jnp.moveaxis(Cm, -1, 0), jnp.moveaxis(u, -1, 0))
            state0 = jnp.zeros((b, DI, DS), delta.dtype)
            _, ys = jax.lax.scan(step, state0, xs)
            y = jnp.moveaxis(ys, 0, -1)
            y = y + D[None, :, None] * u
            y = y * jax.nn.silu(z)
            return jnp.swapaxes(y, 1, 2)
        return _ssm_forward(hidden_states, z, in_proj_w, conv_w, conv_b, x_proj_w, dt_proj_w, dt_proj_b, A_log, D)

    def _L0_ffn_ref(x, wa, rg, rgb, rw1, rb1, rw2, rb2, sg, sgb, sw1, sb1, sw2, sb2):
        import jax, jax.numpy as jnp
        import numpy as np
        B, S, D, F, E, SH, K = (2, 512, 512, 256, 16, 2, 2)

        def _experts_all(x, g, gb, w1, b1, w2, b2):
            y = jax.nn.gelu(jnp.einsum('bsd,edf->bsef', x, g) + gb, approximate=False)
            y = y * (jnp.einsum('bsd,edf->bsef', x, w1) + b1)
            return jnp.einsum('bsef,efd->bsed', y, w2) + b2
        aff = jax.nn.sigmoid(jnp.einsum('bsd,de->bse', x, wa))
        topk_p, topk_i = jax.lax.top_k(aff, K)
        topk_p = topk_p / jnp.sum(topk_p, axis=-1, keepdims=True)
        combine = jnp.sum(jax.nn.one_hot(topk_i, E, dtype=x.dtype) * topk_p[..., None], axis=2)
        routed = jnp.einsum('bsed,bse->bsd', _experts_all(x, rg, rgb, rw1, rb1, rw2, rb2), combine)
        shared = jnp.sum(_experts_all(x, sg, sgb, sw1, sb1, sw2, sb2), axis=2)
        return x + shared + routed
    x = x + _L0_xattn_ref(ctx_1024, _layernorm(x, axis=-1), L0_xattn_in_proj_w, L0_xattn_conv_w, L0_xattn_conv_b, L0_xattn_x_proj_w, L0_xattn_dt_proj_w, L0_xattn_dt_proj_b, L0_xattn_A_log, L0_xattn_D)
    x = x + _L0_ffn_ref(_layernorm(x, axis=-1), L0_ffn_wa, L0_ffn_rg, L0_ffn_rgb, L0_ffn_rw1, L0_ffn_rb1, L0_ffn_rw2, L0_ffn_rb2, L0_ffn_sg, L0_ffn_sgb, L0_ffn_sw1, L0_ffn_sb1, L0_ffn_sw2, L0_ffn_sb2)
    return x

_drawn_inputs = setup_inputs


def setup_inputs(seed=0):
    import zlib

    import numpy as np

    out = dict(_drawn_inputs(seed))
    spreads = {'L0_xattn_conv_b': (0.0, 0.1),
     'L0_xattn_D': (1.0, 0.2),
     'L0_ffn_rgb': (0.0, 0.8),
     'L0_ffn_rb1': (0.0, 0.8),
     'L0_ffn_rb2': (0.0, 0.422),
     'L0_ffn_sgb': (0.0, 0.8),
     'L0_ffn_sb1': (0.0, 0.8),
     'L0_ffn_sb2': (0.0, 0.1)}
    factors = {'L0_xattn_dt_proj_w': 4.999, 'L0_ffn_rg': 4.493, 'L0_ffn_rw1': 4.317, 'L0_ffn_rw2': 4.2}
    for name, (base, spread) in spreads.items():
        noise = np.random.default_rng([zlib.crc32(name.encode()), seed]).standard_normal(out[name].shape)
        drawn = base * np.exp(spread * noise) if base else spread * noise
        out[name] = jnp.asarray(drawn.astype(out[name].dtype))
    for name, factor in factors.items():
        out[name] = (out[name] * factor).astype(out[name].dtype)
    return out
```

```python
from contextlib import ExitStack

import concourse.bass as bass
from concourse import mybir

F32 = mybir.dt.float32
I32 = mybir.dt.int32
U32 = mybir.dt.uint32
ALU = mybir.AluOpType
ACT = mybir.ActivationFunctionType
AX_X = mybir.AxisListType.X

P = 128
BANK = 512
B, L, D = 4, 512, 512
DM, DI, DS, DR, DC = 256, 512, 16, 16, 4
E, SH, F, TOPK = 16, 2, 256, 2
T = B * L
NT = T // P
LT = L // P
EC = DI // P
KC = D // P
MC = DM // P
FC = F // P
STEPS = B * DS
NBLK = (T * TOPK + E * (P - 1)) // P
XD = DR + 2 * DS
EPS = 1e-5


def bass_xattn_scan_moe_kernel(nc, x, ctx_t, in_proj_t, conv_w, conv_b, x_proj_t, dt_proj_t, dt_b,
                               a_log, d_skip, wa, r_up, r_b1, r_down, r_b2, s_up, s_bg, s_b1,
                               s_down, s_b2, out):
    xn_dram = nc.dram_tensor("xn_scratch", [T, D], F32, kind="Internal").ap()
    y_dram = nc.dram_tensor("routed_rows", [NBLK * P, D], F32, kind="Internal").ap()
    id_dram = nc.dram_tensor("token_of_slot", [NBLK * P, 1], F32, kind="Internal").ap()

    with ExitStack() as ctx:
        def sb(name, shape, dt=F32):
            return ctx.enter_context(nc.sbuf_tensor(name, shape, dt))

        def sem(name):
            return ctx.enter_context(nc.semaphore(name))

        ps = ctx.enter_context(nc.psum_tensor("ps", [P, 8, BANK], F32))

        r0 = sb("r0", [P, 10240])
        ru = sb("ru", [P, EC * T])
        rd = sb("rd", [P, EC * T])
        rt = sb("rt", [P, NT * DI])
        acc = sb("acc", [P, NT, DI])

        def view(region, start, *shape):
            n = 1
            for s in shape:
                n *= s
            v = region[:, start:start + n]
            if len(shape) == 2:
                v = v.rearrange("p (a b) -> p a b", b=shape[1])
            if len(shape) == 3:
                v = v.rearrange("p (a b c) -> p a b c", b=shape[1], c=shape[2])
            return v

        ctx_sb = view(rt, 0, MC, T)
        inp_sb = view(rt, MC * T, MC, DI)
        u = view(ru, 0, EC, T)
        delta = view(rd, 0, EC, T)
        du_t = view(rt, 0, NT, DI)
        conv = view(r0, 0, 2, L)
        e_abs = view(r0, 0, EC, L)
        relu_v = view(r0, 2048, EC, L)
        one_e = view(r0, 4096, EC, L)
        du = view(r0, 6144, EC, L)
        d_u = view(r0, 8192, EC, L)
        decay = view(r0, 0, 2, EC, L)
        state = view(r0, 4096, 2, EC, L)
        dbu_t = view(ru, 0, 2, LT, DI)
        xb = view(r0, 0, 2, LT, D)
        gate = view(r0, 4096, EC, L)
        xn = view(r0, 6144, LT, D)
        xn_t = view(rd, 0, KC, T)
        sup_sb = view(ru, 4096, SH, KC * 2 * F).rearrange("p s (k f) -> p s k f", k=KC)
        sdown_sb = view(ru, 0, SH, FC * D).rearrange("p s (c d) -> p s c d", c=FC)
        sy_t = view(ru, 2048, SH * FC, L)
        comb_t = view(r0, 8192, NT, P)
        hb = view(rd, 0, 2, 2 * F)
        hg = view(rd, 1024, 2, F)
        hy = view(rd, 1536, 2, F)
        hy_t = view(rd, 2048, 2, F)
        y_sb = view(rd, 2560, 2, D)
        b1_all = view(rt, 0, E, 2 * F)
        up_w = view(r0, 0, 2, KC * 2 * F).rearrange("p s (k f) -> p s k f", k=KC)
        down_w = view(r0, 4096, 2, FC * D).rearrange("p s (c d) -> p s c d", c=FC)
        xg = view(r0, 6144, 2, D)
        xg_t = view(r0, 7168, 2, D)
        y1 = view(r0, 0, 2, D)
        y2 = view(r0, 1024, 2, D)
        o_sb = view(r0, 2048, 2, D)

        ident = sb("ident", [P, P])
        before = sb("before", [P, P])
        ones = sb("ones", [P, P])
        xproj_sb = sb("xproj_sb", [P, EC, XD])
        dtproj_sb = sb("dtproj_sb", [DR, DI])
        x_dbl = sb("x_dbl", [XD, L])
        convw_sb = sb("convw_sb", [P, EC, DC])
        convb_sb = sb("convb_sb", [P, EC])
        dtb_sb = sb("dtb_sb", [P, EC])
        dskip_sb = sb("dskip_sb", [P, EC])
        nega = sb("nega", [P, EC, DS])
        bc = sb("bc", [P, NT, XD])
        bcol = sb("bcol", [P, 2, LT])
        wa_sb = sb("wa_sb", [P, KC, E])
        sbg_sb = sb("sbg_sb", [P, SH, FC])
        sb1_sb = sb("sb1_sb", [P, SH, FC])
        sb2_sb = sb("sb2_sb", [P, SH, D])
        rb2_sb = sb("rb2_sb", [E, D])
        stats = sb("stats", [P, 4, 6])
        meanvar = sb("meanvar", [P, 4, 2])
        rstd = sb("rstd", [P, 4])
        shift = sb("shift", [P, 4])
        var_eps = sb("var_eps", [P, 4])
        stats2 = sb("stats2", [P, 4, 6])
        meanvar2 = sb("meanvar2", [P, 4, 2])
        var_eps2 = sb("var_eps2", [P, 4])
        rstd2 = sb("rstd2", [P, 4])
        minus_half = sb("minus_half", [P, 4])
        sg = sb("sg", [P, 2, L])
        aff = sb("aff", [P, NT, E])
        top = sb("top", [P, NT, 8])
        topi = sb("topi", [P, NT, 8], U32)
        topf = sb("topf", [P, NT, TOPK])
        cnt_blk = sb("cnt_blk", [P, E])
        wsum = sb("wsum", [P, NT])
        wk = sb("wk", [P, TOPK, NT])
        iota_i = sb("iota_i", [P, 48], I32)
        iota_f = sb("iota_f", [P, 48])
        tok_i = sb("tok_i", [P, NT], I32)
        tok_f = sb("tok_f", [P, NT])
        hot = sb("hot", [P, TOPK, NT, E])
        member = sb("member", [P, NT, E])
        comb_parts = sb("comb_parts", [P, TOPK, NT, E])
        comb = sb("comb", [P, NT, E])
        full = sb("full", [P, E, E])
        nblk = sb("nblk", [P, E])
        blk_end = sb("blk_end", [P, E])
        slot_base = sb("slot_base", [P, E])
        place = sb("place", [P, NT, E])
        picked = sb("picked", [P, TOPK, NT, E])
        slot_f = sb("slot_f", [P, TOPK, NT])
        slot = sb("slot", [P, TOPK, NT], U32)
        blk_cmp = sb("blk_cmp", [P, NBLK, E])
        blk_f = sb("blk_f", [P, NBLK])
        blk_e = sb("blk_e", [P, NBLK], I32)
        ids_r = sb("ids_r", [NBLK, P])
        ids = sb("ids", [P, NBLK], U32)

        names = """
        waits_passed loaded_first loaded_scan loaded_bias loaded_shared id_zero
        consts_zeroed consts_made alog_exp nega_made
        proj_ready conv_first conv_tap conv_done u_ready
        xd_ready xd_copied bc_ready bc_copied dt_ready dt_read abs_made exp_made onep_made lost_made
        ln_made relu_less delta_ready du_made dskip_made dut_ready dut_copied dsk_ready dsk_copied
        decay_ready bcol_ready dbut_ready dbu_ready state_ready st_ready mac_done
        x_even x_odd ln1_stat ln1_aggr ln1_var ln1_rstd ln1_ready gate_ready gt_ready gated x1_ready
        ln2_stat ln2_aggr ln2_var ln2_rstd xn_ready xnt_ready xnt_copied base_xn base_ready logits_ready
        xn_stored b2s_made
        aff_ready top_made topi_made topf_made hot_made member_made rank_ready count_ready
        cnt_made full_made nblk_made end_made base_made place_made picked_made slotf_made slots_ready
        wsum_made wrec_made weights_ready comb_part comb_ready combt_ready combt_copied
        blkc_made blkf_made blkm_made blocks_ready ids_stored ids_loaded idst_ready ids_ready
        sh_ready sg_ready sy_ready so_ready so_added b2_ready b2_added
        up_even up_odd down_even down_odd xg_even xg_odd xgt_ready xgt_copied h_ready hb_ready hg_ready
        hy_ready hyt_ready hyt_copied o_ready y_ready y_even y_odd
        g_even g_odd half_done out_ready o_even o_odd
        """.split()
        S = {n: sem(n) for n in names}

        def tile(tensor, t):
            return tensor[:, bass.ds(t, 1)].rearrange("p o n -> p (o n)")

        def since(eng, semaphore, count):
            if not (isinstance(count, int) and count <= 0):
                eng.wait_ge(semaphore, count)

        def wait_apart(eng, semaphore, count):
            eng.wait_ge(semaphore, count)
            eng.sem_inc(S["waits_passed"], 1)

        block = ctx.enter_context(nc.Block())
        ds = bass.ds

        @block.sync
        def _(sp):
            s = S
            sp.dma_start(inp_sb, in_proj_t).then_inc(s["loaded_first"], 16)
            sp.dma_start(convw_sb[:], conv_w).then_inc(s["loaded_first"], 16)
            sp.dma_start(convb_sb[:], conv_b).then_inc(s["loaded_first"], 16)
            sp.dma_start(ctx_sb, ctx_t).then_inc(s["loaded_first"], 16)
            sp.dma_start(xproj_sb[:], x_proj_t).then_inc(s["loaded_scan"], 16)
            sp.dma_start(dtproj_sb[:], dt_proj_t).then_inc(s["loaded_scan"], 16)
            sp.dma_start(dtb_sb[:], dt_b).then_inc(s["loaded_scan"], 16)
            sp.dma_start(dskip_sb[:], d_skip).then_inc(s["loaded_scan"], 16)
            sp.dma_start(nega[:], a_log).then_inc(s["loaded_scan"], 16)
            sp.dma_start(wa_sb[:], wa).then_inc(s["loaded_shared"], 16)
            sp.dma_start(sbg_sb[:], s_bg).then_inc(s["loaded_shared"], 16)
            sp.dma_start(sb1_sb[:], s_b1).then_inc(s["loaded_shared"], 16)
            sp.dma_start(sb2_sb[:], s_b2.unsqueeze(0).to_broadcast([P, SH, D])).then_inc(s["loaded_shared"], 16)
            sp.dma_start(rb2_sb[:], r_b2).then_inc(s["loaded_shared"], 16)
            sp.wait_ge(s["dut_copied"], NT)
            sp.wait_ge(s["dsk_copied"], NT)
            sp.dma_start(sup_sb, s_up).then_inc(s["loaded_shared"], 16)
            sp.wait_ge(s["mac_done"], LT * STEPS)
            sp.dma_start(xb[:, 0], x[0]).then_inc(s["x_even"], 16)
            sp.dma_start(xb[:, 1], x[1]).then_inc(s["x_odd"], 16)
            sp.dma_start(sdown_sb, s_down).then_inc(s["loaded_shared"], 16)
            sp.dma_start(b1_all, r_b1.unsqueeze(0).to_broadcast([P, E, 2 * F])).then_inc(s["loaded_bias"], 16)
            for b in range(B):
                for lt in range(LT):
                    sp.wait_ge(s["xn_ready"], b * LT + lt + 1)
                    sp.dma_start(xn_dram[(b * LT + lt) * P:(b * LT + lt + 1) * P, :],
                                 xn[:, lt, :]).then_inc(s["xn_stored"], 16)
                if b + 2 < B:
                    sp.wait_ge(s["x1_ready"], (b + 1) * LT)
                    sp.wait_ge(s["gate_ready"], (b + 1) * EC)
                    sp.dma_start(xb[:, b % 2], x[b + 2]).then_inc(s["x_odd" if b % 2 else "x_even"], 16)
            sp.wait_ge(s["ids_stored"], 16 * TOPK * NT)
            sp.dma_start(ids_r[:], id_dram.rearrange("(j p) o -> j (p o)", p=P)).then_inc(s["ids_loaded"], 16)
            sp.wait_ge(s["blocks_ready"], 1)
            sp.wait_ge(s["base_ready"], NT)

            def load_up(j, half):
                e = sp.value_load(blk_e[0:1, ds(j, 1)], min_val=0, max_val=E - 1)
                sp.dma_start(up_w[:, half], r_up[ds(e, 1)]).then_inc(s["up_odd" if half else "up_even"], 16)

            def load_down(j, half):
                e = sp.value_load(blk_e[0:1, ds(j, 1)], min_val=0, max_val=E - 1)
                sp.dma_start(down_w[:, half], r_down[ds(e, 1)]).then_inc(s["down_odd" if half else "down_even"], 16)

            for j in range(2):
                load_up(j, j)
                load_down(j, j)
            with sp.Fori(0, (NBLK - 2) // 2) as jj:
                for half in range(2):
                    wait_apart(sp, s["h_ready"], 2 * jj + half + 1)
                    load_up(2 * jj + half + 2, half)
                    wait_apart(sp, s["o_ready"], 2 * jj + half + 1)
                    load_down(2 * jj + half + 2, half)
            sp.wait_ge(s["h_ready"], NBLK - 2)
            load_up(NBLK - 1, (NBLK - 1) % 2)
            sp.wait_ge(s["o_ready"], NBLK - 2)
            load_down(NBLK - 1, (NBLK - 1) % 2)
            for t in range(NT):
                sp.wait_ge(s["out_ready"], t + 1)
                sp.dma_start(out[t * P:(t + 1) * P, :], o_sb[:, t % 2]).then_inc(s["o_odd" if t % 2 else "o_even"], 16)
            sp.wait_ge(s["o_even"], 16 * (NT // 2))
            sp.wait_ge(s["o_odd"], 16 * (NT // 2))

        @block.gpsimd
        def _(pool):
            s = S
            pool.memset(ident[:], 0.0).then_inc(s["consts_zeroed"], 1)
            pool.memset(ones[:], 1.0).then_inc(s["consts_zeroed"], 1)
            pool.memset(ids_r[:], 0.0).then_inc(s["consts_zeroed"], 1)
            pool.memset(minus_half[:], -0.5).then_inc(s["consts_zeroed"], 1)
            pool.wait_ge(s["consts_zeroed"], 4)
            pool.affine_select(out=ident[:], in_=ident[:], compare_op=ALU.not_equal, fill=1.0, base=0,
                               pattern=[[-1, P]], channel_multiplier=1).then_inc(s["consts_made"], 1)
            pool.affine_select(out=before[:], in_=ones[:], compare_op=ALU.is_gt, fill=0.0, base=0,
                               pattern=[[1, P]], channel_multiplier=-1).then_inc(s["consts_made"], 1)
            pool.iota(iota_i[:], [[1, 48]], base=0, channel_multiplier=0).then_inc(s["consts_made"], 1)
            pool.iota(tok_i[:], [[P, NT]], base=0, channel_multiplier=1).then_inc(s["consts_made"], 1)
            pool.dma_start(id_dram.rearrange("(j p) o -> j (p o)", p=P), ids_r[:]).then_inc(s["id_zero"], 16)
            pool.wait_ge(s["consts_made"], 4)
            pool.tensor_copy(iota_f[:], iota_i[:]).then_inc(s["consts_made"], 1)
            pool.tensor_copy(tok_f[:], tok_i[:]).then_inc(s["consts_made"], 1)
            with pool.Fori(0, B) as b:
                pool.wait_ge(s["delta_ready"], b + 1)
                pool.wait_ge(s["dut_ready"], LT * b)
                pool.tensor_tensor(du, delta[:, :, ds(b * L, L)], u[:, :, ds(b * L, L)],
                                   ALU.mult).then_inc(s["du_made"], 1)
            pool.wait_ge(s["dsk_copied"], NT)
            pool.wait_ge(s["dut_copied"], NT)
            def turned_products(b, n, half):
                k = b * DS + n
                since(pool, s["dbu_ready"], EC * (k - 1))
                pool.tensor_copy(bcol[:, half], bc[:, b * LT:(b + 1) * LT, ds(n + DR, 1)].rearrange(
                    "p t o -> p (t o)")).then_inc(s["bcol_ready"], 1)
                wait_apart(pool, s["bcol_ready"], k + 1)
                for lt in range(LT):
                    pool.tensor_scalar(dbu_t[:, half, lt], du_t[:, b * LT + lt], bcol[:, half, lt:lt + 1],
                                       1.0, ALU.mult, ALU.mult).then_inc(s["dbut_ready"], 1)

            for b in range(B):
                if b == 0:
                    turned_products(0, 0, 0)
                    turned_products(0, 1, 1)
                with pool.Fori(1 if b == 0 else 0, DS // 2) as nn:
                    for half in range(2):
                        turned_products(b, 2 * nn + half, half)
            pool.wait_ge(s["loaded_shared"], 16 * 7)
            pool.tensor_tensor(sb2_sb[:, 0], sb2_sb[:, 0], sb2_sb[:, 1], ALU.add).then_inc(s["b2s_made"], 1)
            pool.wait_ge(s["b2s_made"], 1)
            with pool.Fori(0, B) as b:
                pool.wait_ge(s["gate_ready"], EC * b)
                pool.wait_ge(s["ln1_var"], b + 1)
                pool.tensor_tensor(rstd[:], var_eps[:], minus_half[:], ALU.pow).then_inc(s["ln1_rstd"], 1)
                pool.wait_ge(s["ln2_var"], b + 1)
                pool.tensor_tensor(rstd2[:], var_eps2[:], minus_half[:], ALU.pow).then_inc(s["ln2_rstd"], 1)
                for lt in range(LT):
                    t = b * LT + lt
                    pool.wait_ge(s["xn_ready"], t + 1)
                    pool.tensor_tensor(tile(acc, t), tile(acc, t), xn[:, lt], ALU.add).then_inc(s["base_xn"], 1)
                    wait_apart(pool, s["base_xn"], t + 1)
                    pool.tensor_tensor(tile(acc, t), tile(acc, t), sb2_sb[:, 0], ALU.add).then_inc(s["base_ready"], 1)
            pool.wait_ge(s["slots_ready"], 1)
            pool.wait_ge(s["id_zero"], 16)
            for k in range(TOPK):
                for t in range(NT):
                    pool.indirect_dma_start(out=id_dram, out_offset=bass.IndirectOffsetOnAxis(slot[:, k, t:t + 1], 0),
                                            in_=tok_f[:, t:t + 1], in_offset=None).then_inc(s["ids_stored"], 16)
            pool.wait_ge(s["ids_ready"], 1)
            pool.wait_ge(s["xn_stored"], 16 * NT)

            def fetch(j):
                pool.indirect_dma_start(out=xg[:, j % 2], out_offset=None, in_=xn_dram,
                                        in_offset=bass.IndirectOffsetOnAxis(ids[:, j:j + 1], 0)).then_inc(
                                            s["xg_odd" if j % 2 else "xg_even"], 16)

            fetch(0)
            fetch(1)
            for j in range(NBLK):
                if j + 2 < NBLK:
                    pool.wait_ge(s["xgt_ready"], j + 1)
                    fetch(j + 2)
                pool.wait_ge(s["y_ready"], j + 1)
                pool.dma_start(y_dram[j * P:(j + 1) * P, :], y_sb[:, j % 2]).then_inc(s["y_odd" if j % 2 else "y_even"], 16)
            pool.wait_ge(s["y_even"], 16 * ((NBLK + 1) // 2))
            pool.wait_ge(s["y_odd"], 16 * (NBLK // 2))
            for t in range(NT):
                if t >= 2:
                    pool.wait_ge(s["out_ready"], t - 1)
                g = s["g_odd" if t % 2 else "g_even"]
                pool.indirect_dma_start(out=y1[:, t % 2], out_offset=None, in_=y_dram,
                                        in_offset=bass.IndirectOffsetOnAxis(slot[:, 0, t:t + 1], 0)).then_inc(g, 16)
                pool.indirect_dma_start(out=y2[:, t % 2], out_offset=None, in_=y_dram,
                                        in_offset=bass.IndirectOffsetOnAxis(slot[:, 1, t:t + 1], 0)).then_inc(g, 16)

        @block.scalar
        def _(act):
            s = S
            act.wait_ge(s["loaded_scan"], 16 * 5)
            act.activation(nega[:], nega[:], ACT.Exp).then_inc(s["alog_exp"], 1)
            act.wait_ge(s["alog_exp"], 1)
            act.mul(nega[:], nega[:], -1.0).then_inc(s["nega_made"], 1)
            act.wait_ge(s["loaded_first"], 16 * 4)
            act.preload_act_table(ACT.Silu)
            with act.Fori(0, B) as b:
                for ec in range(EC):
                    i = b * EC + ec
                    act.wait_ge(s["proj_ready"], i + 1)
                    act.activation(conv[:, ec % 2], ps[:, ec % 2], ACT.Identity, bias=convb_sb[:, ec:ec + 1],
                                   scale=convw_sb[:, ec, DC - 1:DC]).then_inc(s["conv_first"], 1)
                    act.wait_ge(s["conv_done"], i + 1)
                    act.activation(u[:, ec, ds(b * L, L)], conv[:, ec % 2], ACT.Silu).then_inc(s["u_ready"], 1)
            act.preload_act_table_set("natural_log_exp_and_others")
            with act.Fori(0, B) as b:
                act.wait_ge(s["xd_ready"], b + 1)
                act.copy(x_dbl[:], ps[0:XD, 2]).then_inc(s["xd_copied"], 1)
                act.wait_ge(s["bc_ready"], b + 1)
                act.copy(bc[:, ds(b * LT, LT)].rearrange("p t c -> p (t c)"),
                         ps[:, 3, 0:LT * XD]).then_inc(s["bc_copied"], 1)
                act.wait_ge(s["delta_ready"], b)
                for ec in range(EC):
                    act.wait_ge(s["dt_ready"], b * EC + ec + 1)
                    act.activation(e_abs[:, ec], ps[:, 4 + ec % 2], ACT.Abs, bias=dtb_sb[:, ec:ec + 1]).then_inc(s["abs_made"], 1)
                    act.activation(relu_v[:, ec], ps[:, 4 + ec % 2], ACT.Relu, bias=dtb_sb[:, ec:ec + 1]).then_inc(s["dt_read"], 1)
                act.wait_ge(s["abs_made"], EC * (b + 1))
                act.activation(e_abs, e_abs, ACT.Exp, scale=-1.0).then_inc(s["exp_made"], 1)
                act.wait_ge(s["lost_made"], b + 1)
                act.activation(one_e, one_e, ACT.Ln).then_inc(s["ln_made"], 1)
                for lt in range(LT):
                    t = b * LT + lt
                    act.wait_ge(s["dut_ready"], t + 1)
                    act.copy(tile(du_t, t), ps[:, 6]).then_inc(s["dut_copied"], 1)
                    act.wait_ge(s["dsk_ready"], t + 1)
                    act.copy(tile(acc, t), ps[:, 7]).then_inc(s["dsk_copied"], 1)
            act.wait_ge(s["nega_made"], 1)
            act.wait_ge(s["delta_ready"], B)

            def decays(k, half):
                for ec in range(EC):
                    since(act, s["state_ready"], EC * (k - 2) + ec + 1)
                    act.activation(decay[:, half, ec], delta[:, ec, ds((k // DS) * L, L)], ACT.Exp,
                                   scale=nega[:, ec, ds(k % DS, 1)]).then_inc(s["decay_ready"], 1)

            decays(0, 0)
            decays(1, 1)
            with act.Fori(1, STEPS // 2) as kk:
                for half in range(2):
                    decays(2 * kk + half, half)
            act.preload_act_table(ACT.Silu)
            with act.Fori(0, B // 2) as bb:
                for half in range(2):
                    b = 2 * bb + half
                    act.wait_ge(s["ln1_ready"], b + 1)
                    act.wait_ge(s["gt_ready"], LT * b)
                    for ec in range(EC):
                        act.activation(gate[:, ec], xb[:, half, ec], ACT.Silu, bias=shift[:, ec:ec + 1],
                                       scale=rstd[:, ec:ec + 1]).then_inc(s["gate_ready"], 1)
                    for lt in range(LT):
                        t = b * LT + lt
                        act.wait_ge(s["xnt_ready"], t + 1)
                        act.copy(xn_t[:, :, ds(t * P, P)], ps[:, 2 + lt % 2].rearrange(
                            "p (k n) -> p k n", n=P)).then_inc(s["xnt_copied"], 1)
            act.wait_ge(s["logits_ready"], NT)
            act.activation(aff[:].rearrange("p t e -> p (t e)"), ps[:, 4, 0:NT * E], ACT.Sigmoid).then_inc(s["aff_ready"], 1)
            for r in range(NT // 4):
                act.wait_ge(s["combt_ready"], r + 1)
                act.copy(comb_t[0:E, 4 * r:4 * r + 4].rearrange("p t n -> p (t n)"), ps[0:E, 5]).then_inc(s["combt_copied"], 1)
            act.preload_act_table(ACT.Gelu)
            with act.Fori(0, B) as b:
                for q in range(SH * FC):
                    act.wait_ge(s["sh_ready"], b * SH * FC + q + 1)
                    act.activation(sg[:, q % 2], ps[:, 2 * (q % 2)], ACT.Gelu,
                                   bias=sbg_sb[:, q // FC, q % FC:q % FC + 1]).then_inc(s["sg_ready"], 1)

            def turn_tokens(j, half):
                act.wait_ge(s["xgt_ready"], j + 1)
                since(act, s["h_ready"], j - 1)
                act.copy(xg_t[:, half], ps[:, 4]).then_inc(s["xgt_copied"], 1)

            def hidden_gate(j, half):
                act.wait_ge(s["hb_ready"], j + 1)
                act.activation(hg[:, half], hb[:, half, 0:F], ACT.Gelu).then_inc(s["hg_ready"], 1)

            def turn_hidden(j, half):
                act.wait_ge(s["hyt_ready"], j + 1)
                act.copy(hy_t[:, half], ps[:, 2 + half, 0:F]).then_inc(s["hyt_copied"], 1)

            def block_result(j, half, pair):
                act.wait_ge(s["o_ready"], j + 1)
                since(act, s["y_odd" if half else "y_even"], 16 * pair)
                act.copy(y_sb[:, half], ps[:, 6 + half]).then_inc(s["y_ready"], 1)

            turn_tokens(0, 0)
            turn_tokens(1, 1)
            hidden_gate(0, 0)
            turn_hidden(0, 0)
            turn_tokens(2, 0)
            hidden_gate(1, 1)
            turn_hidden(1, 1)
            block_result(0, 0, 0)
            turn_tokens(3, 1)
            with act.Fori(1, (NBLK - 3) // 2) as jj:
                for half in range(2):
                    j = 2 * jj + half
                    hidden_gate(j, half)
                    turn_hidden(j, half)
                    block_result(j - 1, 1 - half, jj - 1 if half == 0 else jj)
                    turn_tokens(j + 2, half)
            for j in range(NBLK - 3, NBLK):
                hidden_gate(j, j % 2)
                turn_hidden(j, j % 2)
                block_result(j - 1, (j - 1) % 2, (j - 1) // 2)
                if j + 2 < NBLK:
                    turn_tokens(j + 2, j % 2)
            block_result(NBLK - 1, (NBLK - 1) % 2, (NBLK - 1) // 2)

        @block.vector
        def _(dve):
            s = S
            with dve.Fori(0, B) as b:
                for ec in range(EC):
                    i = b * EC + ec
                    dve.wait_ge(s["conv_first"], i + 1)
                    for back in range(1, DC):
                        if back > 1:
                            dve.wait_ge(s["conv_tap"], (DC - 2) * i + back - 1)
                        dve.scalar_tensor_tensor(
                            out=conv[:, ec % 2, back:L], in0=ps[:, ec % 2, 0:L - back],
                            scalar=convw_sb[:, ec, DC - 1 - back:DC - back], in1=conv[:, ec % 2, back:L],
                            op0=ALU.mult, op1=ALU.add).then_inc(s["conv_done" if back == DC - 1 else "conv_tap"], 1)
            dve.wait_ge(s["loaded_scan"], 16 * 5)
            dve.wait_ge(s["u_ready"], NT)
            with dve.Fori(0, B) as b:
                dve.wait_ge(s["dsk_ready"], LT * b)
                for ec in range(EC):
                    dve.tensor_scalar(d_u[:, ec], u[:, ec, ds(b * L, L)], dskip_sb[:, ec:ec + 1], None,
                                      ALU.mult).then_inc(s["dskip_made"], 1)
                dve.wait_ge(s["exp_made"], b + 1)
                dve.tensor_scalar(one_e, e_abs, 1.0, None, ALU.add).then_inc(s["onep_made"], 1)
                dve.wait_ge(s["onep_made"], b + 1)
                dve.scalar_tensor_tensor(out=e_abs, in0=one_e, scalar=-1.0, in1=e_abs, op0=ALU.add,
                                         op1=ALU.subtract).then_inc(s["lost_made"], 1)
                dve.wait_ge(s["lost_made"], b + 1)
                dve.wait_ge(s["dt_read"], EC * (b + 1))
                dve.tensor_tensor(relu_v, relu_v, e_abs, ALU.subtract).then_inc(s["relu_less"], 1)
                dve.wait_ge(s["ln_made"], b + 1)
                dve.wait_ge(s["relu_less"], b + 1)
                dve.tensor_tensor(delta[:, :, ds(b * L, L)], relu_v, one_e, ALU.add).then_inc(s["delta_ready"], 1)

            def scans(k, half):
                since(dve, s["st_ready"], LT * (k - 1))
                for ec in range(EC):
                    dve.wait_ge(s["decay_ready"], EC * k + ec + 1)
                    dve.wait_ge(s["dbu_ready"], EC * k + ec + 1)
                    dve.tensor_tensor_scan(state[:, half, ec], decay[:, half, ec], ps[:, ec], 0.0, ALU.mult,
                                           ALU.add).then_inc(s["state_ready"], 1)

            def sums(k):
                since(dve, s["mac_done"], LT * k)
                for lt in range(LT):
                    t = (k // DS) * LT + lt
                    dve.wait_ge(s["st_ready"], LT * k + lt + 1)
                    dve.scalar_tensor_tensor(
                        out=tile(acc, t), in0=ps[:, 4 + lt], scalar=tile(bc, t)[:, ds(k % DS + DR + DS, 1)],
                        in1=tile(acc, t), op0=ALU.mult, op1=ALU.add).then_inc(s["mac_done"], 1)

            scans(0, 0)
            scans(1, 1)
            sums(0)
            with dve.Fori(1, STEPS // 2) as kk:
                for half in range(2):
                    scans(2 * kk + half, half)
                    sums(2 * kk + half - 1)
            sums(STEPS - 1)
            dve.wait_ge(s["mac_done"], LT * STEPS)
            with dve.Fori(0, B // 2) as bb:
                for half in range(2):
                    b = 2 * bb + half
                    dve.wait_ge(s["x_odd" if half else "x_even"], 16 * (bb + 1))
                    for ec in range(EC):
                        dve.bn_stats(stats[:, ec], xb[:, half, ec]).then_inc(s["ln1_stat"], 1)
                    wait_apart(dve, s["ln1_stat"], EC * (b + 1))
                    for ec in range(EC):
                        dve.bn_aggr(meanvar[:, ec], stats[:, ec]).then_inc(s["ln1_aggr"], 1)
                    dve.wait_ge(s["ln1_aggr"], EC * (b + 1))
                    dve.wait_ge(s["gate_ready"], EC * b)
                    dve.tensor_scalar(var_eps[:], meanvar[:, :, 1], EPS, None, ALU.add).then_inc(s["ln1_var"], 1)
                    dve.wait_ge(s["ln1_rstd"], b + 1)
                    dve.scalar_tensor_tensor(out=shift[:], in0=meanvar[:, :, 0], scalar=-1.0, in1=rstd[:],
                                             op0=ALU.mult, op1=ALU.mult).then_inc(s["ln1_ready"], 1)
                    dve.wait_ge(s["xn_stored"], 16 * LT * b)
                    dve.wait_ge(s["xnt_ready"], LT * b)
                    dve.wait_ge(s["base_xn"], LT * b)
                    for lt in range(LT):
                        t = b * LT + lt
                        dve.wait_ge(s["gt_ready"], t + 1)
                        dve.tensor_tensor(tile(acc, t), ps[:, lt % 2], tile(acc, t), ALU.mult).then_inc(s["gated"], 1)
                        dve.wait_ge(s["gated"], t + 1)
                        dve.tensor_tensor(tile(acc, t), tile(acc, t), xb[:, half, lt], ALU.add).then_inc(s["x1_ready"], 1)
                        wait_apart(dve, s["x1_ready"], t + 1)
                        dve.bn_stats(stats2[:, lt], tile(acc, t)).then_inc(s["ln2_stat"], 1)
                        wait_apart(dve, s["ln2_stat"], t + 1)
                        dve.bn_aggr(meanvar2[:, lt], stats2[:, lt]).then_inc(s["ln2_aggr"], 1)
                    dve.wait_ge(s["ln2_aggr"], LT * (b + 1))
                    dve.tensor_scalar(var_eps2[:], meanvar2[:, :, 1], EPS, None, ALU.add).then_inc(s["ln2_var"], 1)
                    dve.wait_ge(s["ln2_rstd"], b + 1)
                    for lt in range(LT):
                        dve.tensor_scalar(xn[:, lt], tile(acc, b * LT + lt), meanvar2[:, lt, 0:1], rstd2[:, lt:lt + 1],
                                          ALU.subtract, ALU.mult).then_inc(s["xn_ready"], 1)
            dve.wait_ge(s["consts_made"], 6)
            dve.wait_ge(s["aff_ready"], 1)
            for t in range(NT):
                dve.max(top[:, t], aff[:, t]).then_inc(s["top_made"], 1)
            dve.wait_ge(s["top_made"], NT)
            for t in range(NT):
                dve.max_index(topi[:, t], top[:, t], aff[:, t]).then_inc(s["topi_made"], 1)
            dve.wait_ge(s["topi_made"], NT)
            dve.tensor_copy(topf[:], topi[:, :, 0:TOPK]).then_inc(s["topf_made"], 1)
            dve.wait_ge(s["topf_made"], 1)
            every_e = iota_f[:, 0:E].unsqueeze(1).to_broadcast([P, NT, E])
            for k in range(TOPK):
                dve.tensor_tensor(hot[:, k], every_e, topf[:, :, k:k + 1].to_broadcast([P, NT, E]),
                                  ALU.is_equal).then_inc(s["hot_made"], 1)
            dve.wait_ge(s["hot_made"], TOPK)
            dve.tensor_tensor(member[:], hot[:, 0], hot[:, 1], ALU.add).then_inc(s["member_made"], 1)
            dve.wait_ge(s["count_ready"], 1)
            dve.tensor_scalar(cnt_blk[:], ps[:, 6, 0:E], 1.0 / P, None, ALU.mult).then_inc(s["cnt_made"], 1)
            dve.wait_ge(s["cnt_made"], 1)
            dve.tensor_tensor(full[:], cnt_blk[:].unsqueeze(2).to_broadcast([P, E, E]),
                              iota_f[:, 0:E].unsqueeze(1).to_broadcast([P, E, E]), ALU.is_gt).then_inc(s["full_made"], 1)
            dve.wait_ge(s["full_made"], 1)
            dve.tensor_reduce(nblk[:], full[:], AX_X, ALU.add).then_inc(s["nblk_made"], 1)
            dve.wait_ge(s["nblk_made"], 1)
            dve.tensor_tensor_scan(blk_end[:], ones[:, 0:E], nblk[:], 0.0, ALU.mult, ALU.add).then_inc(s["end_made"], 1)
            dve.wait_ge(s["end_made"], 1)
            dve.tensor_tensor(slot_base[:], blk_end[:], nblk[:], ALU.subtract).then_inc(s["base_made"], 1)
            dve.wait_ge(s["base_made"], 1)
            dve.wait_ge(s["rank_ready"], 1)
            dve.scalar_tensor_tensor(out=place[:], in0=slot_base[:].unsqueeze(1).to_broadcast([P, NT, E]),
                                     scalar=float(P), in1=ps[:, 5, 0:NT * E].rearrange("p (t e) -> p t e", e=E),
                                     op0=ALU.mult, op1=ALU.add).then_inc(s["place_made"], 1)
            dve.wait_ge(s["place_made"], 1)
            for k in range(TOPK):
                dve.tensor_tensor(picked[:, k], hot[:, k], place[:], ALU.mult).then_inc(s["picked_made"], 1)
            dve.wait_ge(s["picked_made"], TOPK)
            dve.tensor_reduce(slot_f[:], picked[:], AX_X, ALU.add).then_inc(s["slotf_made"], 1)
            dve.wait_ge(s["slotf_made"], 1)
            dve.tensor_copy(slot[:], slot_f[:]).then_inc(s["slots_ready"], 1)
            dve.tensor_tensor(blk_cmp[:], blk_end[:].unsqueeze(1).to_broadcast([P, NBLK, E]),
                              iota_f[:, 0:NBLK].unsqueeze(2).to_broadcast([P, NBLK, E]), ALU.is_le).then_inc(s["blkc_made"], 1)
            dve.wait_ge(s["blkc_made"], 1)
            dve.tensor_reduce(blk_f[:], blk_cmp[:], AX_X, ALU.add).then_inc(s["blkf_made"], 1)
            dve.wait_ge(s["blkf_made"], 1)
            dve.tensor_scalar(blk_e[:], blk_f[:], float(E - 1), None, ALU.min).then_inc(s["blocks_ready"], 1)
            dve.tensor_tensor(wsum[:], top[:, :, 0], top[:, :, 1], ALU.add).then_inc(s["wsum_made"], 1)
            dve.wait_ge(s["wsum_made"], 1)
            dve.reciprocal(wsum[:], wsum[:]).then_inc(s["wrec_made"], 1)
            dve.wait_ge(s["wrec_made"], 1)
            for k in range(TOPK):
                dve.tensor_tensor(wk[:, k], top[:, :, k], wsum[:], ALU.mult).then_inc(s["weights_ready"], 1)
            dve.wait_ge(s["weights_ready"], TOPK)
            for k in range(TOPK):
                dve.tensor_tensor(comb_parts[:, k], hot[:, k], wk[:, k].unsqueeze(2).to_broadcast([P, NT, E]),
                                  ALU.mult).then_inc(s["comb_part"], 1)
            dve.wait_ge(s["comb_part"], TOPK)
            dve.tensor_tensor(comb[:], comb_parts[:, 0], comb_parts[:, 1], ALU.add).then_inc(s["comb_ready"], 1)
            dve.wait_ge(s["loaded_shared"], 16 * 7)
            with dve.Fori(0, B) as b:
                dve.wait_ge(s["so_ready"], LT * b)
                for q in range(SH * FC):
                    dve.wait_ge(s["sg_ready"], b * SH * FC + q + 1)
                    dve.scalar_tensor_tensor(out=sy_t[:, q], in0=ps[:, 2 * (q % 2) + 1],
                                             scalar=sb1_sb[:, q // FC, q % FC:q % FC + 1], in1=sg[:, q % 2],
                                             op0=ALU.add, op1=ALU.mult).then_inc(s["sy_ready"], 1)
                for lt in range(LT):
                    t = b * LT + lt
                    dve.wait_ge(s["so_ready"], t + 1)
                    dve.wait_ge(s["base_ready"], t + 1)
                    dve.tensor_tensor(tile(acc, t), ps[:, 6 + lt % 2], tile(acc, t), ALU.add).then_inc(s["so_added"], 1)
            dve.wait_ge(s["so_added"], NT)
            for t in range(NT):
                dve.wait_ge(s["b2_ready"], t + 1)
                dve.tensor_tensor(acc[:, t], ps[:, t % 2], acc[:, t], ALU.add).then_inc(s["b2_added"], 1)
            dve.wait_ge(s["idst_ready"], 1)
            dve.tensor_copy(ids[:], ps[:, 5, 0:NBLK]).then_inc(s["ids_ready"], 1)
            dve.wait_ge(s["blocks_ready"], 1)
            dve.wait_ge(s["loaded_bias"], 16)

            def hidden(j, half):
                e = dve.value_load(blk_e[0:1, ds(j, 1)], min_val=0, max_val=E - 1)
                dve.wait_ge(s["h_ready"], j + 1)
                dve.tensor_tensor(hb[:, half], ps[:, half], tile(b1_all, e), ALU.add).then_inc(s["hb_ready"], 1)
                since(dve, s["hyt_ready"], j - 1)
                dve.wait_ge(s["hg_ready"], j + 1)
                dve.wait_ge(s["hb_ready"], j + 1)
                dve.tensor_tensor(hy[:, half], hg[:, half], hb[:, half, F:2 * F], ALU.mult).then_inc(s["hy_ready"], 1)

            hidden(0, 0)
            hidden(1, 1)
            with dve.Fori(1, NBLK // 2) as jj:
                for half in range(2):
                    hidden(2 * jj + half, half)
            hidden(NBLK - 1, (NBLK - 1) % 2)
            dve.wait_ge(s["b2_added"], NT)
            for t in range(NT):
                half = t % 2
                dve.wait_ge(s["g_odd" if half else "g_even"], 16 * TOPK * (t // 2 + 1))
                dve.scalar_tensor_tensor(out=y1[:, half], in0=y1[:, half], scalar=wk[:, 0, t:t + 1], in1=acc[:, t],
                                         op0=ALU.mult, op1=ALU.add).then_inc(s["half_done"], 1)
                dve.wait_ge(s["half_done"], t + 1)
                since(dve, s["o_odd" if half else "o_even"], 16 * (t // 2))
                dve.scalar_tensor_tensor(out=o_sb[:, half], in0=y2[:, half], scalar=wk[:, 1, t:t + 1], in1=y1[:, half],
                                         op0=ALU.mult, op1=ALU.add).then_inc(s["out_ready"], 1)

        @block.tensor
        def _(pe):
            s = S
            pe.wait_ge(s["loaded_first"], 16 * 4)
            with pe.Fori(0, B) as b:
                for ec in range(EC):
                    i = b * EC + ec
                    if ec >= 2:
                        pe.wait_ge(s["conv_done"], i - 1)
                    else:
                        pe.wait_ge(s["conv_done"], b * EC)
                    for mc in range(MC):
                        mm = pe.matmul(ps[:, ec % 2], inp_sb[:, mc, ec * P:(ec + 1) * P], ctx_sb[:, mc, ds(b * L, L)],
                                       start=(mc == 0), stop=(mc == MC - 1))
                    mm.then_inc(s["proj_ready"], 1)
            pe.wait_ge(s["loaded_scan"], 16 * 5)
            pe.wait_ge(s["consts_made"], 2)
            with pe.Fori(0, B) as b:
                pe.wait_ge(s["u_ready"], EC * (b + 1))
                pe.wait_ge(s["xd_copied"], b)
                for ec in range(EC):
                    mm = pe.matmul(ps[0:XD, 2], xproj_sb[:, ec, :], u[:, ec, ds(b * L, L)],
                                   start=(ec == 0), stop=(ec == EC - 1))
                mm.then_inc(s["xd_ready"], 1)
                pe.wait_ge(s["bc_copied"], b)
                wait_apart(pe, s["xd_copied"], b + 1)
                for lt in range(LT):
                    mm = pe.transpose(ps[:, 3, lt * XD:(lt + 1) * XD], x_dbl[:, lt * P:(lt + 1) * P], ident[0:XD, 0:XD])
                mm.then_inc(s["bc_ready"], 1)
                for ec in range(EC):
                    if ec >= 2:
                        pe.wait_ge(s["dt_read"], b * EC + ec - 1)
                    else:
                        pe.wait_ge(s["dt_read"], b * EC)
                    pe.matmul(ps[:, 4 + ec % 2], dtproj_sb[:, ec * P:(ec + 1) * P], x_dbl[0:DR, :],
                              start=True, stop=True).then_inc(s["dt_ready"], 1)
                pe.wait_ge(s["dskip_made"], EC * (b + 1))
                pe.wait_ge(s["du_made"], b + 1)
                for lt in range(LT):
                    t = b * LT + lt
                    pe.wait_ge(s["dut_copied"], t)
                    for ec in range(EC):
                        mm = pe.transpose(ps[:, 6, ec * P:(ec + 1) * P], du[:, ec, lt * P:(lt + 1) * P], ident[:])
                    mm.then_inc(s["dut_ready"], 1)
                    pe.wait_ge(s["dsk_copied"], t)
                    for ec in range(EC):
                        mm = pe.transpose(ps[:, 7, ec * P:(ec + 1) * P], d_u[:, ec, lt * P:(lt + 1) * P], ident[:])
                    mm.then_inc(s["dsk_ready"], 1)

            def products(k, half):
                pe.wait_ge(s["dbut_ready"], LT * (k + 1))
                for ec in range(EC):
                    since(pe, s["state_ready"], EC * (k - 1) + ec + 1)
                    for lt in range(LT):
                        mm = pe.transpose(ps[:, ec, lt * P:(lt + 1) * P], dbu_t[:, half, lt, ec * P:(ec + 1) * P], ident[:])
                    mm.then_inc(s["dbu_ready"], 1)

            def states(k, half):
                pe.wait_ge(s["state_ready"], EC * (k + 1))
                for lt in range(LT):
                    since(pe, s["mac_done"], LT * (k - 1) + lt + 1)
                    for ec in range(EC):
                        mm = pe.transpose(ps[:, 4 + lt, ec * P:(ec + 1) * P], state[:, half, ec, lt * P:(lt + 1) * P], ident[:])
                    mm.then_inc(s["st_ready"], 1)

            products(0, 0)
            products(1, 1)
            states(0, 0)
            with pe.Fori(1, STEPS // 2) as kk:
                for half in range(2):
                    products(2 * kk + half, half)
                    states(2 * kk + half - 1, 1 - half)
            states(STEPS - 1, 1)
            pe.wait_ge(s["loaded_shared"], 16 * 7)
            pe.wait_ge(s["mac_done"], LT * STEPS)
            for b in range(B):
                pe.wait_ge(s["gate_ready"], EC * (b + 1))
                for lt in range(LT):
                    t = b * LT + lt
                    since(pe, s["gated"], t - 1)
                    for ec in range(EC):
                        mm = pe.transpose(ps[:, lt % 2, ec * P:(ec + 1) * P], gate[:, ec, lt * P:(lt + 1) * P], ident[:])
                    mm.then_inc(s["gt_ready"], 1)
                for lt in range(LT):
                    t = b * LT + lt
                    pe.wait_ge(s["xn_ready"], t + 1)
                    since(pe, s["xnt_copied"], t - 1)
                    for kc in range(KC):
                        mm = pe.transpose(ps[:, 2 + lt % 2, kc * P:(kc + 1) * P], xn[:, lt, kc * P:(kc + 1) * P], ident[:])
                    mm.then_inc(s["xnt_ready"], 1)
                    pe.wait_ge(s["xnt_copied"], t + 1)
                    for kc in range(KC):
                        mm = pe.matmul(ps[:, 4, t * E:(t + 1) * E], xn_t[:, kc, t * P:(t + 1) * P], wa_sb[:, kc, :],
                                       start=(kc == 0), stop=(kc == KC - 1))
                    mm.then_inc(s["logits_ready"], 1)
            pe.wait_ge(s["member_made"], 1)
            for t in range(NT):
                mm = pe.matmul(ps[:, 6, 0:E], ones[:], member[:, t], start=(t == 0), stop=(t == NT - 1))
            mm.then_inc(s["count_ready"], 1)
            pe.matmul(ps[:, 5, 0:NT * E], before[:], member[:].rearrange("p t e -> p (t e)"), start=True, stop=False)
            for t in range(NT - 1):
                mm = pe.matmul(ps[:, 5, (t + 1) * E:NT * E], ones[:],
                               member[:, t:t + 1].to_broadcast([P, NT - 1 - t, E]), start=False, stop=(t == NT - 2))
            mm.then_inc(s["rank_ready"], 1)
            pe.wait_ge(s["place_made"], 1)
            pe.wait_ge(s["comb_ready"], 1)
            for r in range(NT // 4):
                since(pe, s["combt_copied"], r)
                for i in range(4):
                    mm = pe.matmul(ps[0:E, 5, i * P:(i + 1) * P], comb[:, 4 * r + i], ident[:], start=True, stop=True)
                mm.then_inc(s["combt_ready"], 1)
            with pe.Fori(0, B) as b:
                for q in range(SH * FC):
                    e, fc = q // FC, q % FC
                    if q >= 2:
                        pe.wait_ge(s["sy_ready"], b * SH * FC + q - 1)
                    else:
                        pe.wait_ge(s["sy_ready"], b * SH * FC)
                    for part in range(2):
                        col = part * F + fc * P
                        for kc in range(KC):
                            mm = pe.matmul(ps[:, 2 * (q % 2) + part], sup_sb[:, e, kc, col:col + P], xn_t[:, kc, ds(b * L, L)],
                                           start=(kc == 0), stop=(kc == KC - 1))
                    mm.then_inc(s["sh_ready"], 1)
                pe.wait_ge(s["sy_ready"], SH * FC * (b + 1))
                for lt in range(LT):
                    if lt >= 2:
                        pe.wait_ge(s["so_added"], b * LT + lt - 1)
                    else:
                        pe.wait_ge(s["so_added"], b * LT)
                    for q in range(SH * FC):
                        mm = pe.matmul(ps[:, 6 + lt % 2], sy_t[:, q, lt * P:(lt + 1) * P], sdown_sb[:, q // FC, q % FC, :],
                                       start=(q == 0), stop=(q == SH * FC - 1))
                    mm.then_inc(s["so_ready"], 1)
            pe.wait_ge(s["combt_copied"], NT // 4)
            for t in range(NT):
                since(pe, s["b2_added"], t - 1)
                pe.matmul(ps[:, t % 2], comb_t[0:E, t], rb2_sb[:], start=True, stop=True).then_inc(s["b2_ready"], 1)
            pe.wait_ge(s["ids_loaded"], 16)
            pe.transpose(ps[:, 5, 0:NBLK], ids_r[:], ident[0:NBLK, 0:NBLK]).then_inc(s["idst_ready"], 1)
            pe.wait_ge(s["b2_added"], NT)

            def turn_tokens(j, half, pair):
                pe.wait_ge(s["xg_odd" if half else "xg_even"], 16 * (pair + 1))
                since(pe, s["xgt_copied"], j)
                for kc in range(KC):
                    mm = pe.transpose(ps[:, 4, kc * P:(kc + 1) * P], xg[:, half, kc * P:(kc + 1) * P], ident[:])
                mm.then_inc(s["xgt_ready"], 1)

            def up(j, half, pair):
                pe.wait_ge(s["xgt_copied"], j + 1)
                pe.wait_ge(s["up_odd" if half else "up_even"], 16 * (pair + 1))
                since(pe, s["hb_ready"], j - 1)
                for kc in range(KC):
                    mm = pe.matmul(ps[:, half], xg_t[:, half, kc * P:(kc + 1) * P], up_w[:, half, kc, :],
                                   start=(kc == 0), stop=(kc == KC - 1))
                mm.then_inc(s["h_ready"], 1)

            def turn_hidden(j, half):
                pe.wait_ge(s["hy_ready"], j + 1)
                since(pe, s["hyt_copied"], j - 1)
                for fc in range(FC):
                    mm = pe.transpose(ps[:, 2 + half, fc * P:(fc + 1) * P], hy[:, half, fc * P:(fc + 1) * P], ident[:])
                mm.then_inc(s["hyt_ready"], 1)

            def down(j, half, pair):
                pe.wait_ge(s["hyt_copied"], j + 1)
                pe.wait_ge(s["down_odd" if half else "down_even"], 16 * (pair + 1))
                since(pe, s["y_ready"], j - 1)
                for fc in range(FC):
                    mm = pe.matmul(ps[:, 6 + half], hy_t[:, half, fc * P:(fc + 1) * P], down_w[:, half, fc, :],
                                   start=(fc == 0), stop=(fc == FC - 1))
                mm.then_inc(s["o_ready"], 1)

            turn_tokens(0, 0, 0)
            turn_tokens(1, 1, 0)
            up(0, 0, 0)
            up(1, 1, 0)
            turn_hidden(0, 0)
            turn_tokens(2, 0, 1)
            up(2, 0, 1)
            turn_hidden(1, 1)
            down(0, 0, 0)
            turn_tokens(3, 1, 1)
            with pe.Fori(1, (NBLK - 3) // 2) as jj:
                for half in range(2):
                    j = 2 * jj + half
                    up(j + 1, 1 - half, jj + half)
                    turn_hidden(j, half)
                    down(j - 1, 1 - half, jj - 1 + half)
                    turn_tokens(j + 2, half, jj + 1)
            for j in range(NBLK - 3, NBLK):
                if j + 1 < NBLK:
                    up(j + 1, (j + 1) % 2, (j + 1) // 2)
                turn_hidden(j, j % 2)
                down(j - 1, (j - 1) % 2, (j - 1) // 2)
                if j + 2 < NBLK:
                    turn_tokens(j + 2, j % 2, (j + 2) // 2)
            down(NBLK - 1, (NBLK - 1) % 2, (NBLK - 1) // 2)


def _columns(v, n):
    return v.reshape(n, P).T


def _rows(w, n):
    import numpy as np
    w = w.reshape(*w.shape[:-2], n, P, w.shape[-1])
    return np.swapaxes(w, -3, -2)


def kernel(**inputs):
    import numpy as np
    import concourse.bacc as bacc
    from concourse.bass_utils import run_bass_kernel_spmd

    i = {k.replace("L0_xattn_", "").replace("L0_ffn_", "ffn_"): np.asarray(v) for k, v in inputs.items()}
    laid = {
        "x": i["x"].reshape(B, LT, P, D).transpose(0, 2, 1, 3),
        "ctx_t": _rows(i["ctx_1024"].reshape(T, DM).T, MC),
        "in_proj_t": _rows(i["in_proj_w"].T, MC),
        "conv_w": _rows(i["conv_w"], EC),
        "conv_b": _columns(i["conv_b"], EC),
        "x_proj_t": _rows(i["x_proj_w"].T, EC),
        "dt_proj_t": i["dt_proj_w"].T,
        "dt_b": _columns(i["dt_proj_b"], EC),
        "a_log": _rows(i["A_log"], EC),
        "d_skip": _columns(i["D"], EC),
        "wa": _rows(i["ffn_wa"], KC),
        "r_up": _rows(np.concatenate([i["ffn_rg"], i["ffn_rw1"]], axis=2), KC).reshape(E, P, KC * 2 * F),
        "r_b1": np.concatenate([i["ffn_rgb"], i["ffn_rb1"]], axis=1),
        "r_down": _rows(i["ffn_rw2"], FC).reshape(E, P, FC * D),
        "r_b2": i["ffn_rb2"],
        "s_up": _rows(np.concatenate([i["ffn_sg"], i["ffn_sw1"]], axis=2), KC).transpose(1, 0, 2, 3),
        "s_bg": i["ffn_sgb"].reshape(SH, FC, P).transpose(2, 0, 1),
        "s_b1": i["ffn_sb1"].reshape(SH, FC, P).transpose(2, 0, 1),
        "s_down": _rows(i["ffn_sw2"], FC).transpose(1, 0, 2, 3),
        "s_b2": i["ffn_sb2"],
    }
    nc = bacc.Bacc("TRN2", target_bir_lowering=False, num_devices=1)
    arrays, args = {}, []
    for name, a in laid.items():
        a = np.ascontiguousarray(a)
        arrays[f"in_{name}"] = a
        args.append(nc.dram_tensor(f"in_{name}", a.shape, mybir.dt.from_np(a.dtype), kind="ExternalInput").ap())
    out = nc.dram_tensor("out", [T, D], F32, kind="ExternalOutput").ap()
    bass_xattn_scan_moe_kernel(nc, *args, out)
    r = run_bass_kernel_spmd(nc, [arrays], core_ids=[0])
    return r.results[0]["out"].reshape(B, L, D)
```

```python
from contextlib import ExitStack

import concourse.bass as bass
from concourse import mybir

F32 = mybir.dt.float32
I32 = mybir.dt.int32
U32 = mybir.dt.uint32
ALU = mybir.AluOpType
ACT = mybir.ActivationFunctionType
AX_X = mybir.AxisListType.X

P = 128
BANK = 512
B, L, D = 4, 512, 512
DM, DI, DS, DR, DC = 256, 512, 16, 16, 4
E, SH, F, TOPK = 16, 2, 256, 2
T = B * L
NT = T // P
LT = L // P
EC = DI // P
KC = D // P
MC = DM // P
FC = F // P
STEPS = B * DS
NBLK = (T * TOPK + E * (P - 1)) // P
SLOTS = 3
RING = 4
XD = DR + 2 * DS
EPS = 1e-5


def bass_xattn_scan_moe_kernel(nc, x, ctx_t, in_proj_t, conv_w, conv_b, x_proj_t, dt_proj_t, dt_b,
                               a_log, d_skip, wa, r_up, r_b1, r_down, r_b2, s_up, s_bg, s_b1,
                               s_down, s_b2, out):
    xn_dram = nc.dram_tensor("xn_scratch", [T + P, D], F32, kind="Internal").ap()
    pair_dram = nc.dram_tensor("pair_of_slot", [NBLK * P, 2], F32, kind="Internal").ap()

    with ExitStack() as ctx:
        def sb(name, shape, dt=F32):
            return ctx.enter_context(nc.sbuf_tensor(name, shape, dt))

        def sem(name):
            return ctx.enter_context(nc.semaphore(name))

        ps = ctx.enter_context(nc.psum_tensor("ps", [P, 8, BANK], F32))

        r0 = sb("r0", [P, 10240])
        ru = sb("ru", [P, EC * T])
        rd = sb("rd", [P, EC * T])
        rt = sb("rt", [P, NT * DI])
        acc = sb("acc", [P, NT, DI])

        def view(region, start, *shape):
            n = 1
            for s in shape:
                n *= s
            v = region[:, start:start + n]
            if len(shape) == 2:
                v = v.rearrange("p (a b) -> p a b", b=shape[1])
            if len(shape) == 3:
                v = v.rearrange("p (a b c) -> p a b c", b=shape[1], c=shape[2])
            return v

        ctx_sb = view(rt, 0, MC, T)
        inp_sb = view(rt, MC * T, MC, DI)
        u = view(ru, 0, EC, T)
        delta = view(rd, 0, EC, T)
        du_t = view(rt, 0, NT, DI)
        x_dbl = view(rt, 3 * T, B, L)
        diag_d = view(rd, 7168, EC, P)
        no_rows = view(rd, 7680, D)
        conv = view(r0, 8192, 4, L)
        e_abs = view(r0, 0, 2, EC, L)
        one_e = view(r0, 4096, 2, EC, L)
        PROJ_BANK = DT_BANK = (0, 1, 4, 5)
        TURN_BANK = (6, 7, 2, 3)
        decay = view(r0, 0, 2, EC, L)
        state = view(r0, 4096, 2, EC, L)
        dbu_t = view(ru, 0, 2, LT, DI)
        xb = (view(r0, 8192, LT, D), view(r0, 0, LT, D))
        xn = (view(r0, 6144, LT, D), view(r0, 2048, LT, D))
        gate = view(r0, 4096, EC, L)
        SIDE_BANK = (4, 5, 6, 7)
        xn_t = view(rd, 0, KC, T)
        sup_sb = view(ru, 4096, SH, KC * 2 * F).rearrange("p s (k f) -> p s k f", k=KC)
        sdown_sb = view(ru, 0, SH, FC * D).rearrange("p s (c d) -> p s c d", c=FC)
        sy_t = view(ru, 2048, SH * FC, L)
        comb_t = view(r0, 9216, 2, 4, P)
        hb = view(rd, 0, 2, 2 * F)
        hg = view(rd, 1024, 2, F)
        hy = view(rd, 1536, 2, F)
        hy_t = view(rd, 2048, 2, F)
        y_sb = view(rd, 2560, 2, D)
        b1_all = view(rt, 0, E, 2 * F)
        xg = view(rd, 3584, RING, D)
        xg_t = view(rd, 3584 + RING * D, 2, D)
        up_w = view(r0, 0, SLOTS, KC * 2 * F).rearrange("p s (k f) -> p s k f", k=KC)
        down_w = view(r0, SLOTS * KC * 2 * F, SLOTS, FC * D).rearrange("p s (c d) -> p s c d", c=FC)

        ident = sb("ident", [P, P])
        before = sb("before", [P, P])
        ones = sb("ones", [P, P])
        xproj_sb = sb("xproj_sb", [P, EC, XD])
        dtproj_sb = sb("dtproj_sb", [DR, DI])
        convw_sb = sb("convw_sb", [P, EC, DC])
        convb_sb = sb("convb_sb", [P, EC])
        dtb_sb = sb("dtb_sb", [P, EC])
        dskip_sb = sb("dskip_sb", [P, EC])
        nega = sb("nega", [P, EC, DS])
        bc = sb("bc", [P, NT, XD])
        bcol = sb("bcol", [P, 2, LT])
        wa_sb = sb("wa_sb", [P, KC, E])
        sbg_sb = sb("sbg_sb", [P, SH, FC])
        sb1_sb = sb("sb1_sb", [P, SH, FC])
        sb2_sb = sb("sb2_sb", [P, SH, D])
        rb2_sb = sb("rb2_sb", [E, D])
        stats = sb("stats", [P, 4, 6])
        meanvar = sb("meanvar", [P, 4, 2])
        rstd = sb("rstd", [P, 4])
        shift = sb("shift", [P, 4])
        var_eps = sb("var_eps", [P, 4])
        stats2 = sb("stats2", [P, 4, 6])
        meanvar2 = sb("meanvar2", [P, 4, 2])
        var_eps2 = sb("var_eps2", [P, 4])
        rstd2 = sb("rstd2", [P, 4])
        minus_half = sb("minus_half", [P, 4])
        sg = sb("sg", [P, 2, L])
        aff = sb("aff", [P, NT, E])
        top = sb("top", [P, NT, 8])
        topi = sb("topi", [P, NT, 8], U32)
        topf = sb("topf", [P, NT, TOPK])
        cnt_blk = sb("cnt_blk", [P, E])
        wsum = sb("wsum", [P, NT])
        pair = sb("pair", [P, TOPK, NT, 2])
        pad_i = sb("pad_i", [NBLK, P], I32)
        iota_i = sb("iota_i", [P, 48], I32)
        iota_f = sb("iota_f", [P, 48])
        tok_i = sb("tok_i", [P, NT], I32)
        tok_f = sb("tok_f", [P, NT])
        hot = sb("hot", [P, TOPK, NT, E])
        member = sb("member", [P, NT, E])
        comb_parts = sb("comb_parts", [P, TOPK, NT, E])
        comb = sb("comb", [P, NT, E])
        full = sb("full", [P, E, E])
        nblk = sb("nblk", [P, E])
        blk_end = sb("blk_end", [P, E])
        slot_base = sb("slot_base", [P, E])
        place = sb("place", [P, NT, E])
        picked = sb("picked", [P, TOPK, NT, E])
        slot_f = sb("slot_f", [P, TOPK, NT])
        slot = sb("slot", [P, TOPK, NT], U32)
        blk_cmp = sb("blk_cmp", [P, NBLK, E])
        blk_f = sb("blk_f", [P, NBLK])
        blk_e = sb("blk_e", [P, NBLK], I32)
        blk_new = sb("blk_new", [P, NBLK])
        blk_run = sb("blk_run", [P, NBLK])
        blk_load = sb("blk_load", [P, NBLK], I32)
        blk_slot = sb("blk_slot", [P, NBLK], I32)
        pair_r = sb("pair_r", [NBLK, P, 2])
        ids = sb("ids", [P, NBLK], U32)
        row_w = sb("row_w", [P, NBLK])

        names = """
        waits_passed loaded_first loaded_scan loaded_bias loaded_shared id_zero
        ctx_0 ctx_1 ctx_2 ctx_3
        consts_zeroed consts_made diag_made alog_exp nega_made
        proj_ready conv_first conv_tap conv_done u_ready
        xd_ready xd_copied bc_ready bc_copied dt_ready dt_read abs_made exp_made onep_made lost_made
        ln_made relu_less delta_ready du_made dut_ready dut_copied_a dut_copied_v dsk_ready dsk_copied
        decay_ready bcol_ready dbut_ready dbu_ready state_ready st_ready mac_done
        x_even x_odd ln1_stat ln1_aggr ln1_var ln1_rstd ln1_ready gate_ready gt_ready gated x1_ready
        ln2_stat ln2_aggr ln2_var ln2_rstd xn_ready xnt_ready xnt_copied base_xn base_ready logits_ready
        xn_even_stored xn_odd_stored b2s_made
        logits_copied aff_ready top_made topi_made topf_made hot_made member_made rank_ready count_ready
        cnt_made full_made nblk_made end_made base_made place_made picked_made slotf_made slots_ready
        wsum_made wrec_made weights_ready comb_part comb_ready combt_ready combt_copied
        blkc_made blkf_made blkm_made new_made run_made blocks_ready pair_made ids_stored ids_loaded idst_ready ids_ready
        base_stored pad_stored weights_moved
        sh_ready sg_ready sy_ready so_ready so_added b2_ready b2_added
        up_0 up_1 up_2 up_3 down_0 down_1 down_2 down_3 xg_0 xg_1 xg_2 xg_3 xgt_ready xgt_copied h_ready
        hb_ready hg_ready hy_ready hyt_ready hyt_copied o_ready y_ready y_even y_odd
        """.split()
        S = {n: sem(n) for n in names}

        def tile(tensor, t):
            return tensor[:, bass.ds(t, 1)].rearrange("p o n -> p (o n)")

        def since(eng, semaphore, count):
            if not (isinstance(count, int) and count <= 0):
                eng.wait_ge(semaphore, count)

        def wait_apart(eng, semaphore, count):
            eng.wait_ge(semaphore, count)
            eng.sem_inc(S["waits_passed"], 1)

        block = ctx.enter_context(nc.Block())
        ds = bass.ds

        @block.sync
        def _(sp):
            s = S
            sp.dma_start(inp_sb, in_proj_t).then_inc(s["loaded_first"], 16)
            sp.dma_start(convw_sb[:], conv_w).then_inc(s["loaded_first"], 16)
            sp.dma_start(convb_sb[:], conv_b).then_inc(s["loaded_first"], 16)
            for b in range(B):
                sp.dma_start(ctx_sb[:, :, b * L:(b + 1) * L], ctx_t[:, :, b * L:(b + 1) * L]).then_inc(s[f"ctx_{b}"], 16)
            sp.dma_start(xproj_sb[:], x_proj_t).then_inc(s["loaded_scan"], 16)
            sp.dma_start(dtproj_sb[:], dt_proj_t).then_inc(s["loaded_scan"], 16)
            sp.dma_start(dtb_sb[:], dt_b).then_inc(s["loaded_scan"], 16)
            sp.dma_start(dskip_sb[:], d_skip).then_inc(s["loaded_scan"], 16)
            sp.dma_start(nega[:], a_log).then_inc(s["loaded_scan"], 16)
            sp.dma_start(wa_sb[:], wa).then_inc(s["loaded_shared"], 16)
            sp.dma_start(sbg_sb[:], s_bg).then_inc(s["loaded_shared"], 16)
            sp.dma_start(sb1_sb[:], s_b1).then_inc(s["loaded_shared"], 16)
            sp.dma_start(sb2_sb[:], s_b2.unsqueeze(0).to_broadcast([P, SH, D])).then_inc(s["loaded_shared"], 16)
            sp.dma_start(rb2_sb[:], r_b2).then_inc(s["loaded_shared"], 16)
            sp.wait_ge(s["u_ready"], NT)
            sp.dma_start(xb[0], x[0]).then_inc(s["x_even"], 16)
            sp.wait_ge(s["dut_ready"], NT)
            sp.dma_start(sup_sb, s_up).then_inc(s["loaded_shared"], 16)
            sp.wait_ge(s["mac_done"], LT * STEPS)
            sp.dma_start(xb[1], x[1]).then_inc(s["x_odd"], 16)
            sp.dma_start(sdown_sb, s_down).then_inc(s["loaded_shared"], 16)
            sp.dma_start(b1_all, r_b1.unsqueeze(0).to_broadcast([P, E, 2 * F])).then_inc(s["loaded_bias"], 16)
            for b in range(B):
                if b + 2 < B:
                    sp.wait_ge(s["x1_ready"], (b + 1) * LT)
                    sp.wait_ge(s["gate_ready"], (b + 1) * EC)
                    sp.dma_start(xb[b % 2], x[b + 2]).then_inc(s["x_odd" if b % 2 else "x_even"], 16)
                for lt in range(LT):
                    t = b * LT + lt
                    sp.wait_ge(s["xn_ready"], t + 1)
                    sp.dma_start(xn_dram[t * P:(t + 1) * P, :], xn[b % 2][:, lt, :]).then_inc(s["xn_odd_stored" if b % 2 else "xn_even_stored"], 16)
            sp.wait_ge(s["blocks_ready"], 2)
            sp.wait_ge(s["base_ready"], NT)
            sp.wait_ge(s["xnt_ready"], NT)
            sp.wait_ge(s["xn_even_stored"], 16 * NT // 2)
            sp.wait_ge(s["xn_odd_stored"], 16 * NT // 2)

            def load(weights, r_weights, loaded, j, r):
                e = sp.value_load(blk_e[0:1, ds(j, 1)], min_val=0, max_val=E - 1)
                new = sp.value_load(blk_load[0:1, ds(j, 1)], min_val=0, max_val=1)
                slot_j = sp.value_load(blk_slot[0:1, ds(j, 1)], min_val=0, max_val=SLOTS - 1)
                sp.dma_start(weights[:, ds(slot_j, 1)], r_weights[ds(e, 1)], cond=new).then_inc(s[f"{loaded}_{r}"], 16)

            def load_up(j, r):
                if not isinstance(j, int) or j >= SLOTS:
                    wait_apart(sp, s["h_ready"], j - SLOTS + 1)
                load(up_w, r_up, "up", j, r)

            def load_down(j, r):
                if not isinstance(j, int) or j >= SLOTS:
                    wait_apart(sp, s["o_ready"], j - SLOTS + 1)
                load(down_w, r_down, "down", j, r)

            load_up(0, 0)
            load_up(1, 1)
            load_up(2, 2)
            load_down(0, 0)
            sp.wait_ge(s["ids_stored"], 16 * TOPK * NT)
            sp.dma_start(pair_r[:].rearrange("j p o -> j (p o)"),
                         pair_dram.rearrange("(j p) o -> j (p o)", p=P)).then_inc(s["ids_loaded"], 16)
            for j in range(1, RING):
                load_up(j + 2, (j + 2) % RING)
                load_down(j, j)
            with sp.Fori(1, (NBLK - 2) // RING) as jj:
                for r in range(RING):
                    load_up(RING * jj + r + 2, (r + 2) % RING)
                    load_down(RING * jj + r, r)
            for j in range((NBLK - 2) // RING * RING, NBLK):
                if j + 2 < NBLK:
                    load_up(j + 2, (j + 2) % RING)
                load_down(j, j % RING)

        @block.gpsimd
        def _(pool):
            s = S
            pool.memset(ident[:], 0.0).then_inc(s["consts_zeroed"], 1)
            pool.memset(ones[:], 1.0).then_inc(s["consts_zeroed"], 1)
            pool.memset(pair_r[:], 0.0).then_inc(s["consts_zeroed"], 1)
            pool.memset(no_rows, 0.0).then_inc(s["consts_zeroed"], 1)
            pool.iota(pad_i[:], [[1, P]], base=T, channel_multiplier=0).then_inc(s["consts_zeroed"], 1)
            pool.memset(minus_half[:], -0.5).then_inc(s["consts_zeroed"], 1)
            pool.wait_ge(s["consts_zeroed"], 6)
            pool.affine_select(out=ident[:], in_=ident[:], compare_op=ALU.not_equal, fill=1.0, base=0,
                               pattern=[[-1, P]], channel_multiplier=1).then_inc(s["consts_made"], 1)
            pool.affine_select(out=before[:], in_=ones[:], compare_op=ALU.is_gt, fill=0.0, base=0,
                               pattern=[[1, P]], channel_multiplier=-1).then_inc(s["consts_made"], 1)
            pool.iota(iota_i[:], [[1, 48]], base=0, channel_multiplier=0).then_inc(s["consts_made"], 1)
            pool.iota(tok_i[:], [[P, NT]], base=0, channel_multiplier=1).then_inc(s["consts_made"], 1)
            pool.tensor_copy(pair_r[:, :, 0], pad_i[:]).then_inc(s["consts_made"], 1)
            pool.wait_ge(s["consts_made"], 5)
            pool.dma_start(xn_dram[T:T + P, :], no_rows).then_inc(s["pad_stored"], 16)
            pool.dma_start(out[T:T + P, :], no_rows).then_inc(s["pad_stored"], 16)
            pool.dma_start(pair_dram.rearrange("(j p) o -> j (p o)", p=P),
                           pair_r[:].rearrange("j p o -> j (p o)")).then_inc(s["id_zero"], 16)
            pool.tensor_copy(iota_f[:], iota_i[:]).then_inc(s["consts_made"], 1)
            pool.tensor_copy(tok_f[:], tok_i[:]).then_inc(s["consts_made"], 1)
            pool.wait_ge(s["loaded_scan"], 16 * 5)
            for ec in range(EC):
                pool.tensor_scalar(diag_d[:, ec], ident[:], dskip_sb[:, ec:ec + 1], 1.0, ALU.mult,
                                   ALU.mult).then_inc(s["diag_made"], 1)

            def less_lost(b):
                pool.wait_ge(s["lost_made"], b + 1)
                pool.wait_ge(s["dt_read"], EC * (b + 1))
                d = delta[:, :, b * L:(b + 1) * L]
                pool.tensor_tensor(d, d, e_abs[:, b % 2], ALU.subtract).then_inc(s["relu_less"], 1)

            def delta_u(b):
                pool.wait_ge(s["delta_ready"], b + 1)
                pool.wait_ge(s["xd_ready"], b + 1)
                pool.wait_ge(s["dsk_ready"], LT * (b + 1))
                ub = u[:, :, b * L:(b + 1) * L]
                pool.tensor_tensor(ub, delta[:, :, b * L:(b + 1) * L], ub, ALU.mult).then_inc(s["du_made"], 1)

            less_lost(0)
            for b in range(1, B):
                less_lost(b)
                delta_u(b - 1)

            def rstd_first(b):
                pool.wait_ge(s["ln1_var"], b + 1)
                since(pool, s["gate_ready"], EC * b)
                pool.tensor_tensor(rstd[:], var_eps[:], minus_half[:], ALU.pow).then_inc(s["ln1_rstd"], 1)

            rstd_first(0)
            delta_u(B - 1)
            pool.wait_ge(s["dut_copied_a"], NT // 2)
            pool.wait_ge(s["dut_copied_v"], NT // 2)
            pool.wait_ge(s["bc_copied"], B)

            def turned_products(b, n, half):
                k = b * DS + n
                since(pool, s["dbu_ready"], EC * (k - 1))
                pool.tensor_copy(bcol[:, half], bc[:, b * LT:(b + 1) * LT, ds(n + DR, 1)].rearrange(
                    "p t o -> p (t o)")).then_inc(s["bcol_ready"], 1)
                wait_apart(pool, s["bcol_ready"], k + 1)
                for lt in range(LT):
                    pool.tensor_scalar(dbu_t[:, half, lt], du_t[:, b * LT + lt], bcol[:, half, lt:lt + 1],
                                       1.0, ALU.mult, ALU.mult).then_inc(s["dbut_ready"], 1)

            for b in range(B):
                if b == 0:
                    turned_products(0, 0, 0)
                    turned_products(0, 1, 1)
                with pool.Fori(1 if b == 0 else 0, DS // 2) as nn:
                    for half in range(2):
                        turned_products(b, 2 * nn + half, half)
            pool.wait_ge(s["loaded_shared"], 16 * 7)
            pool.tensor_tensor(sb2_sb[:, 0], sb2_sb[:, 0], sb2_sb[:, 1], ALU.add).then_inc(s["b2s_made"], 1)
            pool.wait_ge(s["b2s_made"], 1)

            def rstd_second(b):
                pool.wait_ge(s["ln2_var"], b + 1)
                pool.tensor_tensor(rstd2[:], var_eps2[:], minus_half[:], ALU.pow).then_inc(s["ln2_rstd"], 1)

            def base(b):
                for lt in range(LT):
                    t = b * LT + lt
                    pool.wait_ge(s["xn_ready"], t + 1)
                    pool.tensor_tensor(acc[:, t], acc[:, t], xn[b % 2][:, lt], ALU.add).then_inc(s["base_xn"], 1)
                    pool.wait_ge(s["base_xn"], t + 1)
                    pool.tensor_tensor(acc[:, t], acc[:, t], sb2_sb[:, 0], ALU.add).then_inc(s["base_ready"], 1)

            rstd_second(0)
            for b in range(1, B):
                rstd_first(b)
                base(b - 1)
                rstd_second(b)
            base(B - 1)
            pool.wait_ge(s["slots_ready"], 1)
            pool.wait_ge(s["pair_made"], 1)
            pool.wait_ge(s["weights_ready"], TOPK)
            pool.wait_ge(s["id_zero"], 16)
            for k in range(TOPK):
                for t in range(NT):
                    pool.indirect_dma_start(out=pair_dram, out_offset=bass.IndirectOffsetOnAxis(slot[:, k, t:t + 1], 0),
                                            in_=pair[:, k, t, :], in_offset=None).then_inc(s["ids_stored"], 16)
            pool.wait_ge(s["ids_ready"], 1)
            pool.wait_ge(s["xn_even_stored"], 16 * NT // 2)
            pool.wait_ge(s["xn_odd_stored"], 16 * NT // 2)
            pool.wait_ge(s["pad_stored"], 16 * 2)
            pool.wait_ge(s["sh_ready"], SH * FC * B)

            def fetch(j):
                pool.indirect_dma_start(out=xg[:, j % RING], out_offset=None, in_=xn_dram,
                                        in_offset=bass.IndirectOffsetOnAxis(ids[:, j:j + 1], 0)).then_inc(
                                            s[f"xg_{j % RING}"], 16)

            for j in range(RING):
                fetch(j)
            for t in range(NT):
                if t < NT - LT:
                    pool.wait_ge(s["b2_added"], t + 1)
                else:
                    pool.wait_ge(s["so_added"], t + 1)
                pool.dma_start(out[t * P:(t + 1) * P, :], acc[:, t]).then_inc(s["base_stored"], 16)
            pool.wait_ge(s["ids_ready"], 2)
            pool.wait_ge(s["base_stored"], 16 * NT)
            for j in range(NBLK):
                if j + RING < NBLK:
                    pool.wait_ge(s["xgt_ready"], j + 1)
                    fetch(j + RING)
                pool.wait_ge(s["y_ready"], j + 1)
                if j > 0:
                    pool.wait_ge(s["y_even" if j % 2 else "y_odd"], 16 * ((j + 1) // 2))
                pool.indirect_dma_start(out=out, out_offset=bass.IndirectOffsetOnAxis(ids[:, j:j + 1], 0),
                                        in_=y_sb[:, j % 2], in_offset=None, compute_op=ALU.add).then_inc(
                                            s["y_odd" if j % 2 else "y_even"], 16)
            pool.wait_ge(s["y_even"], 16 * ((NBLK + 1) // 2))
            pool.wait_ge(s["y_odd"], 16 * (NBLK // 2))

        @block.scalar
        def _(act):
            s = S
            act.wait_ge(s["loaded_scan"], 16 * 5)
            act.activation(nega[:], nega[:], ACT.Exp).then_inc(s["alog_exp"], 1)
            act.wait_ge(s["alog_exp"], 1)
            act.mul(nega[:], nega[:], -1.0).then_inc(s["nega_made"], 1)
            act.wait_ge(s["loaded_first"], 16 * 3)
            act.preload_act_table(ACT.Silu)

            def last_tap(i):
                act.wait_ge(s["proj_ready"], i + 1)
                since(act, s["u_ready"], i - 3)
                act.activation(conv[:, i % 4], ps[:, PROJ_BANK[i % 4]], ACT.Identity, bias=convb_sb[:, i % EC:i % EC + 1],
                               scale=convw_sb[:, i % EC, DC - 1:DC]).then_inc(s["conv_first"], 1)

            def silu(i):
                b, ec = i // EC, i % EC
                act.wait_ge(s["conv_done"], i + 1)
                act.activation(u[:, ec, b * L:(b + 1) * L], conv[:, i % 4], ACT.Silu).then_inc(s["u_ready"], 1)

            def copy_x_dbl(b):
                act.wait_ge(s["xd_ready"], b + 1)
                act.copy(x_dbl[0:XD, b], ps[0:XD, 2]).then_inc(s["xd_copied"], 1)

            def copy_bc(b):
                act.wait_ge(s["bc_ready"], b + 1)
                act.copy(bc[:, b * LT:(b + 1) * LT].rearrange("p t c -> p (t c)"),
                         ps[:, 3, 0:LT * XD]).then_inc(s["bc_copied"], 1)

            def copy_d_u(t):
                act.wait_ge(s["dsk_ready"], t + 1)
                act.copy(acc[:, t], ps[:, 6 + t % 2]).then_inc(s["dsk_copied"], 1)

            def copies(b, part):
                if part == 1:
                    copy_x_dbl(b)
                    copy_d_u(LT * b)
                if part == 2:
                    copy_d_u(LT * b + 1)
                    copy_bc(b)
                if part == 3:
                    copy_d_u(LT * b + 2)
                    copy_d_u(LT * b + 3)

            last_tap(0)
            for i in range(NT):
                if i + 1 < NT:
                    last_tap(i + 1)
                silu(i)
                if i >= EC:
                    copies(i // EC - 1, i % EC)

            act.preload_act_table_set("natural_log_exp_and_others")

            def exponential(b):
                since(act, s["relu_less"], b - 1)
                for ec in range(EC):
                    v = ps[:, DT_BANK[ec]]
                    act.wait_ge(s["dt_ready"], b * EC + ec + 1)
                    act.activation(e_abs[:, b % 2, ec], v, ACT.Abs, bias=dtb_sb[:, ec:ec + 1]).then_inc(s["abs_made"], 1)
                    act.activation(delta[:, ec, b * L:(b + 1) * L], v, ACT.Relu, bias=dtb_sb[:, ec:ec + 1]).then_inc(s["dt_read"], 1)
                act.wait_ge(s["abs_made"], EC * (b + 1))
                act.activation(e_abs[:, b % 2], e_abs[:, b % 2], ACT.Exp, scale=-1.0).then_inc(s["exp_made"], 1)

            def logarithm(b):
                act.wait_ge(s["lost_made"], b + 1)
                act.activation(one_e[:, b % 2], one_e[:, b % 2], ACT.Ln).then_inc(s["ln_made"], 1)

            def copy_du(b):
                for lt in range(0, LT, 2):
                    t = b * LT + lt
                    act.wait_ge(s["dut_ready"], t + 1)
                    act.copy(du_t[:, t], ps[:, TURN_BANK[lt]]).then_inc(s["dut_copied_a"], 1)

            act.wait_ge(s["pad_stored"], 16 * 2)
            exponential(0)
            for part in range(1, 4):
                copies(B - 1, part)
            exponential(1)
            logarithm(0)
            exponential(2)
            logarithm(1)
            copy_du(0)
            exponential(3)
            logarithm(2)
            copy_du(1)
            logarithm(3)
            copy_du(2)
            copy_du(3)
            act.wait_ge(s["nega_made"], 1)
            act.wait_ge(s["delta_ready"], B)

            def decays(k, half):
                for ec in range(EC):
                    since(act, s["state_ready"], EC * (k - 2) + ec + 1)
                    act.activation(decay[:, half, ec], delta[:, ec, ds((k // DS) * L, L)], ACT.Exp,
                                   scale=nega[:, ec, ds(k % DS, 1)]).then_inc(s["decay_ready"], 1)

            decays(0, 0)
            decays(1, 1)
            with act.Fori(1, STEPS // 2) as kk:
                for half in range(2):
                    decays(2 * kk + half, half)
            def gates(b):
                act.wait_ge(s["ln1_ready"], b + 1)
                since(act, s["gt_ready"], LT * b)
                for ec in range(EC):
                    act.activation(gate[:, ec], xb[b % 2][:, ec], ACT.Silu, bias=shift[:, ec:ec + 1],
                                   scale=rstd[:, ec:ec + 1]).then_inc(s["gate_ready"], 1)

            def turn_normed(b):
                for lt in range(LT):
                    t = b * LT + lt
                    act.wait_ge(s["xnt_ready"], t + 1)
                    act.copy(xn_t[:, :, t * P:(t + 1) * P], ps[:, SIDE_BANK[lt]].rearrange(
                        "p (k n) -> p k n", n=P)).then_inc(s["xnt_copied"], 1)

            def gelu(i):
                q = i % (SH * FC)
                act.wait_ge(s["sh_ready"], i + 1)
                since(act, s["sy_ready"], i - 1)
                act.activation(sg[:, i % 2], ps[:, 2 * (i % 2)], ACT.Gelu,
                               bias=sbg_sb[:, q // FC, q % FC:q % FC + 1]).then_inc(s["sg_ready"], 1)

            def copy_logits(first, last):
                act.wait_ge(s["logits_ready"], LT * last)
                act.copy(aff[:, LT * first:LT * last].rearrange("p t e -> p (t e)"),
                         ps[:, SIDE_BANK[0], LT * first * E:LT * last * E]).then_inc(s["logits_copied"], 1)

            def turn_weights(r):
                act.wait_ge(s["combt_ready"], r + 1)
                if r >= 2:
                    act.wait_ge(s["b2_ready"], LT * (r - 1))
                act.copy(comb_t[0:E, r % 2].rearrange("p t n -> p (t n)"), ps[0:E, SIDE_BANK[r % 2]]).then_inc(s["combt_copied"], 1)

            act.wait_ge(s["mac_done"], LT * STEPS)
            act.wait_ge(s["loaded_shared"], 16 * 7)
            gates(0)
            turn_normed(0)
            gates(1)
            gelu(0)
            gelu(1)
            turn_normed(1)
            gates(2)
            gelu(2)
            gelu(3)
            turn_normed(2)
            gates(3)
            copy_logits(0, B - 1)
            gelu(4)
            gelu(5)
            turn_normed(3)
            gelu(6)
            copy_logits(B - 1, B)
            act.wait_ge(s["logits_copied"], 2)
            act.activation(aff[:], aff[:], ACT.Sigmoid).then_inc(s["aff_ready"], 1)
            for i in range(7, 13):
                gelu(i)
            turn_weights(0)
            turn_weights(1)
            gelu(13)
            turn_weights(2)
            gelu(14)
            turn_weights(3)
            gelu(15)

            def turn_tokens(j, half):
                act.wait_ge(s["xgt_ready"], j + 1)
                since(act, s["h_ready"], j - 1)
                act.copy(xg_t[:, half], ps[:, 4]).then_inc(s["xgt_copied"], 1)

            def hidden_gate(j, half):
                act.wait_ge(s["hb_ready"], j + 1)
                act.activation(hg[:, half], hb[:, half, 0:F], ACT.Gelu).then_inc(s["hg_ready"], 1)

            def turn_hidden(j, half):
                act.wait_ge(s["hyt_ready"], j + 1)
                act.copy(hy_t[:, half], ps[:, 2 + half, 0:F]).then_inc(s["hyt_copied"], 1)

            def block_result(j, half, pair):
                act.wait_ge(s["o_ready"], j + 1)
                if not (isinstance(pair, int) and pair <= 0):
                    wait_apart(act, s["y_odd" if half else "y_even"], 16 * pair)
                act.activation(y_sb[:, half], ps[:, 6 + half], ACT.Copy, scale=row_w[:, ds(j, 1)]).then_inc(s["y_ready"], 1)

            turn_tokens(0, 0)
            turn_tokens(1, 1)
            hidden_gate(0, 0)
            turn_hidden(0, 0)
            turn_tokens(2, 0)
            hidden_gate(1, 1)
            turn_hidden(1, 1)
            block_result(0, 0, 0)
            turn_tokens(3, 1)
            for j in (2, 3):
                hidden_gate(j, j % 2)
                turn_hidden(j, j % 2)
                block_result(j - 1, (j - 1) % 2, (j - 1) // 2)
                turn_tokens(j + 2, j % 2)
            with act.Fori(2, (NBLK - 3) // 2) as jj:
                for half in range(2):
                    j = 2 * jj + half
                    hidden_gate(j, half)
                    turn_hidden(j, half)
                    block_result(j - 1, 1 - half, jj - 1 if half == 0 else jj)
                    turn_tokens(j + 2, half)
            for j in range(NBLK - 3, NBLK):
                hidden_gate(j, j % 2)
                turn_hidden(j, j % 2)
                block_result(j - 1, (j - 1) % 2, (j - 1) // 2)
                if j + 2 < NBLK:
                    turn_tokens(j + 2, j % 2)
            block_result(NBLK - 1, (NBLK - 1) % 2, (NBLK - 1) // 2)

        @block.vector
        def _(dve):
            s = S
            for i in range(NT):
                dve.wait_ge(s["conv_first"], i + 1)
                c, ec = conv[:, i % 4], i % EC
                for back in range(1, DC):
                    if back > 1:
                        dve.wait_ge(s["conv_tap"], (DC - 2) * i + back - 1)
                    dve.scalar_tensor_tensor(
                        out=c[:, back:L], in0=ps[:, PROJ_BANK[i % 4], 0:L - back],
                        scalar=convw_sb[:, ec, DC - 1 - back:DC - back], in1=c[:, back:L],
                        op0=ALU.mult, op1=ALU.add).then_inc(s["conv_done" if back == DC - 1 else "conv_tap"], 1)

            def one_and_lost(b):
                e_b, one_b = e_abs[:, b % 2], one_e[:, b % 2]
                dve.wait_ge(s["exp_made"], b + 1)
                since(dve, s["delta_ready"], b - 1)
                dve.tensor_scalar(one_b, e_b, 1.0, None, ALU.add).then_inc(s["onep_made"], 1)
                dve.wait_ge(s["onep_made"], b + 1)
                dve.scalar_tensor_tensor(out=e_b, in0=one_b, scalar=-1.0, in1=e_b, op0=ALU.add,
                                         op1=ALU.subtract).then_inc(s["lost_made"], 1)

            def add_logarithm(b):
                d = delta[:, :, b * L:(b + 1) * L]
                dve.wait_ge(s["ln_made"], b + 1)
                dve.wait_ge(s["relu_less"], b + 1)
                dve.tensor_tensor(d, one_e[:, b % 2], d, ALU.add).then_inc(s["delta_ready"], 1)

            def first_norm(b):
                dve.wait_ge(s["x_odd" if b % 2 else "x_even"], 16 * (b // 2 + 1))
                for ec in range(EC):
                    dve.bn_stats(stats[:, ec], xb[b % 2][:, ec]).then_inc(s["ln1_stat"], 1)
                dve.wait_ge(s["ln1_stat"], EC * (b + 1))
                for ec in range(EC):
                    dve.bn_aggr(meanvar[:, ec], stats[:, ec]).then_inc(s["ln1_aggr"], 1)
                dve.wait_ge(s["ln1_aggr"], EC * (b + 1))
                since(dve, s["gate_ready"], EC * b)
                dve.tensor_scalar(var_eps[:], meanvar[:, :, 1], EPS, None, ALU.add).then_inc(s["ln1_var"], 1)
                dve.wait_ge(s["ln1_rstd"], b + 1)
                dve.scalar_tensor_tensor(out=shift[:], in0=meanvar[:, :, 0], scalar=-1.0, in1=rstd[:],
                                         op0=ALU.mult, op1=ALU.mult).then_inc(s["ln1_ready"], 1)

            def copy_du(b):
                for lt in range(1, LT, 2):
                    t = b * LT + lt
                    dve.wait_ge(s["dut_ready"], t + 1)
                    dve.tensor_copy(du_t[:, t], ps[:, TURN_BANK[lt]]).then_inc(s["dut_copied_v"], 1)

            one_and_lost(0)
            one_and_lost(1)
            add_logarithm(0)
            one_and_lost(2)
            add_logarithm(1)
            copy_du(0)
            one_and_lost(3)
            add_logarithm(2)
            copy_du(1)
            add_logarithm(3)
            copy_du(2)
            first_norm(0)
            copy_du(3)
            dve.wait_ge(s["bc_copied"], B)
            dve.wait_ge(s["dsk_copied"], NT)

            def scans(k, half):
                since(dve, s["st_ready"], LT * (k - 1))
                for ec in range(EC):
                    dve.wait_ge(s["decay_ready"], EC * k + ec + 1)
                    dve.wait_ge(s["dbu_ready"], EC * k + ec + 1)
                    dve.tensor_tensor_scan(state[:, half, ec], decay[:, half, ec], ps[:, ec], 0.0, ALU.mult,
                                           ALU.add).then_inc(s["state_ready"], 1)

            def sums(k):
                since(dve, s["mac_done"], LT * k)
                for lt in range(LT):
                    t = (k // DS) * LT + lt
                    dve.wait_ge(s["st_ready"], LT * k + lt + 1)
                    dve.scalar_tensor_tensor(
                        out=tile(acc, t), in0=ps[:, 4 + lt], scalar=tile(bc, t)[:, ds(k % DS + DR + DS, 1)],
                        in1=tile(acc, t), op0=ALU.mult, op1=ALU.add).then_inc(s["mac_done"], 1)

            scans(0, 0)
            scans(1, 1)
            sums(0)
            with dve.Fori(1, STEPS // 2) as kk:
                for half in range(2):
                    scans(2 * kk + half, half)
                    sums(2 * kk + half - 1)
            sums(STEPS - 1)
            def gate_and_add(b, tiles):
                for lt in tiles:
                    t = b * LT + lt
                    dve.wait_ge(s["gt_ready"], t + 1)
                    dve.tensor_tensor(acc[:, t], ps[:, SIDE_BANK[lt]], acc[:, t], ALU.mult).then_inc(s["gated"], 1)
                    dve.wait_ge(s["gated"], t + 1)
                    dve.tensor_tensor(acc[:, t], acc[:, t], xb[b % 2][:, lt], ALU.add).then_inc(s["x1_ready"], 1)
                    dve.wait_ge(s["x1_ready"], t + 1)
                    dve.bn_stats(stats2[:, lt], acc[:, t]).then_inc(s["ln2_stat"], 1)
                    dve.wait_ge(s["ln2_stat"], t + 1)
                    dve.bn_aggr(meanvar2[:, lt], stats2[:, lt]).then_inc(s["ln2_aggr"], 1)

            def normed(b):
                dve.wait_ge(s["ln2_aggr"], LT * (b + 1))
                dve.tensor_scalar(var_eps2[:], meanvar2[:, :, 1], EPS, None, ALU.add).then_inc(s["ln2_var"], 1)
                dve.wait_ge(s["ln2_rstd"], b + 1)
                if b >= 2:
                    dve.wait_ge(s["xn_odd_stored" if b % 2 else "xn_even_stored"], 16 * LT * (b // 2))
                    dve.wait_ge(s["xnt_ready"], LT * (b - 1))
                    dve.wait_ge(s["base_xn"], LT * (b - 1))
                for lt in range(LT):
                    dve.tensor_scalar(xn[b % 2][:, lt], acc[:, b * LT + lt], meanvar2[:, lt, 0:1], rstd2[:, lt:lt + 1],
                                      ALU.subtract, ALU.mult).then_inc(s["xn_ready"], 1)

            def hidden_shared(i):
                q = i % (SH * FC)
                dve.wait_ge(s["sg_ready"], i + 1)
                since(dve, s["so_ready"], LT * (i // (SH * FC)))
                dve.scalar_tensor_tensor(out=sy_t[:, q], in0=ps[:, 2 * (i % 2) + 1],
                                         scalar=sb1_sb[:, q // FC, q % FC:q % FC + 1], in1=sg[:, i % 2],
                                         op0=ALU.add, op1=ALU.mult).then_inc(s["sy_ready"], 1)

            def add_shared(b):
                for lt in range(LT):
                    t = b * LT + lt
                    dve.wait_ge(s["so_ready"], t + 1)
                    dve.wait_ge(s["base_ready"], t + 1)
                    dve.tensor_tensor(acc[:, t], ps[:, 6 + lt % 2], acc[:, t], ALU.add).then_inc(s["so_added"], 1)

            def add_biases(b):
                for lt in range(LT):
                    t = b * LT + lt
                    dve.wait_ge(s["b2_ready"], t + 1)
                    dve.tensor_tensor(acc[:, t], ps[:, 6 + lt % 2], acc[:, t], ALU.add).then_inc(s["b2_added"], 1)

            def pick_experts():
                dve.wait_ge(s["consts_made"], 7)
                dve.wait_ge(s["aff_ready"], 1)
                for t in range(NT):
                    dve.max(top[:, t], aff[:, t]).then_inc(s["top_made"], 1)
                dve.wait_ge(s["top_made"], NT)
                for t in range(NT):
                    dve.max_index(topi[:, t], top[:, t], aff[:, t]).then_inc(s["topi_made"], 1)
                dve.wait_ge(s["topi_made"], NT)
                dve.tensor_copy(topf[:], topi[:, :, 0:TOPK]).then_inc(s["topf_made"], 1)
                dve.wait_ge(s["topf_made"], 1)
                every_e = iota_f[:, 0:E].unsqueeze(1).to_broadcast([P, NT, E])
                for k in range(TOPK):
                    dve.tensor_tensor(hot[:, k], every_e, topf[:, :, k:k + 1].to_broadcast([P, NT, E]),
                                      ALU.is_equal).then_inc(s["hot_made"], 1)
                dve.wait_ge(s["hot_made"], TOPK)
                dve.tensor_tensor(member[:], hot[:, 0], hot[:, 1], ALU.add).then_inc(s["member_made"], 1)

            def weigh_pairs():
                dve.tensor_tensor(wsum[:], top[:, :, 0], top[:, :, 1], ALU.add).then_inc(s["wsum_made"], 1)
                dve.wait_ge(s["wsum_made"], 1)
                dve.reciprocal(wsum[:], wsum[:]).then_inc(s["wrec_made"], 1)
                dve.wait_ge(s["wrec_made"], 1)
                dve.tensor_copy(pair[:, :, :, 0], tok_f[:].unsqueeze(1).to_broadcast([P, TOPK, NT])).then_inc(s["pair_made"], 1)
                for k in range(TOPK):
                    dve.tensor_tensor(pair[:, k, :, 1], top[:, :, k], wsum[:], ALU.mult).then_inc(s["weights_ready"], 1)
                dve.wait_ge(s["weights_ready"], TOPK)
                for k in range(TOPK):
                    dve.tensor_tensor(comb_parts[:, k], hot[:, k], pair[:, k, :, 1].unsqueeze(2).to_broadcast([P, NT, E]),
                                      ALU.mult).then_inc(s["comb_part"], 1)
                dve.wait_ge(s["comb_part"], TOPK)
                dve.tensor_tensor(comb[:], comb_parts[:, 0], comb_parts[:, 1], ALU.add).then_inc(s["comb_ready"], 1)

            def place_pairs():
                dve.wait_ge(s["count_ready"], 1)
                dve.tensor_scalar(cnt_blk[:], ps[:, SIDE_BANK[0], 0:E], 1.0 / P, None, ALU.mult).then_inc(s["cnt_made"], 1)
                dve.wait_ge(s["cnt_made"], 1)
                dve.tensor_tensor(full[:], cnt_blk[:].unsqueeze(2).to_broadcast([P, E, E]),
                                  iota_f[:, 0:E].unsqueeze(1).to_broadcast([P, E, E]), ALU.is_gt).then_inc(s["full_made"], 1)
                dve.wait_ge(s["full_made"], 1)
                dve.tensor_reduce(nblk[:], full[:], AX_X, ALU.add).then_inc(s["nblk_made"], 1)
                dve.wait_ge(s["nblk_made"], 1)
                dve.tensor_tensor_scan(blk_end[:], ones[:, 0:E], nblk[:], 0.0, ALU.mult, ALU.add).then_inc(s["end_made"], 1)
                dve.wait_ge(s["end_made"], 1)
                dve.tensor_tensor(slot_base[:], blk_end[:], nblk[:], ALU.subtract).then_inc(s["base_made"], 1)
                dve.wait_ge(s["base_made"], 1)
                dve.wait_ge(s["rank_ready"], 1)
                dve.scalar_tensor_tensor(out=place[:], in0=slot_base[:].unsqueeze(1).to_broadcast([P, NT, E]),
                                         scalar=float(P), in1=ps[:, SIDE_BANK[1], 0:NT * E].rearrange("p (t e) -> p t e", e=E),
                                         op0=ALU.mult, op1=ALU.add).then_inc(s["place_made"], 1)
                dve.wait_ge(s["place_made"], 1)
                for k in range(TOPK):
                    dve.tensor_tensor(picked[:, k], hot[:, k], place[:], ALU.mult).then_inc(s["picked_made"], 1)
                dve.wait_ge(s["picked_made"], TOPK)
                dve.tensor_reduce(slot_f[:], picked[:], AX_X, ALU.add).then_inc(s["slotf_made"], 1)
                dve.wait_ge(s["slotf_made"], 1)
                dve.tensor_copy(slot[:], slot_f[:]).then_inc(s["slots_ready"], 1)
                dve.tensor_tensor(blk_cmp[:], blk_end[:].unsqueeze(1).to_broadcast([P, NBLK, E]),
                                  iota_f[:, 0:NBLK].unsqueeze(2).to_broadcast([P, NBLK, E]), ALU.is_le).then_inc(s["blkc_made"], 1)
                dve.wait_ge(s["blkc_made"], 1)
                dve.tensor_reduce(blk_f[:], blk_cmp[:], AX_X, ALU.add).then_inc(s["blkf_made"], 1)
                dve.wait_ge(s["blkf_made"], 1)
                dve.tensor_scalar(blk_e[:], blk_f[:], float(E - 1), None, ALU.min).then_inc(s["blkm_made"], 1)
                dve.wait_ge(s["blkm_made"], 1)
                dve.memset(blk_new[:, 0:1], 1.0).then_inc(s["new_made"], 1)
                dve.tensor_tensor(blk_new[:, 1:NBLK], blk_e[:, 1:NBLK], blk_e[:, 0:NBLK - 1], ALU.not_equal).then_inc(s["new_made"], 1)
                dve.wait_ge(s["new_made"], 2)
                dve.tensor_copy(blk_load[:], blk_new[:]).then_inc(s["blocks_ready"], 1)
                dve.tensor_tensor_scan(blk_run[:], ones[:, 0:NBLK], blk_new[:], -1.0, ALU.mult, ALU.add).then_inc(s["run_made"], 1)
                dve.wait_ge(s["run_made"], 1)
                rounds = (E - 1) // SLOTS
                turn = iota_f[:, SLOTS:SLOTS * rounds + 1:SLOTS]
                dve.tensor_tensor(blk_cmp[:, :, 0:rounds], blk_run[:].unsqueeze(2).to_broadcast([P, NBLK, rounds]),
                                  turn.unsqueeze(1).to_broadcast([P, NBLK, rounds]), ALU.is_ge).then_inc(s["run_made"], 1)
                dve.wait_ge(s["run_made"], 2)
                dve.tensor_reduce(blk_f[:], blk_cmp[:, :, 0:rounds], AX_X, ALU.add).then_inc(s["run_made"], 1)
                dve.wait_ge(s["run_made"], 3)
                dve.scalar_tensor_tensor(out=blk_slot[:], in0=blk_f[:], scalar=-float(SLOTS), in1=blk_run[:],
                                         op0=ALU.mult, op1=ALU.add).then_inc(s["blocks_ready"], 1)

            every, early, late = range(LT), range(LT // 2), range(LT // 2, LT)
            gate_and_add(0, every)
            normed(0)
            first_norm(1)
            gate_and_add(1, early)
            hidden_shared(0)
            gate_and_add(1, late)
            normed(1)
            hidden_shared(1)
            first_norm(2)
            gate_and_add(2, early)
            hidden_shared(2)
            gate_and_add(2, late)
            normed(2)
            hidden_shared(3)
            add_shared(0)
            first_norm(3)
            gate_and_add(3, early)
            hidden_shared(4)
            gate_and_add(3, late)
            normed(3)
            hidden_shared(5)
            hidden_shared(6)
            hidden_shared(7)
            add_shared(1)
            pick_experts()
            hidden_shared(8)
            hidden_shared(9)
            place_pairs()
            weigh_pairs()
            hidden_shared(10)
            hidden_shared(11)
            add_shared(2)
            hidden_shared(12)
            hidden_shared(13)
            add_biases(0)
            hidden_shared(14)
            add_biases(1)
            hidden_shared(15)
            add_biases(2)
            dve.wait_ge(s["idst_ready"], 1)
            dve.tensor_copy(ids[:], ps[:, SIDE_BANK[0], 0:NBLK]).then_inc(s["ids_ready"], 1)
            dve.tensor_copy(row_w[:], ps[:, SIDE_BANK[0], NBLK:2 * NBLK]).then_inc(s["ids_ready"], 1)
            add_shared(3)
            dve.wait_ge(s["blocks_ready"], 2)
            dve.wait_ge(s["loaded_bias"], 16)

            def hidden(j, half):
                e = dve.value_load(blk_e[0:1, ds(j, 1)], min_val=0, max_val=E - 1)
                dve.wait_ge(s["h_ready"], j + 1)
                dve.tensor_tensor(hb[:, half], ps[:, half], tile(b1_all, e), ALU.add).then_inc(s["hb_ready"], 1)
                since(dve, s["hyt_ready"], j - 1)
                dve.wait_ge(s["hg_ready"], j + 1)
                dve.wait_ge(s["hb_ready"], j + 1)
                dve.tensor_tensor(hy[:, half], hg[:, half], hb[:, half, F:2 * F], ALU.mult).then_inc(s["hy_ready"], 1)

            hidden(0, 0)
            hidden(1, 1)
            with dve.Fori(1, NBLK // 2) as jj:
                for half in range(2):
                    hidden(2 * jj + half, half)
            hidden(NBLK - 1, (NBLK - 1) % 2)

        @block.tensor
        def _(pe):
            s = S
            def project_in(b):
                pe.wait_ge(s[f"ctx_{b}"], 16)
                for ec in range(EC):
                    i = b * EC + ec
                    since(pe, s["conv_done"], i - 3)
                    for mc in range(MC):
                        mm = pe.matmul(ps[:, PROJ_BANK[i % 4]], inp_sb[:, mc, ec * P:(ec + 1) * P],
                                       ctx_sb[:, mc, b * L:(b + 1) * L], start=(mc == 0), stop=(mc == MC - 1))
                    mm.then_inc(s["proj_ready"], 1)

            def project_x(b):
                pe.wait_ge(s["u_ready"], EC * (b + 1))
                since(pe, s["xd_copied"], b)
                for ec in range(EC):
                    mm = pe.matmul(ps[0:XD, 2], xproj_sb[:, ec, :], u[:, ec, b * L:(b + 1) * L],
                                   start=(ec == 0), stop=(ec == EC - 1))
                mm.then_inc(s["xd_ready"], 1)
                for lt in range(LT):
                    t = b * LT + lt
                    since(pe, s["dsk_copied"], t - 1)
                    for ec in range(EC):
                        mm = pe.matmul(ps[:, 6 + t % 2, ec * P:(ec + 1) * P], u[:, ec, t * P:(t + 1) * P], diag_d[:, ec],
                                       start=True, stop=True)
                    mm.then_inc(s["dsk_ready"], 1)
                    if lt == 1:
                        pe.wait_ge(s["xd_copied"], b + 1)
                        since(pe, s["bc_copied"], b)
                        for i in range(LT):
                            mm = pe.transpose(ps[:, 3, i * XD:(i + 1) * XD], x_dbl[0:XD, b, i * P:(i + 1) * P], ident[0:XD, 0:XD])
                        mm.then_inc(s["bc_ready"], 1)

            def project_dt(b):
                pe.wait_ge(s["xd_copied"], b + 1)
                for ec in range(EC):
                    since(pe, s["dt_read"], EC * (b - 1) + ec + 1)
                    pe.matmul(ps[:, DT_BANK[ec]], dtproj_sb[:, ec * P:(ec + 1) * P], x_dbl[0:DR, b],
                              start=True, stop=True).then_inc(s["dt_ready"], 1)

            def turn_du(b):
                pe.wait_ge(s["du_made"], b + 1)
                if b == 0:
                    pe.wait_ge(s["dsk_copied"], NT)
                    pe.wait_ge(s["bc_copied"], B)
                for lt in range(LT):
                    t = b * LT + lt
                    since(pe, s["dut_copied_v" if lt % 2 else "dut_copied_a"], 2 * (b - 1) + lt // 2 + 1)
                    for ec in range(EC):
                        mm = pe.transpose(ps[:, TURN_BANK[lt], ec * P:(ec + 1) * P], u[:, ec, t * P:(t + 1) * P], ident[:])
                    mm.then_inc(s["dut_ready"], 1)

            pe.wait_ge(s["loaded_first"], 16 * 3)
            project_in(0)
            pe.wait_ge(s["loaded_scan"], 16 * 5)
            pe.wait_ge(s["consts_made"], 2)
            pe.wait_ge(s["diag_made"], EC)
            for b in range(1, B):
                project_in(b)
                project_x(b - 1)
            pe.wait_ge(s["conv_done"], NT)
            project_dt(0)
            project_x(B - 1)
            project_dt(1)
            project_dt(2)
            turn_du(0)
            project_dt(3)
            turn_du(1)
            turn_du(2)
            turn_du(3)
            pe.wait_ge(s["dut_copied_a"], NT // 2)
            pe.wait_ge(s["dut_copied_v"], NT // 2)

            def products(k, half):
                pe.wait_ge(s["dbut_ready"], LT * (k + 1))
                for ec in range(EC):
                    since(pe, s["state_ready"], EC * (k - 1) + ec + 1)
                    for lt in range(LT):
                        mm = pe.transpose(ps[:, ec, lt * P:(lt + 1) * P], dbu_t[:, half, lt, ec * P:(ec + 1) * P], ident[:])
                    mm.then_inc(s["dbu_ready"], 1)

            def states(k, half):
                pe.wait_ge(s["state_ready"], EC * (k + 1))
                for lt in range(LT):
                    since(pe, s["mac_done"], LT * (k - 1) + lt + 1)
                    for ec in range(EC):
                        mm = pe.transpose(ps[:, 4 + lt, ec * P:(ec + 1) * P], state[:, half, ec, lt * P:(lt + 1) * P], ident[:])
                    mm.then_inc(s["st_ready"], 1)

            products(0, 0)
            products(1, 1)
            states(0, 0)
            with pe.Fori(1, STEPS // 2) as kk:
                for half in range(2):
                    products(2 * kk + half, half)
                    states(2 * kk + half - 1, 1 - half)
            states(STEPS - 1, 1)
            def turn_gates(b):
                pe.wait_ge(s["gate_ready"], EC * (b + 1))
                since(pe, s["xnt_copied"], LT * b)
                if b == B - 1:
                    pe.wait_ge(s["logits_copied"], 1)
                    pe.wait_ge(s["so_added"], LT)
                for lt in range(LT):
                    for ec in range(EC):
                        mm = pe.transpose(ps[:, SIDE_BANK[lt], ec * P:(ec + 1) * P], gate[:, ec, lt * P:(lt + 1) * P], ident[:])
                    mm.then_inc(s["gt_ready"], 1)

            def turn_normed(b):
                for lt in range(LT):
                    pe.wait_ge(s["xn_ready"], b * LT + lt + 1)
                    for kc in range(KC):
                        mm = pe.transpose(ps[:, SIDE_BANK[lt], kc * P:(kc + 1) * P], xn[b % 2][:, lt, kc * P:(kc + 1) * P], ident[:])
                    mm.then_inc(s["xnt_ready"], 1)

            def logits(b):
                pe.wait_ge(s["xnt_copied"], LT * (b + 1))
                for t in range(b * LT, (b + 1) * LT):
                    for kc in range(KC):
                        mm = pe.matmul(ps[:, SIDE_BANK[0], t * E:(t + 1) * E], xn_t[:, kc, t * P:(t + 1) * P], wa_sb[:, kc, :],
                                       start=(kc == 0), stop=(kc == KC - 1))
                    mm.then_inc(s["logits_ready"], 1)

            def up_shared(i):
                b, q = i // (SH * FC), i % (SH * FC)
                e, fc = q // FC, q % FC
                pe.wait_ge(s["xnt_copied"], LT * (b + 1))
                since(pe, s["sy_ready"], i - 1)
                for part in range(2):
                    col = part * F + fc * P
                    for kc in range(KC):
                        mm = pe.matmul(ps[:, 2 * (i % 2) + part], sup_sb[:, e, kc, col:col + P], xn_t[:, kc, b * L:(b + 1) * L],
                                       start=(kc == 0), stop=(kc == KC - 1))
                mm.then_inc(s["sh_ready"], 1)

            def bias_product(t, first):
                return pe.matmul(ps[:, 6 + t % 2], comb_t[0:E, t // LT % 2, t % LT], rb2_sb[:], start=first, stop=True)

            def down_shared(b):
                pe.wait_ge(s["sy_ready"], SH * FC * (b + 1))
                if b == 0:
                    pe.wait_ge(s["xnt_copied"], LT * (B - 1))
                if b == 1:
                    pe.wait_ge(s["xnt_copied"], LT * B)
                for lt in range(LT):
                    t = b * LT + lt
                    since(pe, s["so_added"], t - 1)
                    if b == B - 1:
                        pe.wait_ge(s["b2_added"], LT * (B - 1))
                    for q in range(SH * FC):
                        mm = pe.matmul(ps[:, 6 + lt % 2], sy_t[:, q, lt * P:(lt + 1) * P], sdown_sb[:, q // FC, q % FC, :],
                                       start=(q == 0), stop=(q == SH * FC - 1 and b < B - 1))
                    if b == B - 1:
                        mm = bias_product(t, False)
                    mm.then_inc(s["so_ready"], 1)

            def turn_weights(r):
                pe.wait_ge(s["comb_ready"], 1)
                pe.wait_ge(s["place_made"], 1)
                since(pe, s["combt_copied"], r - 1)
                for i in range(LT):
                    mm = pe.matmul(ps[0:E, SIDE_BANK[r % 2], i * P:(i + 1) * P], comb[:, LT * r + i], ident[:], start=True, stop=True)
                mm.then_inc(s["combt_ready"], 1)

            def biases(b):
                pe.wait_ge(s["combt_copied"], b + 1)
                pe.wait_ge(s["so_added"], LT * (B - 1))
                for lt in range(LT):
                    t = b * LT + lt
                    since(pe, s["b2_added"], t - 1)
                    bias_product(t, True).then_inc(s["b2_ready"], 1)

            def count_and_rank():
                pe.wait_ge(s["member_made"], 1)
                for t in range(NT):
                    mm = pe.matmul(ps[:, SIDE_BANK[0], 0:E], ones[:], member[:, t], start=(t == 0), stop=(t == NT - 1))
                mm.then_inc(s["count_ready"], 1)
                pe.matmul(ps[:, SIDE_BANK[1], 0:NT * E], before[:], member[:].rearrange("p t e -> p (t e)"), start=True, stop=False)
                for t in range(NT - 1):
                    mm = pe.matmul(ps[:, SIDE_BANK[1], (t + 1) * E:NT * E], ones[:],
                                   member[:, t:t + 1].to_broadcast([P, NT - 1 - t, E]), start=False, stop=(t == NT - 2))
                mm.then_inc(s["rank_ready"], 1)

            pe.wait_ge(s["loaded_shared"], 16 * 7)
            pe.wait_ge(s["mac_done"], LT * STEPS)
            turn_gates(0)
            turn_normed(0)
            up_shared(0)
            turn_gates(1)
            up_shared(1)
            turn_normed(1)
            up_shared(2)
            turn_gates(2)
            up_shared(3)
            turn_normed(2)
            down_shared(0)
            for b in range(B - 1):
                logits(b)
            up_shared(4)
            turn_gates(3)
            up_shared(5)
            turn_normed(3)
            up_shared(6)
            logits(B - 1)
            up_shared(7)
            down_shared(1)
            up_shared(8)
            up_shared(9)
            count_and_rank()
            up_shared(10)
            up_shared(11)
            down_shared(2)
            up_shared(12)
            turn_weights(0)
            turn_weights(1)
            up_shared(13)
            biases(0)
            turn_weights(2)
            up_shared(14)
            biases(1)
            turn_weights(3)
            up_shared(15)
            biases(2)
            pe.wait_ge(s["combt_copied"], B)
            pe.wait_ge(s["ids_loaded"], 16)
            for o in range(2):
                mm = pe.transpose(ps[:, SIDE_BANK[0], o * NBLK:(o + 1) * NBLK], pair_r[:, :, o], ident[0:NBLK, 0:NBLK])
            mm.then_inc(s["idst_ready"], 1)
            down_shared(3)
            pe.wait_ge(s["blocks_ready"], 2)
            pe.wait_ge(s["sy_ready"], SH * FC * B)
            pe.wait_ge(s["ids_ready"], 2)
            pe.wait_ge(s["so_added"], NT)

            def turn_tokens(j, r, round_):
                pe.wait_ge(s[f"xg_{r}"], 16 * (round_ + 1))
                since(pe, s["xgt_copied"], j)
                for kc in range(KC):
                    mm = pe.transpose(ps[:, 4, kc * P:(kc + 1) * P], xg[:, r, kc * P:(kc + 1) * P], ident[:])
                mm.then_inc(s["xgt_ready"], 1)

            def up(j, r, round_):
                slot_j = pe.value_load(blk_slot[0:1, ds(j, 1)], min_val=0, max_val=SLOTS - 1)
                pe.wait_ge(s["xgt_copied"], j + 1)
                pe.wait_ge(s[f"up_{r}"], 16 * (round_ + 1))
                since(pe, s["hb_ready"], j - 1)
                for kc in range(KC):
                    mm = pe.matmul(ps[:, r % 2], xg_t[:, r % 2, kc * P:(kc + 1) * P],
                                   up_w[:, ds(slot_j, 1), kc, :].rearrange("p o f -> p (o f)"),
                                   start=(kc == 0), stop=(kc == KC - 1))
                mm.then_inc(s["h_ready"], 1)

            def turn_hidden(j, r):
                pe.wait_ge(s["hy_ready"], j + 1)
                since(pe, s["hyt_copied"], j - 1)
                for fc in range(FC):
                    mm = pe.transpose(ps[:, 2 + r % 2, fc * P:(fc + 1) * P], hy[:, r % 2, fc * P:(fc + 1) * P], ident[:])
                mm.then_inc(s["hyt_ready"], 1)

            def down(j, r, round_):
                slot_j = pe.value_load(blk_slot[0:1, ds(j, 1)], min_val=0, max_val=SLOTS - 1)
                pe.wait_ge(s["hyt_copied"], j + 1)
                pe.wait_ge(s[f"down_{r}"], 16 * (round_ + 1))
                since(pe, s["y_ready"], j - 1)
                for fc in range(FC):
                    mm = pe.matmul(ps[:, 6 + r % 2], hy_t[:, r % 2, fc * P:(fc + 1) * P],
                                   down_w[:, ds(slot_j, 1), fc, :].rearrange("p o d -> p (o d)"),
                                   start=(fc == 0), stop=(fc == FC - 1))
                mm.then_inc(s["o_ready"], 1)

            def step(j, round_, r):
                up(j + 1, (r + 1) % RING, round_ + (r + 1) // RING)
                turn_hidden(j, r)
                down(j - 1, (r - 1) % RING, round_ + (r - 1) // RING)
                turn_tokens(j + 2, (r + 2) % RING, round_ + (r + 2) // RING)

            turn_tokens(0, 0, 0)
            turn_tokens(1, 1, 0)
            up(0, 0, 0)
            up(1, 1, 0)
            turn_hidden(0, 0)
            turn_tokens(2, 2, 0)
            for j in range(1, RING):
                step(j, 0, j)
            with pe.Fori(1, (NBLK - 2) // RING) as jj:
                for r in range(RING):
                    step(RING * jj + r, jj, r)
            for j in range((NBLK - 2) // RING * RING, NBLK - 2):
                step(j, j // RING, j % RING)
            up(NBLK - 1, (NBLK - 1) % RING, (NBLK - 1) // RING)
            turn_hidden(NBLK - 2, (NBLK - 2) % RING)
            down(NBLK - 3, (NBLK - 3) % RING, (NBLK - 3) // RING)
            turn_hidden(NBLK - 1, (NBLK - 1) % RING)
            down(NBLK - 2, (NBLK - 2) % RING, (NBLK - 2) // RING)
            down(NBLK - 1, (NBLK - 1) % RING, (NBLK - 1) // RING)


def _columns(v, n):
    return v.reshape(n, P).T


def _rows(w, n):
    import numpy as np
    w = w.reshape(*w.shape[:-2], n, P, w.shape[-1])
    return np.swapaxes(w, -3, -2)


def kernel(**inputs):
    import numpy as np
    import concourse.bacc as bacc
    from concourse.bass_utils import run_bass_kernel_spmd

    i = {k.replace("L0_xattn_", "").replace("L0_ffn_", "ffn_"): np.asarray(v) for k, v in inputs.items()}
    laid = {
        "x": i["x"].reshape(B, LT, P, D).transpose(0, 2, 1, 3),
        "ctx_t": _rows(i["ctx_1024"].reshape(T, DM).T, MC),
        "in_proj_t": _rows(i["in_proj_w"].T, MC),
        "conv_w": _rows(i["conv_w"], EC),
        "conv_b": _columns(i["conv_b"], EC),
        "x_proj_t": _rows(i["x_proj_w"].T, EC),
        "dt_proj_t": i["dt_proj_w"].T,
        "dt_b": _columns(i["dt_proj_b"], EC),
        "a_log": _rows(i["A_log"], EC),
        "d_skip": _columns(i["D"], EC),
        "wa": _rows(i["ffn_wa"], KC),
        "r_up": _rows(np.concatenate([i["ffn_rg"], i["ffn_rw1"]], axis=2), KC).reshape(E, P, KC * 2 * F),
        "r_b1": np.concatenate([i["ffn_rgb"], i["ffn_rb1"]], axis=1),
        "r_down": _rows(i["ffn_rw2"], FC).reshape(E, P, FC * D),
        "r_b2": i["ffn_rb2"],
        "s_up": _rows(np.concatenate([i["ffn_sg"], i["ffn_sw1"]], axis=2), KC).transpose(1, 0, 2, 3),
        "s_bg": i["ffn_sgb"].reshape(SH, FC, P).transpose(2, 0, 1),
        "s_b1": i["ffn_sb1"].reshape(SH, FC, P).transpose(2, 0, 1),
        "s_down": _rows(i["ffn_sw2"], FC).transpose(1, 0, 2, 3),
        "s_b2": i["ffn_sb2"],
    }
    nc = bacc.Bacc("TRN2", target_bir_lowering=False, num_devices=1)
    arrays, args = {}, []
    for name, a in laid.items():
        a = np.ascontiguousarray(a)
        arrays[f"in_{name}"] = a
        args.append(nc.dram_tensor(f"in_{name}", a.shape, mybir.dt.from_np(a.dtype), kind="ExternalInput").ap())
    out = nc.dram_tensor("out", [T + P, D], F32, kind="ExternalOutput").ap()
    bass_xattn_scan_moe_kernel(nc, *args, out)
    r = run_bass_kernel_spmd(nc, [arrays], core_ids=[0])
    return r.results[0]["out"][:T].reshape(B, L, D)
```

```python
from contextlib import ExitStack

import concourse.bass as bass
from concourse import mybir

F32 = mybir.dt.float32
F32R = mybir.dt.float32r
I32 = mybir.dt.int32
U32 = mybir.dt.uint32
ALU = mybir.AluOpType
ACT = mybir.ActivationFunctionType
AX_X = mybir.AxisListType.X

P = 128
BANK = 512
B, L, D = 4, 512, 512
DM, DI, DS, DR, DC = 256, 512, 16, 16, 4
E, SH, F, TOPK = 16, 2, 256, 2
T = B * L
NT = T // P
LT = L // P
EC = DI // P
KC = D // P
MC = DM // P
FC = F // P
STEPS = B * DS
NBLK = (T * TOPK + E * (P - 1)) // P
SLOTS = 3
RING = 4
XD = DR + 2 * DS
EPS = 1e-5


def bass_xattn_scan_moe_kernel(nc, x, ctx_t, in_proj_t, conv_w, conv_b, x_proj_t, dt_proj_t, dt_b,
                               a_log, d_skip, wa, r_up, r_b1, r_down, r_b2, s_up, s_bg, s_b1,
                               s_down, s_b2, out):
    xn_dram = nc.dram_tensor("xn_scratch", [T + P, D], F32, kind="Internal").ap()
    pair_dram = nc.dram_tensor("pair_of_slot", [NBLK * P, 2], F32, kind="Internal").ap()

    with ExitStack() as ctx:
        def sb(name, shape, dt=F32):
            return ctx.enter_context(nc.sbuf_tensor(name, shape, dt))

        def sem(name):
            return ctx.enter_context(nc.semaphore(name))

        ps = ctx.enter_context(nc.psum_tensor("ps", [P, 8, BANK], F32))

        r0 = sb("r0", [P, 10240])
        with ExitStack() as first:
            mem = first.enter_context(nc.sbuf_tensor("mem", [P, 3 * EC * T], F32))
            acc = first.enter_context(nc.sbuf_tensor("acc", [P, NT, DI], F32))
        split = sb("split", [P, 3 * EC * T])
        split_acc = sb("split_acc", [P, NT * DI])
        ru, rd, rt = (mem[:, i * EC * T:(i + 1) * EC * T] for i in range(3))
        split_u, split_d, split_t = (split[:, i * EC * T:(i + 1) * EC * T] for i in range(3))

        def view(region, start, *shape):
            n = 1
            for s in shape:
                n *= s
            v = region[:, start:start + n]
            if len(shape) == 2:
                v = v.rearrange("p (a b) -> p a b", b=shape[1])
            if len(shape) == 3:
                v = v.rearrange("p (a b c) -> p a b c", b=shape[1], c=shape[2])
            return v

        ctx_sb = view(rt, 0, MC, T)
        inp_sb = view(rt, MC * T, MC, DI)
        u = view(ru, 0, B, EC * L).rearrange("p b (e l) -> p b e l", l=L)
        delta = view(rd, 0, EC, T)
        du_t = view(rt, 0, NT, DI)
        x_dbl = view(rt, 3 * T, B, L)
        d_u = view(r0, 4096, 2, EC, L)
        no_rows = view(rd, 7680, D)
        conv = view(r0, 8192, 4, L)
        e_abs = view(r0, 0, 2, EC, L)
        one_e = view(r0, 4096, 2, EC, L)
        PROJ_BANK = DT_BANK = (0, 1, 4, 5)
        TURN_BANK = (6, 7, 2, 3)
        decay = view(r0, 0, 2, EC, L)
        state = view(r0, 4096, 2, EC, L)
        dbu_t = view(ru, 0, 2, LT, DI)
        SIDE, LAST = LT - 2, LT - 1
        SUMS = (LT - 1) + (LT - 2)
        PRODS = 1 + 2
        PAIRS = STEPS // 2
        BPAIRS = DS // 2
        xb = (view(r0, 8192, LT, D), view(r0, 0, LT, D))
        xn = (view(r0, 6144, LT, D), view(r0, 2048, LT, D))
        gate = view(r0, 4096, EC, L)
        SIDE_BANK = (4, 5, 6, 7)
        x_head, x_rest = (tuple(view(split_d, (2 * i + part) * KC * L, KC, L) for i in range(2)) for part in range(2))
        sup_raw = view(ru, SH * KC * 2 * F, SH, KC * 2 * F).rearrange("p s (k f) -> p s k f", k=KC)
        sup_head, sup_rest = (view(split_u, part * SH * KC * 2 * F, SH, KC * 2 * F).rearrange("p s (k f) -> p s k f", k=KC)
                              for part in range(2))
        sdown_raw = view(rt, SH * FC * D, SH, FC * D).rearrange("p s (c d) -> p s c d", c=FC)
        sdown_head, sdown_rest = (view(split_t, part * SH * FC * D, SH, FC * D).rearrange("p s (c d) -> p s c d", c=FC)
                                  for part in range(2))
        sy_raw = view(rt, 2 * SH * FC * D + SH * FC * L, SH * FC, L)
        sy_head, sy_rest = (view(split_t, 2 * SH * FC * D + part * SH * FC * L, SH * FC, L) for part in range(2))

        def one_pass(ap):
            return ap.bitcast(F32R)

        UP = KC * 2 * F
        up_w = view(r0, 0, SLOTS, UP)
        b1_w = view(r0, SLOTS * UP, SLOTS, 2 * F)
        xg = view(r0, 10240 - RING * D, RING, D)
        B2_AT = EC * T - E // 2 * D
        UPS_AT = B2_AT + E * D
        LATE_AT = UPS_AT + 2 * 2 * UP
        down_w = view(mem, 0, SLOTS, FC * D).rearrange("p s (c d) -> p s c d", c=FC)
        hb = view(mem, SLOTS * FC * D, 2, 2 * F)
        b2_all = view(mem, B2_AT, E, D)
        up_head, up_rest = (view(split, UPS_AT, 2, 2, UP)[:, :, part] for part in range(2))
        up_part = (slice(0, 3 * UP // 8), slice(3 * UP // 8, UP))
        xg_head, xg_rest = (view(split, LATE_AT + part * 2 * D, 2, D) for part in range(2))
        hy_head, hy_rest = (view(split, LATE_AT + 4 * D + part * 2 * F, 2, F) for part in range(2))
        hg = view(mem, LATE_AT + 4 * D + 4 * F, 2, F)
        hy = view(mem, LATE_AT + 4 * D + 6 * F, 2, F)
        dw_head, dw_rest = (view(split_acc, part * RING * FC * D, RING, FC * D) for part in range(2))

        ident = sb("ident", [P, P])
        before = sb("before", [P, P])
        ones = sb("ones", [P, P])
        xproj_sb = sb("xproj_sb", [P, EC, XD])
        dtproj_sb = sb("dtproj_sb", [DR, DI])
        convw_sb = sb("convw_sb", [P, EC, DC])
        convb_sb = sb("convb_sb", [P, EC])
        dtb_sb = sb("dtb_sb", [P, EC])
        dskip_sb = sb("dskip_sb", [P, EC])
        nega = sb("nega", [P, EC, DS])
        bc = sb("bc", [P, NT, XD])
        bcol = sb("bcol", [P, LT - 1, 2])
        wa_raw = sb("wa_raw", [P, KC, E])
        wa_rest = sb("wa_rest", [P, KC, E])
        wa_head = sb("wa_head", [P, KC, E])
        sbg_sb = sb("sbg_sb", [P, SH, FC])
        sb1_sb = sb("sb1_sb", [P, SH, FC])
        sb2_sb = sb("sb2_sb", [P, SH, D])
        stats = sb("stats", [P, 4, 6])
        meanvar = sb("meanvar", [P, 4, 2])
        rstd = sb("rstd", [P, 4])
        shift = sb("shift", [P, 4])
        var_eps = sb("var_eps", [P, 4])
        stats2 = sb("stats2", [P, 4, 6])
        meanvar2 = sb("meanvar2", [P, 4, 2])
        var_eps2 = sb("var_eps2", [P, 4])
        rstd2 = sb("rstd2", [P, 4])
        minus_half = sb("minus_half", [P, 4])
        sg = sb("sg", [P, 2, L])
        aff = sb("aff", [P, NT, E])
        top = sb("top", [P, NT, 8])
        topi = sb("topi", [P, NT, 8], U32)
        topf = sb("topf", [P, NT, TOPK])
        cnt_blk = sb("cnt_blk", [P, E])
        wsum = sb("wsum", [P, NT])
        pair = sb("pair", [P, TOPK, NT, 2])
        pad_i = sb("pad_i", [NBLK, P], I32)
        iota_i = sb("iota_i", [P, 48], I32)
        iota_f = sb("iota_f", [P, 48])
        tok_i = sb("tok_i", [P, NT], I32)
        tok_f = sb("tok_f", [P, NT])
        hot = sb("hot", [P, TOPK, NT, E])
        member = sb("member", [P, NT, E])
        full = sb("full", [P, E, E])
        nblk = sb("nblk", [P, E])
        blk_end = sb("blk_end", [P, E])
        slot_base = sb("slot_base", [P, E])
        place = sb("place", [P, NT, E])
        picked = sb("picked", [P, TOPK, NT, E])
        y_sb = sg
        yb = sb2_sb
        prod = (sg[:, 0], hot[:].rearrange("p k t e -> p (k t e)"), sg[:, 1])
        side = picked[:].rearrange("p k t e -> p (k t e)")
        scores = (prod[1][0:E], side[0:E])
        slot_f = sb("slot_f", [P, TOPK, NT])
        slot = sb("slot", [P, TOPK, NT], U32)
        blk_cmp = sb("blk_cmp", [P, NBLK, E])
        blk_f = sb("blk_f", [P, NBLK])
        blk_e = sb("blk_e", [P, NBLK], I32)
        blk_new = sb("blk_new", [P, NBLK])
        blk_run = sb("blk_run", [P, NBLK])
        blk_load = sb("blk_load", [P, NBLK], I32)
        blk_slot = sb("blk_slot", [P, NBLK], I32)
        pair_r = sb("pair_r", [NBLK, P, 2])
        ids = sb("ids", [P, NBLK], U32)
        row_w = sb("row_w", [P, NBLK])

        names = """
        waits_passed loaded_first loaded_scan loaded_b2 loaded_shared loaded_sdown id_zero
        ctx_0 ctx_1 ctx_2 ctx_3
        consts_zeroed consts_made dskip_made nega_made
        proj_ready conv_first conv_tap conv_done u_ready
        xd_ready xd_copied bc_ready bc_copied dt_ready relu_made abs_made exp_made onep_made lost_made
        ln_made relu_less delta_ready du_made du_last dut_ready dut_copied_a dut_copied_v dsk_ready dsk_copied
        decay_zeroed decay_ready bcol_ready dbut_ready dbut_made_a dbu_ready state_ready st_ready mac_done prod_made prod_added side_added
        x_even x_odd ln1_stat ln1_aggr ln1_var ln1_rstd ln1_ready gate_ready gt_ready gated x1_ready
        ln2_stat ln2_aggr ln2_var ln2_rstd xn_ready xnt_ready xnt_copied base_xn base_ready logits_ready
        xn_even_stored xn_odd_stored b2s_made
        aff_ready top_made topi_made topf_made hot_made member_made rank_ready count_ready
        cnt_made full_made nblk_made base_made place_made picked_made slotf_made slots_ready
        wsum_made weights_ready 
        blkc_made blkm_made new_made run_made blocks_ready pair_made ids_stored ids_loaded idst_ready ids_ready
        base_stored pad_stored
        sh_ready sg_ready sy_ready syh_made syr_made suph_made supr_made sdh_made sdr_made wah_made war_made xr_made scores_ready scores_copied logits_copied so_ready so_added
        up_0 up_1 up_2 up_3 down_0 down_1 down_2 down_3 xg_0 xg_1 xg_2 xg_3 xgt_ready xgt_copied h_ready
        hb_ready hg_ready hy_ready hyt_ready hyt_copied hyr_made xgr_made uph_made upr_made_v upr_made_p dwh_made dwr_made o_ready yb_ready y_ready y_even y_odd
        """.split()
        S = {n: sem(n) for n in names}

        def tile(tensor, t):
            return tensor[:, bass.ds(t, 1)].rearrange("p o n -> p (o n)")

        def since(eng, semaphore, count):
            if not (isinstance(count, int) and count <= 0):
                eng.wait_ge(semaphore, count)

        def wait_apart(eng, semaphore, count):
            eng.wait_ge(semaphore, count)
            eng.sem_inc(S["waits_passed"], 1)

        def up_raw(slot_j, which):
            return up_w[:, bass.ds(slot_j, 1), up_part[which]].rearrange("p o n -> p (o n)")

        block = ctx.enter_context(nc.Block())
        ds = bass.ds

        @block.sync
        def _(sp):
            s = S
            sp.dma_start(inp_sb, in_proj_t).then_inc(s["loaded_first"], 16)
            sp.dma_start(convw_sb[:], conv_w).then_inc(s["loaded_first"], 16)
            sp.dma_start(convb_sb[:], conv_b).then_inc(s["loaded_first"], 16)
            for b in range(B):
                sp.dma_start(ctx_sb[:, :, b * L:(b + 1) * L], ctx_t[:, :, b * L:(b + 1) * L]).then_inc(s[f"ctx_{b}"], 16)
            sp.dma_start(xproj_sb[:], x_proj_t).then_inc(s["loaded_scan"], 16)
            sp.dma_start(dtproj_sb[:], dt_proj_t).then_inc(s["loaded_scan"], 16)
            sp.dma_start(dtb_sb[:], dt_b).then_inc(s["loaded_scan"], 16)
            sp.dma_start(dskip_sb[:], d_skip).then_inc(s["loaded_scan"], 16)
            sp.dma_start(nega[:], a_log).then_inc(s["loaded_scan"], 16)
            sp.dma_start(wa_raw[:], wa).then_inc(s["loaded_shared"], 16)
            sp.dma_start(sbg_sb[:], s_bg).then_inc(s["loaded_shared"], 16)
            sp.dma_start(sb1_sb[:], s_b1).then_inc(s["loaded_shared"], 16)
            sp.dma_start(sb2_sb[:], s_b2.unsqueeze(0).to_broadcast([P, SH, D])).then_inc(s["loaded_shared"], 16)
            sp.wait_ge(s["u_ready"], NT)
            sp.dma_start(xb[0], x[0]).then_inc(s["x_even"], 16)
            sp.wait_ge(s["dut_ready"], NT)
            sp.dma_start(sup_raw, s_up).then_inc(s["loaded_shared"], 16)
            sp.wait_ge(s["mac_done"], SUMS * PAIRS)
            sp.dma_start(xb[1], x[1]).then_inc(s["x_odd"], 16)
            sp.dma_start(sdown_raw, s_down).then_inc(s["loaded_sdown"], 16)
            for b in range(B):
                if b + 2 < B:
                    sp.wait_ge(s["x1_ready"], (b + 1) * LT)
                    sp.wait_ge(s["gate_ready"], (b + 1) * EC)
                    sp.dma_start(xb[b % 2], x[b + 2]).then_inc(s["x_odd" if b % 2 else "x_even"], 16)
                for lt in range(LT):
                    t = b * LT + lt
                    sp.wait_ge(s["xn_ready"], t + 1)
                    sp.dma_start(xn_dram[t * P:(t + 1) * P, :], xn[b % 2][:, lt, :]).then_inc(s["xn_odd_stored" if b % 2 else "xn_even_stored"], 16)
            sp.wait_ge(s["blocks_ready"], 2)
            sp.wait_ge(s["base_ready"], NT)
            sp.wait_ge(s["xnt_ready"], NT)
            sp.wait_ge(s["xn_even_stored"], 16 * NT // 2)
            sp.wait_ge(s["xn_odd_stored"], 16 * NT // 2)

            def load(weights, r_weights, loaded, j, r):
                e = sp.value_load(blk_e[0:1, ds(j, 1)], min_val=0, max_val=E - 1)
                new = sp.value_load(blk_load[0:1, ds(j, 1)], min_val=0, max_val=1)
                slot_j = sp.value_load(blk_slot[0:1, ds(j, 1)], min_val=0, max_val=SLOTS - 1)
                sp.dma_start(weights[:, ds(slot_j, 1)], r_weights[ds(e, 1)].rearrange("e p n -> p e n"), cond=new).then_inc(s[f"{loaded}_{r}"], 16)
                if loaded == "down":
                    sp.dma_start(b1_w[:, ds(slot_j, 1)], r_b1[ds(e, 1)].unsqueeze(0).to_broadcast([P, 1, 2 * F]),
                                 cond=new).then_inc(s[f"down_{r}"], 16)

            def load_up(j, r):
                if not isinstance(j, int) or j >= SLOTS:
                    wait_apart(sp, s["upr_made_v"], j - SLOTS + 1)
                    wait_apart(sp, s["upr_made_p"], j - SLOTS + 1)
                load(up_w, r_up, "up", j, r)

            def load_down(j, r):
                if not isinstance(j, int) or j >= SLOTS:
                    wait_apart(sp, s["dwr_made"], j - SLOTS + 1)
                    wait_apart(sp, s["hb_ready"], j - SLOTS + 1)
                load(down_w, r_down, "down", j, r)

            for j in range(SLOTS):
                load_up(j, j)
            sp.wait_ge(s["sh_ready"], SH * FC * (B - 1))
            sp.dma_start(b2_all[:, E // 2:E], r_b2[E // 2:E].unsqueeze(0).to_broadcast([P, E // 2, D])).then_inc(s["loaded_b2"], 16)
            sp.wait_ge(s["ids_stored"], 16 * TOPK * NT)
            sp.dma_start(pair_r[:].rearrange("j p o -> j (p o)"),
                         pair_dram.rearrange("(j p) o -> j (p o)", p=P)).then_inc(s["ids_loaded"], 16)
            sp.wait_ge(s["sh_ready"], SH * FC * B)
            for j in range(SLOTS):
                load_down(j, j)
            sp.wait_ge(s["base_stored"], 16 * NT)
            sp.dma_start(b2_all[:, 0:E // 2], r_b2[0:E // 2].unsqueeze(0).to_broadcast([P, E // 2, D])).then_inc(s["loaded_b2"], 16)
            for j in range(1, RING):
                if j >= SLOTS:
                    load_down(j, j)
                load_up(j + 2, (j + 2) % RING)
            with sp.Fori(1, (NBLK - 2) // RING) as jj:
                for r in range(RING):
                    load_down(RING * jj + r, r)
                    load_up(RING * jj + r + 2, (r + 2) % RING)
            for j in range((NBLK - 2) // RING * RING, NBLK):
                load_down(j, j % RING)
                if j + 2 < NBLK:
                    load_up(j + 2, (j + 2) % RING)

        @block.gpsimd
        def _(pool):
            s = S
            pool.memset(ident[:], 0.0).then_inc(s["consts_zeroed"], 1)
            pool.memset(ones[:], 1.0).then_inc(s["consts_zeroed"], 1)
            pool.memset(pair_r[:], 0.0).then_inc(s["consts_zeroed"], 1)
            pool.memset(no_rows, 0.0).then_inc(s["consts_zeroed"], 1)
            pool.iota(pad_i[:], [[1, P]], base=T, channel_multiplier=0).then_inc(s["consts_zeroed"], 1)
            pool.memset(minus_half[:], -0.5).then_inc(s["consts_zeroed"], 1)
            pool.wait_ge(s["consts_zeroed"], 6)
            pool.affine_select(out=ident[:], in_=ident[:], compare_op=ALU.not_equal, fill=1.0, base=0,
                               pattern=[[-1, P]], channel_multiplier=1).then_inc(s["consts_made"], 1)
            pool.affine_select(out=one_pass(before[:]), in_=ones[:], compare_op=ALU.is_gt, fill=0.0, base=0,
                               pattern=[[1, P]], channel_multiplier=-1).then_inc(s["consts_made"], 1)
            pool.iota(iota_i[:], [[1, 48]], base=0, channel_multiplier=0).then_inc(s["consts_made"], 1)
            pool.iota(tok_i[:], [[P, NT]], base=0, channel_multiplier=1).then_inc(s["consts_made"], 1)
            pool.tensor_copy(pair_r[:, :, 0], pad_i[:]).then_inc(s["consts_made"], 1)
            pool.wait_ge(s["consts_made"], 5)
            pool.dma_start(xn_dram[T:T + P, :], no_rows).then_inc(s["pad_stored"], 16)
            pool.dma_start(out[T:T + P, :], no_rows).then_inc(s["pad_stored"], 16)
            pool.dma_start(pair_dram.rearrange("(j p) o -> j (p o)", p=P),
                           pair_r[:].rearrange("j p o -> j (p o)")).then_inc(s["id_zero"], 16)
            pool.tensor_copy(iota_f[:], iota_i[:]).then_inc(s["consts_made"], 1)
            pool.tensor_copy(tok_f[:], tok_i[:]).then_inc(s["consts_made"], 1)
            pool.wait_ge(s["loaded_scan"], 16 * 5)
            for b in range(B):
                pool.wait_ge(s["u_ready"], EC * (b + 1))
                since(pool, s["dsk_ready"], LT * (b - 1))
                for ec in range(EC):
                    pool.tensor_scalar(d_u[:, b % 2, ec], u[:, b, ec], dskip_sb[:, ec:ec + 1], 1.0,
                                       ALU.mult, ALU.mult).then_inc(s["dskip_made"], 1)

            def less_lost(b):
                pool.wait_ge(s["lost_made"], b + 1)
                pool.wait_ge(s["relu_made"], EC * (b + 1))
                d = delta[:, :, b * L:(b + 1) * L]
                pool.tensor_tensor(d, d, e_abs[:, b % 2], ALU.subtract).then_inc(s["relu_less"], 1)

            def delta_u(b):
                pool.wait_ge(s["delta_ready"], b + 1)
                pool.wait_ge(s["xd_ready"], b + 1)
                pool.wait_ge(s["dskip_made"], EC * (b + 1))
                pool.tensor_tensor(u[:, b], delta[:, :, b * L:(b + 1) * L], u[:, b], ALU.mult).then_inc(s["du_made"], 1)

            def rstd_first(b):
                pool.wait_ge(s["ln1_var"], b + 1)
                since(pool, s["gate_ready"], EC * b)
                pool.tensor_tensor(rstd[:], var_eps[:], minus_half[:], ALU.pow).then_inc(s["ln1_rstd"], 1)

            less_lost(0)
            rstd_first(0)
            less_lost(1)
            delta_u(0)
            less_lost(2)
            less_lost(3)
            delta_u(1)
            pool.wait_ge(s["dut_copied_a"], NT // 4)
            pool.wait_ge(s["dut_copied_v"], NT // 4)
            pool.wait_ge(s["bc_copied"], B)

            def columns(b, step_pair):
                q = b * BPAIRS + step_pair
                since(pool, s["dbut_ready"], LAST * 2 * q)
                pool.tensor_copy(bcol[:], bc[:, b * LT:b * LT + LAST, ds(2 * step_pair + DR, 2)]).then_inc(s["bcol_ready"], 1)

            def turned_products(b, n, half, step_pair):
                k = b * DS + n
                if half == 0:
                    wait_apart(pool, s["bcol_ready"], b * BPAIRS + step_pair + 1)
                if not (isinstance(k, int) and k < 2):
                    wait_apart(pool, s["dbu_ready"], EC * (k - 1))
                for lt in range(LAST):
                    pool.tensor_scalar(dbu_t[:, half, lt], du_t[:, b * LT + lt], bcol[:, lt, half:half + 1],
                                       1.0, ALU.mult, ALU.mult).then_inc(s["dbut_ready"], 1)

            def add_even(b, step_pair):
                q = b * BPAIRS + step_pair
                wait_apart(pool, s["prod_made"], PRODS * q + 1)
                since(pool, s["prod_added"], PRODS * q)
                pool.tensor_tensor(acc[:, b * LT + LAST], acc[:, b * LT + LAST], prod[0], ALU.add).then_inc(s["prod_added"], 1)

            def add_odd(b, step_pair):
                q = b * BPAIRS + step_pair
                wait_apart(pool, s["prod_made"], PRODS * q + 2)
                if isinstance(step_pair, int) and step_pair == 0:
                    since(pool, s["side_added"], b)
                    pool.tensor_copy(side, prod[1]).then_inc(s["prod_added"], 1)
                else:
                    since(pool, s["prod_added"], PRODS * (q - 1) + 2)
                    pool.tensor_tensor(side, side, prod[1], ALU.add).then_inc(s["prod_added"], 1)
                wait_apart(pool, s["prod_made"], PRODS * q + 3)
                since(pool, s["prod_added"], PRODS * q + 1)
                pool.tensor_tensor(acc[:, b * LT + LAST], acc[:, b * LT + LAST], prod[2], ALU.add).then_inc(s["prod_added"], 1)

            def add_side(b):
                pool.wait_ge(s["mac_done"], SUMS * (b + 1) * BPAIRS)
                pool.wait_ge(s["prod_added"], PRODS * (b + 1) * BPAIRS)
                pool.tensor_tensor(acc[:, b * LT + SIDE], acc[:, b * LT + SIDE], side, ALU.add).then_inc(s["side_added"], 1)

            columns(0, 0)
            for b in range(B):
                if b == 1:
                    pool.wait_ge(s["dut_copied_a"], NT // 2)
                    pool.wait_ge(s["dut_copied_v"], NT // 2)
                for step_pair in range(3):
                    turned_products(b, 2 * step_pair, 0, step_pair)
                    if step_pair >= 2:
                        add_odd(b, step_pair - 2)
                    elif b >= 1:
                        add_odd(b - 1, BPAIRS + step_pair - 2)
                    turned_products(b, 2 * step_pair + 1, 1, step_pair)
                    columns(b, step_pair + 1)
                    if step_pair >= 1:
                        add_even(b, step_pair - 1)
                    elif b >= 1:
                        add_even(b - 1, BPAIRS - 1)
                    if step_pair == 1 and b >= 1:
                        add_side(b - 1)
                with pool.Fori(3, BPAIRS - 1) as step_pair:
                    turned_products(b, 2 * step_pair, 0, step_pair)
                    add_odd(b, step_pair - 2)
                    turned_products(b, 2 * step_pair + 1, 1, step_pair)
                    columns(b, step_pair + 1)
                    add_even(b, step_pair - 1)
                turned_products(b, DS - 2, 0, BPAIRS - 1)
                add_odd(b, BPAIRS - 3)
                turned_products(b, DS - 1, 1, BPAIRS - 1)
                if b + 1 < B:
                    columns(b + 1, 0)
                add_even(b, BPAIRS - 2)
            add_odd(B - 1, BPAIRS - 2)
            add_even(B - 1, BPAIRS - 1)
            add_odd(B - 1, BPAIRS - 1)
            add_side(B - 1)
            pool.wait_ge(s["loaded_shared"], 16 * 5)
            pool.tensor_tensor(sb2_sb[:, 0], sb2_sb[:, 0], sb2_sb[:, 1], ALU.add).then_inc(s["b2s_made"], 1)
            pool.wait_ge(s["b2s_made"], 1)

            def rstd_second(b):
                pool.wait_ge(s["ln2_var"], b + 1)
                pool.tensor_tensor(rstd2[:], var_eps2[:], minus_half[:], ALU.pow).then_inc(s["ln2_rstd"], 1)

            def base(b):
                for lt in range(LT):
                    t = b * LT + lt
                    pool.wait_ge(s["xn_ready"], t + 1)
                    pool.tensor_tensor(acc[:, t], acc[:, t], xn[b % 2][:, lt], ALU.add).then_inc(s["base_xn"], 1)
                    pool.wait_ge(s["base_xn"], t + 1)
                    pool.tensor_tensor(acc[:, t], acc[:, t], sb2_sb[:, 0], ALU.add).then_inc(s["base_ready"], 1)

            def rest(to, value, head, made):
                pool.tensor_tensor(one_pass(to), value, head, ALU.subtract).then_inc(s[made], 1)

            pool.wait_ge(s["wah_made"], 1)
            rest(wa_rest[:], wa_raw[:], wa_head[:], "war_made")
            for e in range(SH):
                pool.wait_ge(s["suph_made"], e + 1)
                rest(sup_rest[:, e], sup_raw[:, e], sup_head[:, e], "supr_made")
                if e == 0:
                    rstd_second(0)
            rstd_first(1)
            base(0)
            rstd_second(1)
            pool.wait_ge(s["sdh_made"], 1)
            rest(sdown_rest, sdown_raw, sdown_head, "sdr_made")
            rstd_first(2)
            base(1)
            rstd_first(3)
            rstd_second(2)
            base(2)
            rstd_second(3)
            base(3)
            pool.wait_ge(s["slots_ready"], 1)
            pool.wait_ge(s["pair_made"], 1)
            pool.wait_ge(s["weights_ready"], TOPK)
            pool.wait_ge(s["id_zero"], 16)
            for k in range(TOPK):
                for t in range(NT):
                    pool.indirect_dma_start(out=pair_dram, out_offset=bass.IndirectOffsetOnAxis(slot[:, k, t:t + 1], 0),
                                            in_=pair[:, k, t, :], in_offset=None).then_inc(s["ids_stored"], 16)
            def store_base(t):
                pool.wait_ge(s["so_added"], t + 1)
                pool.dma_start(out[t * P:(t + 1) * P, :], acc[:, t]).then_inc(s["base_stored"], 16)

            for t in range(NT - LT):
                store_base(t)
            pool.wait_ge(s["ids_ready"], 1)
            pool.wait_ge(s["xn_even_stored"], 16 * NT // 2)
            pool.wait_ge(s["xn_odd_stored"], 16 * NT // 2)
            pool.wait_ge(s["pad_stored"], 16 * 2)

            def fetch(j):
                pool.indirect_dma_start(out=xg[:, j % RING], out_offset=None, in_=xn_dram,
                                        in_offset=bass.IndirectOffsetOnAxis(ids[:, j:j + 1], 0)).then_inc(
                                            s[f"xg_{j % RING}"], 16)

            def rest_of_up(j):
                slot_j = pool.value_load(blk_slot[0:1, j:j + 1], min_val=0, max_val=SLOTS - 1)
                pool.wait_ge(s["uph_made"], 2 * j + 2)
                pool.tensor_tensor(one_pass(up_rest[:, j % 2, up_part[1]]), up_raw(slot_j, 1), up_head[:, j % 2, up_part[1]],
                                   ALU.subtract).then_inc(s["upr_made_p"], 1)

            for j in range(RING):
                fetch(j)
            rest_of_up(0)
            for t in range(NT - LT, NT):
                store_base(t)
            pool.wait_ge(s["ids_ready"], 2)
            pool.wait_ge(s["base_stored"], 16 * NT)
            BEHIND = 4
            for i in range(NBLK + BEHIND):
                if 0 < i < NBLK:
                    rest_of_up(i)
                if i + RING < NBLK:
                    pool.wait_ge(s["xgt_ready"], i + 1)
                    fetch(i + RING)
                j = i - BEHIND
                if j < 0:
                    continue
                pool.wait_ge(s["y_ready"], j + 1)
                if j > 0:
                    pool.wait_ge(s["y_even" if j % 2 else "y_odd"], 16 * ((j + 1) // 2))
                pool.indirect_dma_start(out=out, out_offset=bass.IndirectOffsetOnAxis(ids[:, j:j + 1], 0),
                                        in_=y_sb[:, j % 2], in_offset=None, compute_op=ALU.add).then_inc(
                                            s["y_odd" if j % 2 else "y_even"], 16)
            pool.wait_ge(s["y_even"], 16 * ((NBLK + 1) // 2))
            pool.wait_ge(s["y_odd"], 16 * (NBLK // 2))

        @block.scalar
        def _(act):
            s = S
            act.wait_ge(s["loaded_scan"], 16 * 5)
            act.activation(nega[:], nega[:], ACT.Exp).then_inc(s["nega_made"], 1)
            act.wait_ge(s["nega_made"], 1)
            act.mul(nega[:], nega[:], -1.0).then_inc(s["nega_made"], 1)
            act.wait_ge(s["loaded_first"], 16 * 3)
            act.preload_act_table(ACT.Silu)

            def last_tap(i):
                act.wait_ge(s["proj_ready"], i + 1)
                since(act, s["u_ready"], i - 3)
                act.activation(conv[:, i % 4], ps[:, PROJ_BANK[i % 4]], ACT.Identity, bias=convb_sb[:, i % EC:i % EC + 1],
                               scale=convw_sb[:, i % EC, DC - 1:DC]).then_inc(s["conv_first"], 1)

            def silu(i):
                b, ec = i // EC, i % EC
                act.wait_ge(s["conv_done"], i + 1)
                act.activation(u[:, b, ec], conv[:, i % 4], ACT.Silu).then_inc(s["u_ready"], 1)

            def copy_x_dbl(b):
                act.wait_ge(s["xd_ready"], b + 1)
                act.copy(x_dbl[0:XD, b], ps[0:XD, 2]).then_inc(s["xd_copied"], 1)

            def copy_bc(b):
                act.wait_ge(s["bc_ready"], b + 1)
                act.copy(bc[:, b * LT:(b + 1) * LT].rearrange("p t c -> p (t c)"),
                         ps[:, 3, 0:LT * XD]).then_inc(s["bc_copied"], 1)

            def copy_d_u(t):
                act.wait_ge(s["dsk_ready"], t + 1)
                act.copy(acc[:, t], ps[:, 6 + t % 2]).then_inc(s["dsk_copied"], 1)

            def copies(b, part):
                if part == 1:
                    copy_x_dbl(b)
                    copy_d_u(LT * b)
                if part == 2:
                    copy_d_u(LT * b + 1)
                    copy_bc(b)
                if part == 3:
                    copy_d_u(LT * b + 2)
                    copy_d_u(LT * b + 3)

            last_tap(0)
            for i in range(NT):
                if i + 1 < NT:
                    last_tap(i + 1)
                silu(i)
                if i >= EC:
                    copies(i // EC - 1, i % EC)

            act.preload_act_table_set("natural_log_exp_and_others")

            def exponential(b):
                since(act, s["relu_less"], b - 1)
                for ec in range(EC):
                    act.wait_ge(s["dt_ready"], b * EC + ec + 1)
                    act.activation(e_abs[:, b % 2, ec], ps[:, DT_BANK[ec]], ACT.Abs,
                                   bias=dtb_sb[:, ec:ec + 1]).then_inc(s["abs_made"], 1)
                act.wait_ge(s["abs_made"], EC * (b + 1))
                act.activation(e_abs[:, b % 2], e_abs[:, b % 2], ACT.Exp, scale=-1.0).then_inc(s["exp_made"], 1)

            def logarithm(b):
                act.wait_ge(s["lost_made"], b + 1)
                act.activation(one_e[:, b % 2], one_e[:, b % 2], ACT.Ln).then_inc(s["ln_made"], 1)

            def copy_du(b):
                for lt in range(0, LT, 2):
                    t = b * LT + lt
                    act.wait_ge(s["dut_ready"], t + 1)
                    act.copy(du_t[:, t], ps[:, TURN_BANK[lt]]).then_inc(s["dut_copied_a"], 1)

            exponential(0)
            exponential(1)
            for part in range(1, 4):
                copies(B - 1, part)
            logarithm(0)
            exponential(2)
            logarithm(1)
            exponential(3)
            logarithm(2)
            copy_du(0)
            logarithm(3)
            copy_du(1)
            copy_du(2)
            copy_du(3)
            act.wait_ge(s["nega_made"], 2)
            act.wait_ge(s["delta_ready"], B)

            def decays(k, half):
                for ec in range(EC):
                    since(act, s["state_ready"], EC * (k - 2) + ec + 1)
                    act.activation(decay[:, half, ec, 1:L], delta[:, ec, ds((k // DS) * L + 1, L - 1)], ACT.Exp,
                                   scale=nega[:, ec, ds(k % DS, 1)]).then_inc(s["decay_ready"], 1)

            def turned_product(k, half):
                t = (k // DS) * LT + LAST
                since(act, s["dbu_ready"], EC * (k - 1))
                act.activation(dbu_t[:, half, LAST], tile(du_t, t), ACT.Copy,
                               scale=tile(bc, t)[:, ds(k % DS + DR, 1)]).then_inc(s["dbut_made_a"], 1)

            def product(q, which):
                odd, lt = ((0, LAST), (1, SIDE), (1, LAST))[which]
                k = 2 * q + odd
                t = (k // DS) * LT + lt
                since(act, s["prod_added"], PRODS * (q - 1) + which + 1)
                act.wait_ge(s["st_ready"], LT * k + lt + 1)
                act.activation(prod[which], ps[:, 4 + lt], ACT.Copy,
                               scale=tile(bc, t)[:, ds(k % DS + DR + DS, 1)]).then_inc(s["prod_made"], 1)

            turned_product(0, 0)
            decays(0, 0)
            turned_product(1, 1)
            decays(1, 1)
            turned_product(2, 0)
            decays(2, 0)
            turned_product(3, 1)
            product(0, 0)
            decays(3, 1)
            turned_product(4, 0)
            product(0, 1)
            product(0, 2)
            with act.Fori(2, PAIRS - 1) as q:
                decays(2 * q, 0)
                turned_product(2 * q + 1, 1)
                product(q - 1, 0)
                decays(2 * q + 1, 1)
                turned_product(2 * q + 2, 0)
                product(q - 1, 1)
                product(q - 1, 2)
            decays(STEPS - 2, 0)
            turned_product(STEPS - 1, 1)
            product(PAIRS - 2, 0)
            decays(STEPS - 1, 1)
            product(PAIRS - 2, 1)
            product(PAIRS - 2, 2)
            def gates(b):
                act.wait_ge(s["ln1_ready"], b + 1)
                since(act, s["gt_ready"], LT * b)
                for ec in range(EC):
                    act.activation(gate[:, ec], xb[b % 2][:, ec], ACT.Silu, bias=shift[:, ec:ec + 1],
                                   scale=rstd[:, ec:ec + 1]).then_inc(s["gate_ready"], 1)

            def turn_normed(b):
                for lt in range(LT):
                    t = b * LT + lt
                    act.wait_ge(s["xnt_ready"], t + 1)
                    if b >= 2:
                        act.wait_ge(s["sh_ready"], SH * FC * (b - 1))
                        act.wait_ge(s["scores_ready"], b - 1)
                    act.copy(one_pass(x_head[b % 2][:, :, lt * P:(lt + 1) * P]), ps[:, SIDE_BANK[lt]].rearrange(
                        "p (k n) -> p k n", n=P)).then_inc(s["xnt_copied"], 1)

            def gelu(i):
                q = i % (SH * FC)
                act.wait_ge(s["sh_ready"], i + 1)
                since(act, s["sy_ready"], i - 1)
                act.activation(sg[:, i % 2], ps[:, 2 * (i % 2)], ACT.Gelu,
                               bias=sbg_sb[:, q // FC, q % FC:q % FC + 1]).then_inc(s["sg_ready"], 1)

            def hidden_heads(i):
                q = i % (SH * FC)
                act.wait_ge(s["sy_ready"], i + 1)
                act.copy(one_pass(sy_head[:, q]), sy_raw[:, q]).then_inc(s["syh_made"], 1)

            def copy_scores(b):
                act.wait_ge(s["scores_ready"], b + 1)
                if b == 1:
                    act.wait_ge(s["side_added"], B)
                since(act, s["logits_ready"], LT * (b - 1))
                act.copy(scores[b % 2], ps[0:E, SIDE_BANK[1]]).then_inc(s["scores_copied"], 1)

            def copy_logits(first, last):
                act.wait_ge(s["logits_ready"], LT * (last + 1))
                act.copy(aff[:, first * LT:(last + 1) * LT].rearrange("p t e -> p (t e)"),
                         ps[:, SIDE_BANK[0], first * LT * E:(last + 1) * LT * E]).then_inc(s["logits_copied"], 1)

            act.preload_act_table(ACT.Silu)
            act.wait_ge(s["loaded_shared"], 16 * 5)
            act.copy(one_pass(wa_head[:]), wa_raw[:]).then_inc(s["wah_made"], 1)
            product(PAIRS - 1, 0)
            act.wait_ge(s["st_ready"], LT * (STEPS - 1))
            gates(0)
            product(PAIRS - 1, 1)
            product(PAIRS - 1, 2)
            act.wait_ge(s["dbu_ready"], EC * STEPS)
            act.copy(one_pass(sup_head[:, 0]), sup_raw[:, 0]).then_inc(s["suph_made"], 1)
            act.copy(one_pass(sup_head[:, 1]), sup_raw[:, 1]).then_inc(s["suph_made"], 1)
            turn_normed(0)
            gates(1)
            act.wait_ge(s["loaded_sdown"], 16)
            act.copy(one_pass(sdown_head), sdown_raw).then_inc(s["sdh_made"], 1)
            act.wait_ge(s["prod_added"], PRODS * PAIRS)
            gelu(0)
            gelu(1)
            hidden_heads(0)
            gelu(2)
            hidden_heads(1)
            copy_scores(0)
            gelu(3)
            hidden_heads(2)
            copy_logits(0, 0)
            turn_normed(1)
            hidden_heads(3)
            gates(2)
            gelu(4)
            gelu(5)
            hidden_heads(4)
            gates(3)
            copy_scores(1)
            gelu(6)
            hidden_heads(5)
            copy_logits(1, 1)
            turn_normed(2)
            gelu(7)
            hidden_heads(6)
            gelu(8)
            hidden_heads(7)
            gelu(9)
            copy_scores(2)
            turn_normed(3)
            copy_scores(3)
            copy_logits(2, 3)
            act.wait_ge(s["logits_copied"], 3)
            act.activation(aff[:], aff[:], ACT.Sigmoid).then_inc(s["aff_ready"], 1)
            hidden_heads(8)
            hidden_heads(9)
            for i in range(10, 16):
                gelu(i)
                if i > 10:
                    hidden_heads(i - 1)
            hidden_heads(15)

            def turn_tokens(j, half):
                act.wait_ge(s["xgt_ready"], j + 1)
                since(act, s["h_ready"], j - 1)
                act.copy(one_pass(xg_head[:, half]), ps[:, 4 + half]).then_inc(s["xgt_copied"], 1)

            def hidden_gate(j, half):
                act.wait_ge(s["hb_ready"], j + 1)
                act.activation(hg[:, half], hb[:, half, 0:F], ACT.Gelu).then_inc(s["hg_ready"], 1)

            def turn_hidden(j, half):
                act.wait_ge(s["hyt_ready"], j + 1)
                act.copy(one_pass(hy_head[:, half]), ps[:, 2 + half, 0:F]).then_inc(s["hyt_copied"], 1)

            def up_heads(j, r, round_):
                slot_j = act.value_load(blk_slot[0:1, ds(j, 1)], min_val=0, max_val=SLOTS - 1)
                if not isinstance(j, int) or j >= 2:
                    wait_apart(act, s["h_ready"], j - 1)
                wait_apart(act, s[f"up_{r}"], 16 * (round_ + 1))
                for which in range(2):
                    act.copy(one_pass(up_head[:, r % 2, up_part[which]]), up_raw(slot_j, which)).then_inc(s["uph_made"], 1)

            def down_heads(j, r, round_):
                slot_j = act.value_load(blk_slot[0:1, ds(j, 1)], min_val=0, max_val=SLOTS - 1)
                if not isinstance(j, int) or j >= RING:
                    wait_apart(act, s["o_ready"], j - RING + 1)
                wait_apart(act, s[f"down_{r}"], 2 * 16 * (round_ + 1))
                act.copy(one_pass(dw_head[:, r]), down_w[:, ds(slot_j, 1)].rearrange("p o c d -> p (o c d)")).then_inc(s["dwh_made"], 1)

            def block_result(j, half, pair):
                act.wait_ge(s["yb_ready"], j + 1)
                if not (isinstance(pair, int) and pair <= 0):
                    wait_apart(act, s["y_odd" if half else "y_even"], 16 * pair)
                act.activation(y_sb[:, half], yb[:, half], ACT.Copy, scale=row_w[:, ds(j, 1)]).then_inc(s["y_ready"], 1)

            def step(j, round_, r):
                hidden_gate(j, r % 2)
                if not isinstance(j, int) or j + 2 < NBLK:
                    up_heads(j + 2, (r + 2) % RING, round_ + (r + 2) // RING)
                if not isinstance(j, int) or j + 1 < NBLK:
                    down_heads(j + 1, (r + 1) % RING, round_ + (r + 1) // RING)
                if not isinstance(j, int) or j >= 2:
                    block_result(j - 2, r % 2, (RING // 2) * round_ + (r - 2) // 2)
                turn_hidden(j, r % 2)
                if not isinstance(j, int) or j + 3 < NBLK:
                    turn_tokens(j + 3, (r + 1) % 2)

            up_heads(0, 0, 0)
            act.wait_ge(s["so_ready"], NT)
            turn_tokens(0, 0)
            turn_tokens(1, 1)
            up_heads(1, 1, 0)
            act.wait_ge(s["base_stored"], 16 * NT)
            down_heads(0, 0, 0)
            turn_tokens(2, 0)
            for j in range(RING):
                step(j, 0, j)
            with act.Fori(1, (NBLK - 2) // RING) as jj:
                for r in range(RING):
                    step(RING * jj + r, jj, r)
            for j in range((NBLK - 2) // RING * RING, NBLK):
                step(j, j // RING, j % RING)
            for j in range(NBLK - 2, NBLK):
                block_result(j, j % 2, j // 2)

        @block.vector
        def _(dve):
            s = S
            for i in range(NT):
                dve.wait_ge(s["conv_first"], i + 1)
                c, ec = conv[:, i % 4], i % EC
                for back in range(1, DC):
                    if back > 1:
                        dve.wait_ge(s["conv_tap"], (DC - 2) * i + back - 1)
                    dve.scalar_tensor_tensor(
                        out=c[:, back:L], in0=ps[:, PROJ_BANK[i % 4], 0:L - back],
                        scalar=convw_sb[:, ec, DC - 1 - back:DC - back], in1=c[:, back:L],
                        op0=ALU.mult, op1=ALU.add).then_inc(s["conv_done" if back == DC - 1 else "conv_tap"], 1)

            def one_and_lost(b):
                e_b, one_b = e_abs[:, b % 2], one_e[:, b % 2]
                dve.wait_ge(s["exp_made"], b + 1)
                if b < 2:
                    dve.wait_ge(s["dsk_ready"], LT * (B - 2 + b + 1))
                else:
                    dve.wait_ge(s["delta_ready"], b - 1)
                dve.tensor_scalar(one_b, e_b, 1.0, None, ALU.add).then_inc(s["onep_made"], 1)
                dve.wait_ge(s["onep_made"], b + 1)
                dve.scalar_tensor_tensor(out=e_b, in0=one_b, scalar=-1.0, in1=e_b, op0=ALU.add,
                                         op1=ALU.subtract).then_inc(s["lost_made"], 1)

            def relu(b):
                for ec in range(EC):
                    dve.wait_ge(s["abs_made"], b * EC + ec + 1)
                    dve.tensor_scalar(delta[:, ec, b * L:(b + 1) * L], ps[:, DT_BANK[ec]], dtb_sb[:, ec:ec + 1], 0.0,
                                      ALU.add, ALU.max).then_inc(s["relu_made"], 1)

            def add_logarithm(b):
                d = delta[:, :, b * L:(b + 1) * L]
                dve.wait_ge(s["ln_made"], b + 1)
                dve.wait_ge(s["relu_less"], b + 1)
                dve.tensor_tensor(d, one_e[:, b % 2], d, ALU.add).then_inc(s["delta_ready"], 1)

            def delta_u(b):
                dve.wait_ge(s["delta_ready"], b + 1)
                dve.wait_ge(s["xd_ready"], b + 1)
                dve.wait_ge(s["dskip_made"], EC * (b + 1))
                dve.tensor_tensor(u[:, b], delta[:, :, b * L:(b + 1) * L], u[:, b], ALU.mult).then_inc(s["du_last"], 1)

            def first_norm(b):
                dve.wait_ge(s["x_odd" if b % 2 else "x_even"], 16 * (b // 2 + 1))
                for ec in range(EC):
                    dve.bn_stats(stats[:, ec], xb[b % 2][:, ec]).then_inc(s["ln1_stat"], 1)
                dve.wait_ge(s["ln1_stat"], EC * (b + 1))
                for ec in range(EC):
                    dve.bn_aggr(meanvar[:, ec], stats[:, ec]).then_inc(s["ln1_aggr"], 1)
                dve.wait_ge(s["ln1_aggr"], EC * (b + 1))
                since(dve, s["gate_ready"], EC * b)
                dve.tensor_scalar(var_eps[:], meanvar[:, :, 1], EPS, None, ALU.add).then_inc(s["ln1_var"], 1)
                dve.wait_ge(s["ln1_rstd"], b + 1)
                dve.scalar_tensor_tensor(out=shift[:], in0=meanvar[:, :, 0], scalar=-1.0, in1=rstd[:],
                                         op0=ALU.mult, op1=ALU.mult).then_inc(s["ln1_ready"], 1)

            def copy_du(b):
                for lt in range(1, LT, 2):
                    t = b * LT + lt
                    dve.wait_ge(s["dut_ready"], t + 1)
                    dve.tensor_copy(du_t[:, t], ps[:, TURN_BANK[lt]]).then_inc(s["dut_copied_v"], 1)

            dve.wait_ge(s["loaded_scan"], 16 * 5)
            dve.wait_ge(s["pad_stored"], 16 * 2)
            relu(0)
            one_and_lost(0)
            relu(1)
            first_norm(0)
            one_and_lost(1)
            relu(2)
            add_logarithm(0)
            one_and_lost(2)
            relu(3)
            add_logarithm(1)
            one_and_lost(3)
            add_logarithm(2)
            copy_du(0)
            delta_u(2)
            add_logarithm(3)
            delta_u(3)
            copy_du(1)
            copy_du(2)
            copy_du(3)
            dve.wait_ge(s["bc_copied"], B)
            dve.wait_ge(s["dsk_copied"], NT)

            def scans(k, half):
                since(dve, s["st_ready"], LT * (k - 1))
                for ec in range(0, EC, 2):
                    dve.wait_ge(s["decay_ready"], EC * k + ec + 2)
                    dve.wait_ge(s["dbu_ready"], EC * k + ec + 2)
                    dve.tensor_tensor_scan(state[:, half, ec:ec + 2].rearrange("p e l -> p (e l)"),
                                           decay[:, half, ec:ec + 2].rearrange("p e l -> p (e l)"),
                                           ps[:, ec:ec + 2].rearrange("p e l -> p (e l)"), 0.0, ALU.mult,
                                           ALU.add).then_inc(s["state_ready"], 2)

            def sums(q, odd):
                k = 2 * q + odd
                first = SUMS * q + (LAST if odd else 0)
                since(dve, s["mac_done"], first)
                for lt in range(SIDE if odd else LAST):
                    t = (k // DS) * LT + lt
                    dve.wait_ge(s["st_ready"], LT * k + lt + 1)
                    dve.scalar_tensor_tensor(
                        out=tile(acc, t), in0=ps[:, 4 + lt], scalar=tile(bc, t)[:, ds(k % DS + DR + DS, 1)],
                        in1=tile(acc, t), op0=ALU.mult, op1=ALU.add).then_inc(s["mac_done"], 1)

            for half in range(2):
                dve.memset(decay[:, half, :, 0:1], 0.0).then_inc(s["decay_zeroed"], 1)
            dve.wait_ge(s["decay_zeroed"], 2)
            scans(0, 0)
            scans(1, 1)
            sums(0, 0)
            with dve.Fori(1, PAIRS) as q:
                scans(2 * q, 0)
                sums(q - 1, 1)
                scans(2 * q + 1, 1)
                sums(q, 0)
            sums(PAIRS - 1, 1)
            def gate_and_add(b, tiles):
                for lt in tiles:
                    t = b * LT + lt
                    if lt == SIDE:
                        dve.wait_ge(s["side_added"], b + 1)
                    if t == LAST:
                        dve.wait_ge(s["prod_added"], PRODS * PAIRS)
                    dve.wait_ge(s["gt_ready"], t + 1)
                    dve.tensor_tensor(acc[:, t], ps[:, SIDE_BANK[lt]], acc[:, t], ALU.mult).then_inc(s["gated"], 1)
                    dve.wait_ge(s["gated"], t + 1)
                    dve.tensor_tensor(acc[:, t], acc[:, t], xb[b % 2][:, lt], ALU.add).then_inc(s["x1_ready"], 1)
                    dve.wait_ge(s["x1_ready"], t + 1)
                    dve.bn_stats(stats2[:, lt], acc[:, t]).then_inc(s["ln2_stat"], 1)
                    dve.wait_ge(s["ln2_stat"], t + 1)
                    dve.bn_aggr(meanvar2[:, lt], stats2[:, lt]).then_inc(s["ln2_aggr"], 1)

            def normed(b):
                dve.wait_ge(s["ln2_aggr"], LT * (b + 1))
                dve.tensor_scalar(var_eps2[:], meanvar2[:, :, 1], EPS, None, ALU.add).then_inc(s["ln2_var"], 1)
                dve.wait_ge(s["ln2_rstd"], b + 1)
                if b >= 2:
                    dve.wait_ge(s["xn_odd_stored" if b % 2 else "xn_even_stored"], 16 * LT * (b // 2))
                    dve.wait_ge(s["xnt_ready"], LT * (b - 1))
                    dve.wait_ge(s["base_xn"], LT * (b - 1))
                for lt in range(LT):
                    dve.tensor_scalar(xn[b % 2][:, lt], acc[:, b * LT + lt], meanvar2[:, lt, 0:1], rstd2[:, lt:lt + 1],
                                      ALU.subtract, ALU.mult).then_inc(s["xn_ready"], 1)

            def token_rests(b):
                for lt in range(LT):
                    t = b * LT + lt
                    dve.wait_ge(s["xnt_copied"], t + 1)
                    cols = slice(lt * P, (lt + 1) * P)
                    dve.tensor_tensor(one_pass(x_rest[b % 2][:, :, cols]), ps[:, SIDE_BANK[lt]].rearrange("p (k n) -> p k n", n=P),
                                      x_head[b % 2][:, :, cols], ALU.subtract).then_inc(s["xr_made"], 1)

            def hidden_rests(i):
                q = i % (SH * FC)
                dve.wait_ge(s["syh_made"], i + 1)
                dve.tensor_tensor(one_pass(sy_rest[:, q]), sy_raw[:, q], sy_head[:, q], ALU.subtract).then_inc(s["syr_made"], 1)

            def hidden_shared(i):
                q = i % (SH * FC)
                dve.wait_ge(s["sg_ready"], i + 1)
                since(dve, s["so_ready"], LT * (i // (SH * FC)))
                dve.scalar_tensor_tensor(out=sy_raw[:, q], in0=ps[:, 2 * (i % 2) + 1],
                                         scalar=sb1_sb[:, q // FC, q % FC:q % FC + 1], in1=sg[:, i % 2],
                                         op0=ALU.add, op1=ALU.mult).then_inc(s["sy_ready"], 1)

            def add_shared(b, tiles):
                for lt in tiles:
                    t = b * LT + lt
                    dve.wait_ge(s["so_ready"], t + 1)
                    dve.wait_ge(s["base_ready"], t + 1)
                    dve.tensor_tensor(acc[:, t], ps[:, 6 + lt % 2], acc[:, t], ALU.add).then_inc(s["so_added"], 1)

            def pick_experts():
                dve.wait_ge(s["consts_made"], 7)
                dve.wait_ge(s["aff_ready"], 1)
                for t in range(NT):
                    dve.max(top[:, t], aff[:, t]).then_inc(s["top_made"], 1)
                dve.wait_ge(s["top_made"], NT)
                for t in range(NT):
                    dve.max_index(topi[:, t], top[:, t], aff[:, t]).then_inc(s["topi_made"], 1)
                dve.wait_ge(s["topi_made"], NT)
                dve.tensor_copy(topf[:], topi[:, :, 0:TOPK]).then_inc(s["topf_made"], 1)
                dve.wait_ge(s["topf_made"], 1)
                every_e = iota_f[:, 0:E].unsqueeze(1).to_broadcast([P, NT, E])
                for k in range(TOPK):
                    dve.tensor_tensor(hot[:, k], every_e, topf[:, :, k:k + 1].to_broadcast([P, NT, E]),
                                      ALU.is_equal).then_inc(s["hot_made"], 1)
                dve.wait_ge(s["hot_made"], TOPK)
                dve.tensor_tensor(one_pass(member[:]), hot[:, 0], hot[:, 1], ALU.add).then_inc(s["member_made"], 1)

            def weigh_pairs():
                dve.tensor_tensor(wsum[:], top[:, :, 0], top[:, :, 1], ALU.add).then_inc(s["wsum_made"], 1)
                dve.wait_ge(s["wsum_made"], 1)
                dve.reciprocal(wsum[:], wsum[:]).then_inc(s["wsum_made"], 1)
                dve.wait_ge(s["wsum_made"], 2)
                dve.tensor_copy(pair[:, :, :, 0], tok_f[:].unsqueeze(1).to_broadcast([P, TOPK, NT])).then_inc(s["pair_made"], 1)
                for k in range(TOPK):
                    dve.tensor_tensor(pair[:, k, :, 1], top[:, :, k], wsum[:], ALU.mult).then_inc(s["weights_ready"], 1)

            def place_pairs():
                dve.wait_ge(s["count_ready"], 1)
                dve.tensor_scalar(cnt_blk[:], ps[:, SIDE_BANK[0], 0:E], 1.0 / P, None, ALU.mult).then_inc(s["cnt_made"], 1)
                dve.wait_ge(s["cnt_made"], 1)
                dve.tensor_tensor(full[:], cnt_blk[:].unsqueeze(2).to_broadcast([P, E, E]),
                                  iota_f[:, 0:E].unsqueeze(1).to_broadcast([P, E, E]), ALU.is_gt).then_inc(s["full_made"], 1)
                dve.wait_ge(s["full_made"], 1)
                dve.tensor_reduce(nblk[:], full[:], AX_X, ALU.add).then_inc(s["nblk_made"], 1)
                dve.wait_ge(s["nblk_made"], 1)
                dve.tensor_tensor_scan(blk_end[:], ones[:, 0:E], nblk[:], 0.0, ALU.mult, ALU.add).then_inc(s["nblk_made"], 1)
                dve.wait_ge(s["nblk_made"], 2)
                dve.tensor_tensor(slot_base[:], blk_end[:], nblk[:], ALU.subtract).then_inc(s["base_made"], 1)
                dve.wait_ge(s["base_made"], 1)
                dve.wait_ge(s["rank_ready"], 1)
                dve.scalar_tensor_tensor(out=place[:], in0=slot_base[:].unsqueeze(1).to_broadcast([P, NT, E]),
                                         scalar=float(P), in1=ps[:, SIDE_BANK[1], 0:NT * E].rearrange("p (t e) -> p t e", e=E),
                                         op0=ALU.mult, op1=ALU.add).then_inc(s["place_made"], 1)
                dve.wait_ge(s["place_made"], 1)
                for k in range(TOPK):
                    dve.tensor_tensor(picked[:, k], hot[:, k], place[:], ALU.mult).then_inc(s["picked_made"], 1)
                dve.wait_ge(s["picked_made"], TOPK)
                dve.tensor_reduce(slot_f[:], picked[:], AX_X, ALU.add).then_inc(s["slotf_made"], 1)
                dve.wait_ge(s["slotf_made"], 1)
                dve.tensor_copy(slot[:], slot_f[:]).then_inc(s["slots_ready"], 1)

            def list_blocks():
                dve.tensor_tensor(blk_cmp[:], blk_end[:].unsqueeze(1).to_broadcast([P, NBLK, E]),
                                  iota_f[:, 0:NBLK].unsqueeze(2).to_broadcast([P, NBLK, E]), ALU.is_le).then_inc(s["blkc_made"], 1)
                dve.wait_ge(s["blkc_made"], 1)
                dve.tensor_reduce(blk_f[:], blk_cmp[:], AX_X, ALU.add).then_inc(s["blkc_made"], 1)
                dve.wait_ge(s["blkc_made"], 2)
                dve.tensor_scalar(blk_e[:], blk_f[:], float(E - 1), None, ALU.min).then_inc(s["blkm_made"], 1)
                dve.wait_ge(s["blkm_made"], 1)
                dve.memset(blk_new[:, 0:1], 1.0).then_inc(s["new_made"], 1)
                dve.tensor_tensor(blk_new[:, 1:NBLK], blk_e[:, 1:NBLK], blk_e[:, 0:NBLK - 1], ALU.not_equal).then_inc(s["new_made"], 1)
                dve.wait_ge(s["new_made"], 2)
                dve.tensor_copy(blk_load[:], blk_new[:]).then_inc(s["blocks_ready"], 1)
                dve.tensor_tensor_scan(blk_run[:], ones[:, 0:NBLK], blk_new[:], -1.0, ALU.mult, ALU.add).then_inc(s["run_made"], 1)
                dve.wait_ge(s["run_made"], 1)
                rounds = (E - 1) // SLOTS
                turn = iota_f[:, SLOTS:SLOTS * rounds + 1:SLOTS]
                dve.tensor_tensor(blk_cmp[:, :, 0:rounds], blk_run[:].unsqueeze(2).to_broadcast([P, NBLK, rounds]),
                                  turn.unsqueeze(1).to_broadcast([P, NBLK, rounds]), ALU.is_ge).then_inc(s["run_made"], 1)
                dve.wait_ge(s["run_made"], 2)
                dve.tensor_reduce(blk_f[:], blk_cmp[:, :, 0:rounds], AX_X, ALU.add).then_inc(s["run_made"], 1)
                dve.wait_ge(s["run_made"], 3)
                dve.scalar_tensor_tensor(out=blk_slot[:], in0=blk_f[:], scalar=-float(SLOTS), in1=blk_run[:],
                                         op0=ALU.mult, op1=ALU.add).then_inc(s["blocks_ready"], 1)

            every, early, late = range(LT), range(LT // 2), range(LT // 2, LT)
            gate_and_add(0, every)
            normed(0)
            token_rests(0)
            first_norm(1)
            gate_and_add(1, early)
            hidden_shared(0)
            gate_and_add(1, late)
            hidden_shared(1)
            hidden_rests(0)
            normed(1)
            first_norm(2)
            hidden_shared(2)
            hidden_rests(1)
            hidden_shared(3)
            hidden_rests(2)
            token_rests(1)
            hidden_rests(3)
            first_norm(3)
            add_shared(0, every)
            gate_and_add(2, early)
            hidden_shared(4)
            gate_and_add(2, late)
            hidden_shared(5)
            hidden_rests(4)
            normed(2)
            hidden_shared(6)
            hidden_rests(5)
            token_rests(2)
            hidden_shared(7)
            hidden_rests(6)
            gate_and_add(3, every)
            hidden_rests(7)
            normed(3)
            token_rests(3)
            add_shared(1, range(1))
            pick_experts()
            weigh_pairs()
            add_shared(1, range(1, 3))
            place_pairs()
            add_shared(1, range(3, LT))
            hidden_shared(8)
            hidden_shared(9)
            list_blocks()
            hidden_rests(8)
            hidden_rests(9)
            hidden_shared(10)
            hidden_rests(10)
            hidden_shared(11)
            hidden_rests(11)
            add_shared(2, every)
            for i in range(12, 16):
                hidden_shared(i)
                hidden_rests(i)
            dve.wait_ge(s["idst_ready"], 1)
            dve.tensor_copy(ids[:], ps[:, SIDE_BANK[0], 0:NBLK]).then_inc(s["ids_ready"], 1)
            dve.tensor_copy(row_w[:], ps[:, SIDE_BANK[0], NBLK:2 * NBLK]).then_inc(s["ids_ready"], 1)
            dve.wait_ge(s["blocks_ready"], 2)

            def slot_of(j):
                return dve.value_load(blk_slot[0:1, ds(j, 1)], min_val=0, max_val=SLOTS - 1)

            def rest_of_up(j, half, slot_j):
                dve.wait_ge(s["uph_made"], 2 * j + 1)
                dve.tensor_tensor(one_pass(up_rest[:, half, up_part[0]]), up_raw(slot_j, 0), up_head[:, half, up_part[0]],
                                  ALU.subtract).then_inc(s["upr_made_v"], 1)

            rest_of_up(0, 0, slot_of(0))
            add_shared(3, every)
            def rest_of_tokens(j, half):
                dve.wait_ge(s["xgt_copied"], j + 1)
                dve.tensor_tensor(one_pass(xg_rest[:, half]), ps[:, 4 + half], xg_head[:, half], ALU.subtract).then_inc(s["xgr_made"], 1)

            def hidden_bias(j, half, slot_j):
                dve.wait_ge(s["dwh_made"], j + 1)
                dve.wait_ge(s["h_ready"], j + 1)
                dve.tensor_tensor(hb[:, half], ps[:, half], tile(b1_w, slot_j), ALU.add).then_inc(s["hb_ready"], 1)

            def hidden(j, half):
                since(dve, s["hyt_ready"], j - 1)
                dve.wait_ge(s["hg_ready"], j + 1)
                dve.wait_ge(s["hb_ready"], j + 1)
                dve.tensor_tensor(hy[:, half], hg[:, half], hb[:, half, F:2 * F], ALU.mult).then_inc(s["hy_ready"], 1)

            def add_bias(j, half):
                e = dve.value_load(blk_e[0:1, ds(j, 1)], min_val=0, max_val=E - 1)
                since(dve, s["y_ready"], j - 1)
                dve.wait_ge(s["o_ready"], j + 1)
                dve.tensor_tensor(yb[:, half], ps[:, 6 + half], tile(b2_all, e), ALU.add).then_inc(s["yb_ready"], 1)

            def rest_of_hidden(j, half):
                dve.wait_ge(s["hyt_copied"], j + 1)
                dve.tensor_tensor(one_pass(hy_rest[:, half]), ps[:, 2 + half, 0:F], hy_head[:, half], ALU.subtract).then_inc(s["hyr_made"], 1)

            def rest_of_down(j, r, slot_j):
                dve.wait_ge(s["dwh_made"], j + 1)
                dve.tensor_tensor(one_pass(dw_rest[:, r]), down_w[:, ds(slot_j, 1)].rearrange("p o c d -> p (o c d)"),
                                  dw_head[:, r], ALU.subtract).then_inc(s["dwr_made"], 1)

            def step(j, r):
                slot_j = slot_of(j)
                if not isinstance(j, int) or j + 2 < NBLK:
                    slot_next = slot_of(j + 2)
                hidden_bias(j, r % 2, slot_j)
                if not isinstance(j, int) or j >= 1:
                    rest_of_hidden(j - 1, (r - 1) % 2)
                if not isinstance(j, int) or j + 2 < NBLK:
                    rest_of_tokens(j + 2, r % 2)
                hidden(j, r % 2)
                if not isinstance(j, int) or j >= 2:
                    add_bias(j - 2, r % 2)
                if not isinstance(j, int) or j + 2 < NBLK:
                    rest_of_up(j + 2, r % 2, slot_next)
                rest_of_down(j, r, slot_j)

            rest_of_tokens(0, 0)
            rest_of_tokens(1, 1)
            rest_of_up(1, 1, slot_of(1))
            for j in range(RING):
                if j == 2:
                    dve.wait_ge(s["loaded_b2"], 16 * 2)
                step(j, j)
            with dve.Fori(1, (NBLK - 2) // RING) as jj:
                for r in range(RING):
                    step(RING * jj + r, r)
            for j in range((NBLK - 2) // RING * RING, NBLK):
                step(j, j % RING)
            rest_of_hidden(NBLK - 1, (NBLK - 1) % 2)
            for j in range(NBLK - 2, NBLK):
                add_bias(j, j % 2)

        @block.tensor
        def _(pe):
            s = S
            def project_in(b):
                pe.wait_ge(s[f"ctx_{b}"], 16)
                for ec in range(EC):
                    i = b * EC + ec
                    since(pe, s["conv_done"], i - 3)
                    for mc in range(MC):
                        mm = pe.matmul(ps[:, PROJ_BANK[i % 4]], inp_sb[:, mc, ec * P:(ec + 1) * P],
                                       ctx_sb[:, mc, b * L:(b + 1) * L], start=(mc == 0), stop=(mc == MC - 1))
                    mm.then_inc(s["proj_ready"], 1)

            def project_x(b):
                pe.wait_ge(s["u_ready"], EC * (b + 1))
                since(pe, s["xd_copied"], b)
                for ec in range(EC):
                    mm = pe.matmul(ps[0:XD, 2], xproj_sb[:, ec, :], u[:, b, ec],
                                   start=(ec == 0), stop=(ec == EC - 1))
                mm.then_inc(s["xd_ready"], 1)
                for lt in range(LT):
                    t = b * LT + lt
                    pe.wait_ge(s["dskip_made"], EC * (b + 1))
                    since(pe, s["dsk_copied"], t - 1)
                    for ec in range(EC):
                        mm = pe.transpose(ps[:, 6 + t % 2, ec * P:(ec + 1) * P], d_u[:, b % 2, ec, lt * P:(lt + 1) * P], ident[:])
                    mm.then_inc(s["dsk_ready"], 1)
                    if lt == 1:
                        pe.wait_ge(s["xd_copied"], b + 1)
                        since(pe, s["bc_copied"], b)
                        for i in range(LT):
                            mm = pe.transpose(ps[:, 3, i * XD:(i + 1) * XD], x_dbl[0:XD, b, i * P:(i + 1) * P], ident[0:XD, 0:XD])
                        mm.then_inc(s["bc_ready"], 1)

            def project_dt(b):
                pe.wait_ge(s["xd_copied"], b + 1)
                for ec in range(EC):
                    since(pe, s["relu_made"], EC * (b - 1) + ec + 1)
                    pe.matmul(ps[:, DT_BANK[ec]], dtproj_sb[:, ec * P:(ec + 1) * P], x_dbl[0:DR, b],
                              start=True, stop=True).then_inc(s["dt_ready"], 1)

            def turn_du(b):
                if b < 2:
                    pe.wait_ge(s["du_made"], b + 1)
                else:
                    pe.wait_ge(s["du_last"], b - 1)
                if b == 0:
                    pe.wait_ge(s["dsk_copied"], NT)
                    pe.wait_ge(s["bc_copied"], B)
                for lt in range(LT):
                    t = b * LT + lt
                    since(pe, s["dut_copied_v" if lt % 2 else "dut_copied_a"], 2 * (b - 1) + lt // 2 + 1)
                    for ec in range(EC):
                        mm = pe.transpose(ps[:, TURN_BANK[lt], ec * P:(ec + 1) * P], u[:, b, ec, lt * P:(lt + 1) * P], ident[:])
                    mm.then_inc(s["dut_ready"], 1)

            pe.wait_ge(s["loaded_first"], 16 * 3)
            project_in(0)
            pe.wait_ge(s["loaded_scan"], 16 * 5)
            pe.wait_ge(s["consts_made"], 2)
            for b in range(1, B):
                project_in(b)
                project_x(b - 1)
            pe.wait_ge(s["conv_done"], NT)
            project_dt(0)
            project_dt(1)
            project_x(B - 1)
            project_dt(2)
            project_dt(3)
            turn_du(0)
            turn_du(1)
            turn_du(2)
            turn_du(3)
            pe.wait_ge(s["dut_copied_a"], NT // 2)
            pe.wait_ge(s["dut_copied_v"], NT // 2)

            def products(k, half):
                pe.wait_ge(s["dbut_ready"], LAST * (k + 1))
                pe.wait_ge(s["dbut_made_a"], k + 1)
                for ec in range(EC):
                    since(pe, s["state_ready"], EC * (k - 1) + ec + 1)
                    for lt in range(LT):
                        mm = pe.transpose(ps[:, ec, lt * P:(lt + 1) * P], dbu_t[:, half, lt, ec * P:(ec + 1) * P], ident[:])
                    mm.then_inc(s["dbu_ready"], 1)

            def states(q, odd):
                k = 2 * q + odd
                pe.wait_ge(s["state_ready"], EC * (k + 1))
                for lt in range(LT):
                    if lt < SIDE:
                        since(pe, s["mac_done"], SUMS * q + lt + 1 if odd else SUMS * (q - 1) + LAST + lt + 1)
                    elif lt == SIDE and odd:
                        since(pe, s["mac_done"], SUMS * q + SIDE + 1)
                    elif lt == SIDE:
                        since(pe, s["prod_made"], PRODS * (q - 1) + 2)
                    else:
                        since(pe, s["prod_made"], PRODS * q + 1 if odd else PRODS * q)
                    for ec in range(EC):
                        mm = pe.transpose(ps[:, 4 + lt, ec * P:(ec + 1) * P], state[:, odd, ec, lt * P:(lt + 1) * P], ident[:])
                    mm.then_inc(s["st_ready"], 1)

            products(0, 0)
            products(1, 1)
            states(0, 0)
            with pe.Fori(1, PAIRS) as q:
                products(2 * q, 0)
                states(q - 1, 1)
                products(2 * q + 1, 1)
                states(q, 0)
            states(PAIRS - 1, 1)
            def turn_gates(b):
                pe.wait_ge(s["gate_ready"], EC * (b + 1))
                since(pe, s["xr_made"], LT * b)
                since(pe, s["logits_copied"], b - 1)
                if b == 2:
                    pe.wait_ge(s["so_added"], LT)
                for lt in range(LT):
                    for ec in range(EC):
                        mm = pe.transpose(ps[:, SIDE_BANK[lt], ec * P:(ec + 1) * P], gate[:, ec, lt * P:(lt + 1) * P], ident[:])
                    mm.then_inc(s["gt_ready"], 1)

            def turn_normed(b):
                if b in (1, 2):
                    pe.wait_ge(s["logits_copied"], b)
                if b == 3:
                    pe.wait_ge(s["scores_copied"], b)
                for lt in range(LT):
                    pe.wait_ge(s["xn_ready"], b * LT + lt + 1)
                    for kc in range(KC):
                        mm = pe.transpose(ps[:, SIDE_BANK[lt], kc * P:(kc + 1) * P], xn[b % 2][:, lt, kc * P:(kc + 1) * P], ident[:])
                    mm.then_inc(s["xnt_ready"], 1)

            def split_product(to, operands, first=True, last=True):
                n = len(operands)
                for i, (l_head, l_rest, r_head, r_rest) in enumerate(operands):
                    pe.matmul(to, one_pass(l_head), one_pass(r_head), start=(first and i == 0), stop=False)
                    pe.matmul(to, one_pass(l_head), one_pass(r_rest), start=False, stop=False)
                    mm = pe.matmul(to, one_pass(l_rest), one_pass(r_head), start=False,
                                   stop=(last and i == n - 1))
                return mm

            def logits(b):
                pe.wait_ge(s["xr_made"], LT * (b + 1))
                if b + 1 < B:
                    pe.wait_ge(s["gated"], LT * (b + 2))
                split_product(ps[0:E, SIDE_BANK[1]],
                              [(wa_head[:, kc], wa_rest[:, kc], x_head[b % 2][:, kc], x_rest[b % 2][:, kc])
                               for kc in range(KC)]).then_inc(s["scores_ready"], 1)

            def turn_logits(b):
                pe.wait_ge(s["scores_copied"], b + 1)
                if b == 2:
                    pe.wait_ge(s["xr_made"], LT * B)
                for lt in range(LT):
                    t = b * LT + lt
                    pe.transpose(ps[:, SIDE_BANK[0], t * E:(t + 1) * E], scores[b % 2][:, lt * P:(lt + 1) * P],
                                 ident[0:E, 0:E]).then_inc(s["logits_ready"], 1)

            def up_shared(i):
                b, q = i // (SH * FC), i % (SH * FC)
                e, fc = q // FC, q % FC
                since(pe, s["supr_made"], e + 1 if b == 0 else 0)
                pe.wait_ge(s["xr_made"], LT * (b + 1))
                since(pe, s["sy_ready"], i - 1)
                for part in range(2):
                    col = part * F + fc * P
                    mm = split_product(ps[:, 2 * (i % 2) + part],
                                       [(sup_head[:, e, kc, col:col + P], sup_rest[:, e, kc, col:col + P],
                                         x_head[b % 2][:, kc], x_rest[b % 2][:, kc]) for kc in range(KC)])
                mm.then_inc(s["sh_ready"], 1)

            def down_shared(b, tiles=range(LT)):
                if b == 0:
                    pe.wait_ge(s["sdr_made"], 1)
                    pe.wait_ge(s["xr_made"], LT * 2)
                if b == 1:
                    pe.wait_ge(s["xr_made"], LT * B)
                for lt in tiles:
                    t = b * LT + lt
                    since(pe, s["so_added"], t - 1)
                    cols = slice(lt * P, (lt + 1) * P)
                    for q in range(SH * FC):
                        pe.wait_ge(s["syr_made"], SH * FC * b + q + 1)
                        mm = split_product(ps[:, 6 + lt % 2],
                                           [(sy_head[:, q, cols], sy_rest[:, q, cols], sdown_head[:, q // FC, q % FC],
                                             sdown_rest[:, q // FC, q % FC])], first=(q == 0), last=(q == SH * FC - 1))
                    mm.then_inc(s["so_ready"], 1)

            def count_and_rank():
                pe.wait_ge(s["member_made"], 1)
                for t in range(NT):
                    mm = pe.matmul(ps[:, SIDE_BANK[0], 0:E], one_pass(ones[:]), one_pass(member[:, t]), start=(t == 0), stop=(t == NT - 1))
                mm.then_inc(s["count_ready"], 1)
                pe.matmul(ps[:, SIDE_BANK[1], 0:NT * E], one_pass(before[:]), one_pass(member[:].rearrange("p t e -> p (t e)")), start=True, stop=False)
                for t in range(NT - 1):
                    mm = pe.matmul(ps[:, SIDE_BANK[1], (t + 1) * E:NT * E], one_pass(ones[:]),
                                   one_pass(member[:, t:t + 1]).to_broadcast([P, NT - 1 - t, E]), start=False, stop=(t == NT - 2))
                mm.then_inc(s["rank_ready"], 1)

            pe.wait_ge(s["loaded_shared"], 16 * 5)
            pe.wait_ge(s["mac_done"], SUMS * PAIRS)
            pe.wait_ge(s["prod_made"], PRODS * PAIRS)
            turn_gates(0)
            turn_normed(0)
            up_shared(0)
            turn_gates(1)
            up_shared(1)
            up_shared(2)
            pe.wait_ge(s["war_made"], 1)
            logits(0)
            up_shared(3)
            turn_logits(0)
            turn_normed(1)
            down_shared(0)
            turn_gates(2)
            up_shared(4)
            up_shared(5)
            logits(1)
            up_shared(6)
            turn_logits(1)
            turn_normed(2)
            up_shared(7)
            turn_gates(3)
            up_shared(8)
            up_shared(9)
            logits(2)
            turn_normed(3)
            turn_logits(2)
            logits(3)
            down_shared(1, range(1))
            turn_logits(3)
            down_shared(1, range(1, 3))
            count_and_rank()
            down_shared(1, range(3, LT))
            up_shared(10)
            up_shared(11)
            up_shared(12)
            down_shared(2)
            up_shared(13)
            up_shared(14)
            up_shared(15)
            pe.wait_ge(s["place_made"], 1)
            pe.wait_ge(s["ids_loaded"], 16)
            for o in range(2):
                mm = pe.transpose(ps[:, SIDE_BANK[0], o * NBLK:(o + 1) * NBLK], pair_r[:, :, o], ident[0:NBLK, 0:NBLK])
            mm.then_inc(s["idst_ready"], 1)
            down_shared(3)
            pe.wait_ge(s["blocks_ready"], 2)
            pe.wait_ge(s["sy_ready"], SH * FC * B)
            pe.wait_ge(s["ids_ready"], 2)
            pe.wait_ge(s["so_added"], NT)

            def turn_tokens(j, r, round_):
                pe.wait_ge(s[f"xg_{r}"], 16 * (round_ + 1))
                since(pe, s["xgr_made"], j - 1)
                for kc in range(KC):
                    mm = pe.transpose(ps[:, 4 + r % 2, kc * P:(kc + 1) * P], xg[:, r, kc * P:(kc + 1) * P], ident[:])
                mm.then_inc(s["xgt_ready"], 1)

            def up(j, r):
                pe.wait_ge(s["xgr_made"], j + 1)
                pe.wait_ge(s["upr_made_v"], j + 1)
                pe.wait_ge(s["upr_made_p"], j + 1)
                since(pe, s["hb_ready"], j - 1)
                h = r % 2
                mm = split_product(ps[:, h], [(xg_head[:, h, kc * P:(kc + 1) * P], xg_rest[:, h, kc * P:(kc + 1) * P],
                                               up_head[:, h, kc * 2 * F:(kc + 1) * 2 * F],
                                               up_rest[:, h, kc * 2 * F:(kc + 1) * 2 * F]) for kc in range(KC)])
                mm.then_inc(s["h_ready"], 1)

            def turn_hidden(j, r):
                pe.wait_ge(s["hy_ready"], j + 1)
                since(pe, s["hyr_made"], j - 1)
                for fc in range(FC):
                    mm = pe.transpose(ps[:, 2 + r % 2, fc * P:(fc + 1) * P], hy[:, r % 2, fc * P:(fc + 1) * P], ident[:])
                mm.then_inc(s["hyt_ready"], 1)

            def down(j, r):
                pe.wait_ge(s["hyr_made"], j + 1)
                pe.wait_ge(s["dwr_made"], j + 1)
                since(pe, s["yb_ready"], j - 1)
                mm = split_product(ps[:, 6 + r % 2],
                                   [(hy_head[:, r % 2, fc * P:(fc + 1) * P], hy_rest[:, r % 2, fc * P:(fc + 1) * P],
                                     dw_head[:, r, fc * D:(fc + 1) * D], dw_rest[:, r, fc * D:(fc + 1) * D])
                                    for fc in range(FC)])
                mm.then_inc(s["o_ready"], 1)

            def step(j, round_, r):
                up(j + 1, (r + 1) % RING)
                turn_hidden(j, r)
                if not isinstance(j, int) or j + 3 < NBLK:
                    turn_tokens(j + 3, (r + 3) % RING, round_ + (r + 3) // RING)
                if not isinstance(j, int) or j >= 1:
                    down(j - 1, (r - 1) % RING)

            turn_tokens(0, 0, 0)
            turn_tokens(1, 1, 0)
            up(0, 0)
            turn_tokens(2, 2, 0)
            for j in range(RING):
                step(j, 0, j)
            with pe.Fori(1, (NBLK - 2) // RING) as jj:
                for r in range(RING):
                    step(RING * jj + r, jj, r)
            for j in range((NBLK - 2) // RING * RING, NBLK - 2):
                step(j, j // RING, j % RING)
            up(NBLK - 1, (NBLK - 1) % RING)
            turn_hidden(NBLK - 2, (NBLK - 2) % RING)
            down(NBLK - 3, (NBLK - 3) % RING)
            turn_hidden(NBLK - 1, (NBLK - 1) % RING)
            down(NBLK - 2, (NBLK - 2) % RING)
            down(NBLK - 1, (NBLK - 1) % RING)


def _columns(v, n):
    return v.reshape(n, P).T


def _rows(w, n):
    import numpy as np
    w = w.reshape(*w.shape[:-2], n, P, w.shape[-1])
    return np.swapaxes(w, -3, -2)


def kernel(**inputs):
    import numpy as np
    import concourse.bacc as bacc
    from concourse.bass_utils import run_bass_kernel_spmd

    i = {k.replace("L0_xattn_", "").replace("L0_ffn_", "ffn_"): np.asarray(v) for k, v in inputs.items()}
    laid = {
        "x": i["x"].reshape(B, LT, P, D).transpose(0, 2, 1, 3),
        "ctx_t": _rows(i["ctx_1024"].reshape(T, DM).T, MC),
        "in_proj_t": _rows(i["in_proj_w"].T, MC),
        "conv_w": _rows(i["conv_w"], EC),
        "conv_b": _columns(i["conv_b"], EC),
        "x_proj_t": _rows(i["x_proj_w"].T, EC),
        "dt_proj_t": i["dt_proj_w"].T,
        "dt_b": _columns(i["dt_proj_b"], EC),
        "a_log": _rows(i["A_log"], EC),
        "d_skip": _columns(i["D"], EC),
        "wa": _rows(i["ffn_wa"], KC),
        "r_up": _rows(np.concatenate([i["ffn_rg"], i["ffn_rw1"]], axis=2), KC).reshape(E, P, KC * 2 * F),
        "r_b1": np.concatenate([i["ffn_rgb"], i["ffn_rb1"]], axis=1),
        "r_down": _rows(i["ffn_rw2"], FC).reshape(E, P, FC * D),
        "r_b2": i["ffn_rb2"],
        "s_up": _rows(np.concatenate([i["ffn_sg"], i["ffn_sw1"]], axis=2), KC).transpose(1, 0, 2, 3),
        "s_bg": i["ffn_sgb"].reshape(SH, FC, P).transpose(2, 0, 1),
        "s_b1": i["ffn_sb1"].reshape(SH, FC, P).transpose(2, 0, 1),
        "s_down": _rows(i["ffn_sw2"], FC).transpose(1, 0, 2, 3),
        "s_b2": i["ffn_sb2"],
    }
    nc = bacc.Bacc("TRN2", target_bir_lowering=False, num_devices=1)
    arrays, args = {}, []
    for name, a in laid.items():
        a = np.ascontiguousarray(a)
        arrays[f"in_{name}"] = a
        args.append(nc.dram_tensor(f"in_{name}", a.shape, mybir.dt.from_np(a.dtype), kind="ExternalInput").ap())
    out = nc.dram_tensor("out", [T + P, D], F32, kind="ExternalOutput").ap()
    bass_xattn_scan_moe_kernel(nc, *args, out)
    r = run_bass_kernel_spmd(nc, [arrays], core_ids=[0])
    return r.results[0]["out"][:T].reshape(B, L, D)
```
